# Optimizing a Trainium2 kernel written in Bass

```python
import numpy as np
import jax
import jax.numpy as jnp

def _softmax(x, axis=-1):
    return jax.nn.softmax(x, axis=axis)

def _gelu(x):
    return jax.nn.gelu(x, approximate=True)

def _silu(x):
    return jax.nn.silu(x)

def _sigmoid(x):
    return jax.nn.sigmoid(x)

def _layernorm(x, axis=-1, eps=1e-05):
    m = jnp.mean(x, axis=axis, keepdims=True)
    v = jnp.var(x, axis=axis, keepdims=True)
    return (x - m) / jnp.sqrt(v + eps)

def _scatter_add(tgt, idx, src, axis=0):
    return tgt.at[idx].add(src)

def _segment_sum(src, seg, n):
    return jax.ops.segment_sum(src, seg, n)
kernel_name = 'mk_adaln_ffn_d1_seqx_r4_41c87e'

def setup_inputs(seed: int=0):
    np.random.seed(seed)
    _w = jnp.asarray

    def _rec_inputs():
        import jax
        import jax.numpy as jnp
        _rk = jax.random.key(seed)
        x = 7.22e-05 + 1 * jax.random.normal(jax.random.fold_in(_rk, 1), (8, 512, 256), jnp.float32)
        _lenS = 512 - jax.random.randint(jax.random.fold_in(_rk, 7), (8,), 0, max(1, 512 // 4) + 1, jnp.int32)
        _lenS2 = 512 - jax.random.randint(jax.random.fold_in(_rk, 8), (8,), 0, max(1, 512 // 4) + 1, jnp.int32)
        itok_BxS_0_999 = jax.random.randint(jax.random.fold_in(_rk, 11), (8, 512), 0, 250, jnp.int32)
        itok_BxS_0_4 = jax.random.randint(jax.random.fold_in(_rk, 12), (8, 512), 0, 5, jnp.int32)
        cond_512 = 0.00199304 + 1.00034 * jax.random.normal(jax.random.fold_in(_rk, 14), (8, 128), jnp.float32)
        cond_64 = 0.0990542 + 1.04422 * jax.random.normal(jax.random.fold_in(_rk, 15), (8, 64), jnp.float32)
        fside_Bx32_0 = -0.136436 + 0.990155 * jax.random.normal(jax.random.fold_in(_rk, 16), (8, 32), jnp.float32)
        _validS = jnp.arange(512)[None, :] < _lenS[:, None]
        _validS2 = jnp.arange(512)[None, :] < _lenS2[:, None]
        _causal = jnp.tril(jnp.ones((512, 512), dtype=bool))
        mask_BxS_ik0 = jnp.where(jnp.broadcast_to(_validS[:, :], (8, 512)), 0, 1).astype(jnp.int32)
        return (x, itok_BxS_0_999, itok_BxS_0_4, cond_512, cond_64, fside_Bx32_0, mask_BxS_ik0)
    x, itok_BxS_0_999, itok_BxS_0_4, cond_512, cond_64, fside_Bx32_0, mask_BxS_ik0 = _rec_inputs()

    def _L0_cond_setup():
        import jax, jax.numpy as jnp
        import numpy as np
        EPS = 1e-05

        def _ln(x, g, b):
            m = jnp.mean(x, axis=-1, keepdims=True)
            v = jnp.mean((x - m) ** 2, axis=-1, keepdims=True)
            return (x - m) * jax.lax.rsqrt(v + EPS) * g + b

        def _mlp_ln(s, W1, b1, W2, b2, g, b):
            h = jax.nn.silu(s @ W1 + b1) @ W2 + b2
            return _ln(h, g, b)
        key = jax.random.key(seed)
        B, S, D = (4, 512, 256)
        MEM, NOI, RES = (128, 64, 32)
        ks = jax.random.split(key, 40)
        ki = iter(range(40))

        def nrm(shape, scale=0.02):
            return jax.random.normal(ks[next(ki)], shape, jnp.float32) * scale

        def gamma(shape):
            return jnp.ones(shape, jnp.float32) + nrm(shape)
        inp = {'x': jax.random.normal(ks[next(ki)], (B, S, D), jnp.float32), 'pathway_ids': jax.random.randint(ks[next(ki)], (B, S), 0, 250), 'compartment_ids': jax.random.randint(ks[next(ki)], (B, S), 0, 5), 'time_steps': jax.random.randint(ks[next(ki)], (B, S), 0, 5), 'scale_type': jax.random.randint(ks[next(ki)], (B, S), 0, 3), 'memory_state': jax.random.normal(ks[next(ki)], (B, MEM), jnp.float32), 'noise_state': jax.random.normal(ks[next(ki)], (B, NOI), jnp.float32), 'resource_state': jax.random.normal(ks[next(ki)], (B, RES), jnp.float32), 'pw_g': gamma((250, D)), 'pw_b': nrm((250, D)), 'cp_g': gamma((5, D)), 'cp_b': nrm((5, D)), 'tm_g': gamma((5, D)), 'tm_b': nrm((5, D)), 'ms_g': gamma((3, D)), 'ms_b': nrm((3, D)), 'mem_W1': nrm((MEM, D)), 'mem_b1': jnp.zeros((D,)), 'mem_W2': nrm((D, D)), 'mem_b2': jnp.zeros((D,)), 'mem_g': gamma((D,)), 'mem_be': jnp.zeros((D,)), 'noi_W1': nrm((NOI, D)), 'noi_b1': jnp.zeros((D,)), 'noi_W2': nrm((D, D)), 'noi_b2': jnp.zeros((D,)), 'noi_g': gamma((D,)), 'noi_be': jnp.zeros((D,)), 'res_W1': nrm((RES, D)), 'res_b1': jnp.zeros((D,)), 'res_W2': nrm((D, D)), 'res_b2': jnp.zeros((D,)), 'res_g': gamma((D,)), 'res_be': jnp.zeros((D,)), 'int_W1': nrm((6 * D, D)), 'int_b1': jnp.zeros((D,)), 'int_W2': nrm((D, D)), 'int_b2': jnp.zeros((D,)), 'int_g': gamma((D,)), 'int_be': jnp.zeros((D,)), 'aw': jnp.ones((6,), jnp.float32) / 6.0}
        return inp
    _L0_cond_all = _L0_cond_setup()
    _L0_cond_in = {k: v for k, v in _L0_cond_all.items() if k in ('pw_g', 'pw_b', 'cp_g', 'cp_b', 'tm_g', 'tm_b', 'ms_g', 'ms_b', 'mem_W1', 'mem_b1', 'mem_W2', 'mem_b2', 'mem_g', 'mem_be', 'noi_W1', 'noi_b1', 'noi_W2', 'noi_b2', 'noi_g', 'noi_be', 'res_W1', 'res_b1', 'res_W2', 'res_b2', 'res_g', 'res_be', 'int_W1', 'int_b1', 'int_W2', 'int_b2', 'int_g', 'int_be', 'aw')}
    del _L0_cond_all

    def _L0_ffn_setup():
        import jax, jax.numpy as jnp
        import numpy as np
        DIM = 256
        HID = 128
        N_EXPERTS = 16
        TOP_K = 4
        key = jax.random.key(seed)
        ks = jax.random.split(key, 8)
        s = 0.02
        x = jax.random.normal(ks[0], (2, 256, DIM), dtype=jnp.float32)
        gate_w = jax.random.normal(ks[1], (N_EXPERTS, DIM), dtype=jnp.float32) * s
        w1 = jax.random.normal(ks[2], (N_EXPERTS, HID, DIM), dtype=jnp.float32) * s
        w3 = jax.random.normal(ks[3], (N_EXPERTS, HID, DIM), dtype=jnp.float32) * s
        w2 = jax.random.normal(ks[4], (N_EXPERTS, DIM, HID), dtype=jnp.float32) * s
        sw1 = jax.random.normal(ks[5], (HID, DIM), dtype=jnp.float32) * s
        sw3 = jax.random.normal(ks[6], (HID, DIM), dtype=jnp.float32) * s
        sw2 = jax.random.normal(ks[7], (DIM, HID), dtype=jnp.float32) * s
        return {'x': x, 'gate_w': gate_w, 'w1': w1, 'w3': w3, 'w2': w2, 'sw1': sw1, 'sw3': sw3, 'sw2': sw2}
    _L0_ffn_all = _L0_ffn_setup()
    _L0_ffn_in = {k: v for k, v in _L0_ffn_all.items() if k in ('gate_w', 'w1', 'w3', 'w2', 'sw1', 'sw3', 'sw2')}
    del _L0_ffn_all
    return {'x': x, 'itok_BxS_0_999': itok_BxS_0_999, 'itok_BxS_0_4': itok_BxS_0_4, 'cond_512': cond_512, 'cond_64': cond_64, 'fside_Bx32_0': fside_Bx32_0, 'mask_BxS_ik0': mask_BxS_ik0, 'L0_cond_pw_g': _L0_cond_in['pw_g'], 'L0_cond_pw_b': _L0_cond_in['pw_b'], 'L0_cond_cp_g': _L0_cond_in['cp_g'], 'L0_cond_cp_b': _L0_cond_in['cp_b'], 'L0_cond_tm_g': _L0_cond_in['tm_g'], 'L0_cond_tm_b': _L0_cond_in['tm_b'], 'L0_cond_ms_g': _L0_cond_in['ms_g'], 'L0_cond_ms_b': _L0_cond_in['ms_b'], 'L0_cond_mem_W1': _L0_cond_in['mem_W1'], 'L0_cond_mem_b1': _L0_cond_in['mem_b1'], 'L0_cond_mem_W2': _L0_cond_in['mem_W2'], 'L0_cond_mem_b2': _L0_cond_in['mem_b2'], 'L0_cond_mem_g': _L0_cond_in['mem_g'], 'L0_cond_mem_be': _L0_cond_in['mem_be'], 'L0_cond_noi_W1': _L0_cond_in['noi_W1'], 'L0_cond_noi_b1': _L0_cond_in['noi_b1'], 'L0_cond_noi_W2': _L0_cond_in['noi_W2'], 'L0_cond_noi_b2': _L0_cond_in['noi_b2'], 'L0_cond_noi_g': _L0_cond_in['noi_g'], 'L0_cond_noi_be': _L0_cond_in['noi_be'], 'L0_cond_res_W1': _L0_cond_in['res_W1'], 'L0_cond_res_b1': _L0_cond_in['res_b1'], 'L0_cond_res_W2': _L0_cond_in['res_W2'], 'L0_cond_res_b2': _L0_cond_in['res_b2'], 'L0_cond_res_g': _L0_cond_in['res_g'], 'L0_cond_res_be': _L0_cond_in['res_be'], 'L0_cond_int_W1': _L0_cond_in['int_W1'], 'L0_cond_int_b1': _L0_cond_in['int_b1'], 'L0_cond_int_W2': _L0_cond_in['int_W2'], 'L0_cond_int_b2': _L0_cond_in['int_b2'], 'L0_cond_int_g': _L0_cond_in['int_g'], 'L0_cond_int_be': _L0_cond_in['int_be'], 'L0_cond_aw': _L0_cond_in['aw'], 'L0_ffn_gate_w': _L0_ffn_in['gate_w'], 'L0_ffn_w1': _L0_ffn_in['w1'], 'L0_ffn_w3': _L0_ffn_in['w3'], 'L0_ffn_w2': _L0_ffn_in['w2'], 'L0_ffn_sw1': _L0_ffn_in['sw1'], 'L0_ffn_sw3': _L0_ffn_in['sw3'], 'L0_ffn_sw2': _L0_ffn_in['sw2']}

def reference(x, itok_BxS_0_999, itok_BxS_0_4, cond_512, cond_64, fside_Bx32_0, mask_BxS_ik0, L0_cond_pw_g, L0_cond_pw_b, L0_cond_cp_g, L0_cond_cp_b, L0_cond_tm_g, L0_cond_tm_b, L0_cond_ms_g, L0_cond_ms_b, L0_cond_mem_W1, L0_cond_mem_b1, L0_cond_mem_W2, L0_cond_mem_b2, L0_cond_mem_g, L0_cond_mem_be, L0_cond_noi_W1, L0_cond_noi_b1, L0_cond_noi_W2, L0_cond_noi_b2, L0_cond_noi_g, L0_cond_noi_be, L0_cond_res_W1, L0_cond_res_b1, L0_cond_res_W2, L0_cond_res_b2, L0_cond_res_g, L0_cond_res_be, L0_cond_int_W1, L0_cond_int_b1, L0_cond_int_W2, L0_cond_int_b2, L0_cond_int_g, L0_cond_int_be, L0_cond_aw, L0_ffn_gate_w, L0_ffn_w1, L0_ffn_w3, L0_ffn_w2, L0_ffn_sw1, L0_ffn_sw3, L0_ffn_sw2):
    import jax
    import jax.numpy as jnp

    def _L0_cond_ref(x, pathway_ids, compartment_ids, time_steps, scale_type, memory_state, noise_state, resource_state, pw_g, pw_b, cp_g, cp_b, tm_g, tm_b, ms_g, ms_b, mem_W1, mem_b1, mem_W2, mem_b2, mem_g, mem_be, noi_W1, noi_b1, noi_W2, noi_b2, noi_g, noi_be, res_W1, res_b1, res_W2, res_b2, res_g, res_be, int_W1, int_b1, int_W2, int_b2, int_g, int_be, aw):
        import jax, jax.numpy as jnp
        import numpy as np
        EPS = 1e-05

        def _ln(x, g, b):
            m = jnp.mean(x, axis=-1, keepdims=True)
            v = jnp.mean((x - m) ** 2, axis=-1, keepdims=True)
            return (x - m) * jax.lax.rsqrt(v + EPS) * g + b

        def _mlp_ln(s, W1, b1, W2, b2, g, b):
            h = jax.nn.silu(s @ W1 + b1) @ W2 + b2
            return _ln(h, g, b)
        h = _ln(x, pw_g[pathway_ids], pw_b[pathway_ids])
        h = _ln(h, cp_g[compartment_ids], cp_b[compartment_ids])
        t = _ln(x, tm_g[time_steps], tm_b[time_steps])
        m = x + _mlp_ln(memory_state, mem_W1, mem_b1, mem_W2, mem_b2, mem_g, mem_be)[:, None, :]
        n = x + _mlp_ln(noise_state, noi_W1, noi_b1, noi_W2, noi_b2, noi_g, noi_be)[:, None, :]
        r = x + _mlp_ln(resource_state, res_W1, res_b1, res_W2, res_b2, res_g, res_be)[:, None, :]
        s = _ln(x, ms_g[scale_type], ms_b[scale_type])
        w = jax.nn.softmax(aw)
        cat = jnp.concatenate([w[0] * h, w[1] * t, w[2] * m, w[3] * n, w[4] * r, w[5] * s], axis=-1)
        return _mlp_ln(cat, int_W1, int_b1, int_W2, int_b2, int_g, int_be)

    def _L0_ffn_ref(x, gate_w, w1, w3, w2, sw1, sw3, sw2):
        import jax, jax.numpy as jnp
        import numpy as np
        DIM = 256
        HID = 128
        N_EXPERTS = 16
        TOP_K = 4
        bsz, seq_len, dim = x.shape
        xf = x.reshape(-1, dim)
        T = xf.shape[0]
        probs = jax.nn.softmax(xf @ gate_w.T, axis=-1)
        top_w, top_idx = jax.lax.top_k(probs, TOP_K)
        top_w = top_w / jnp.sum(top_w, axis=-1, keepdims=True)
        rows = jnp.arange(T)[:, None]
        combine = jnp.zeros((T, N_EXPERTS), dtype=xf.dtype).at[rows, top_idx].set(top_w)
        h1 = jnp.einsum('td,ehd->teh', xf, w1)
        h3 = jnp.einsum('td,ehd->teh', xf, w3)
        act = jax.nn.silu(h1) * h3
        eout = jnp.einsum('teh,edh->ted', act, w2)
        moe_out = jnp.einsum('ted,te->td', eout, combine)
        shared = jax.nn.silu(xf @ sw1.T) * (xf @ sw3.T) @ sw2.T
        return (moe_out + shared).reshape(bsz, seq_len, dim)
    x = x + _L0_ffn_ref(_L0_cond_ref(x, itok_BxS_0_999, itok_BxS_0_4, itok_BxS_0_4, mask_BxS_ik0, cond_512, cond_64, fside_Bx32_0, L0_cond_pw_g, L0_cond_pw_b, L0_cond_cp_g, L0_cond_cp_b, L0_cond_tm_g, L0_cond_tm_b, L0_cond_ms_g, L0_cond_ms_b, L0_cond_mem_W1, L0_cond_mem_b1, L0_cond_mem_W2, L0_cond_mem_b2, L0_cond_mem_g, L0_cond_mem_be, L0_cond_noi_W1, L0_cond_noi_b1, L0_cond_noi_W2, L0_cond_noi_b2, L0_cond_noi_g, L0_cond_noi_be, L0_cond_res_W1, L0_cond_res_b1, L0_cond_res_W2, L0_cond_res_b2, L0_cond_res_g, L0_cond_res_be, L0_cond_int_W1, L0_cond_int_b1, L0_cond_int_W2, L0_cond_int_b2, L0_cond_int_g, L0_cond_int_be, L0_cond_aw), L0_ffn_gate_w, L0_ffn_w1, L0_ffn_w3, L0_ffn_w2, L0_ffn_sw1, L0_ffn_sw3, L0_ffn_sw2)
    return x

_drawn_inputs = setup_inputs


def setup_inputs(seed=0):
    import zlib

    import numpy as np

    out = dict(_drawn_inputs(seed))
    spreads = {'L0_cond_mem_b1': (0.0, 0.8),
     'L0_cond_mem_b2': (0.0, 0.8),
     'L0_cond_mem_be': (0.0, 0.8),
     'L0_cond_noi_b1': (0.0, 0.8),
     'L0_cond_noi_b2': (0.0, 0.8),
     'L0_cond_noi_be': (0.0, 0.8),
     'L0_cond_res_b1': (0.0, 0.8),
     'L0_cond_res_b2': (0.0, 0.8),
     'L0_cond_res_be': (0.0, 0.8),
     'L0_cond_int_b1': (0.0, 0.8),
     'L0_cond_int_b2': (0.0, 0.441),
     'L0_cond_int_be': (0.0, 0.8),
     'L0_cond_aw': (0.1666666716337204, 0.6)}
    factors = {'cond_512': 8.0,
     'cond_64': 8.0,
     'fside_Bx32_0': 8.0,
     'L0_cond_pw_g': 8.0,
     'L0_cond_pw_b': 8.0,
     'L0_cond_cp_g': 8.0,
     'L0_cond_cp_b': 8.0,
     'L0_cond_tm_g': 8.0,
     'L0_cond_tm_b': 8.0,
     'L0_cond_ms_g': 8.0,
     'L0_cond_ms_b': 8.0,
     'L0_cond_mem_W1': 8.0,
     'L0_cond_mem_W2': 8.0,
     'L0_cond_mem_g': 8.0,
     'L0_cond_noi_W1': 8.0,
     'L0_cond_noi_W2': 8.0,
     'L0_cond_noi_g': 8.0,
     'L0_cond_res_W1': 8.0,
     'L0_cond_res_W2': 8.0,
     'L0_cond_res_g': 8.0,
     'L0_cond_int_W1': 8.0,
     'L0_cond_int_W2': 8.0,
     'L0_cond_int_g': 8.0,
     'L0_ffn_gate_w': 8.0,
     'L0_ffn_w1': 8.0,
     'L0_ffn_w3': 8.0,
     'L0_ffn_w2': 8.0,
     'L0_ffn_sw1': 3.748,
     'L0_ffn_sw3': 4.774,
     'L0_ffn_sw2': 4.657}
    for name, (base, spread) in spreads.items():
        noise = np.random.default_rng([zlib.crc32(name.encode()), seed]).standard_normal(out[name].shape)
        drawn = base * np.exp(spread * noise) if base else spread * noise
        out[name] = jnp.asarray(drawn.astype(out[name].dtype))
    for name, factor in factors.items():
        out[name] = (out[name] * factor).astype(out[name].dtype)
    return out
```

```python
from contextlib import ExitStack

import numpy as np

import concourse.bass as bass
from concourse import mybir

F32 = mybir.dt.float32
F32R = mybir.dt.float32r
BF16 = mybir.dt.bfloat16
I32 = mybir.dt.int32
ALU = mybir.AluOpType
ACT = mybir.ActivationFunctionType
AX = mybir.AxisListType

P = 128
NB, S, D = 8, 512, 256
T = NB * S
TJ = S // P
KT = D // P
NE, TOPK, HID = 16, 4, 128
EPS = 1e-5

CAP = T + P
ROW = 280
COL_W, COL_TOK = D, D + NE
NACC = 4
NBLK = 144
assert NBLK >= T * TOPK // P + NE - 1 and NBLK % NACC == 0
BIG = 3.0e38

SEL = 64
NC, NM = 5, 3
EW = KT * 2 * HID + D
NLATE = 6

C_ID, C_UP, C_CAP, C_BLK, C_SEL, C_TOK, C_END = 0, 128, 256, 272, 274, 275, 279


def wait_past(eng, sem, value):
    if not isinstance(value, int) or value > 0:
        eng.wait_ge(sem, value)


class Shared:
    pass


def build(nc, x, pw_ids, sel_ids, pw_tab, consts, aw, int_w1, int_w2, int_b1, norm_bc,
          tabs, tab_b, gate, mlp_in, mlp_w1, mlp_w2, mlp_b2, mlp_cols, experts, out):
    xlist = nc.dram_tensor("xlist", [(NE * CAP + P), ROW], F32, kind="Internal").ap()
    accs = [nc.dram_tensor(f"acc{a}", [T + P, D], F32, kind="Internal").ap() for a in range(NACC)]

    x_b = x.rearrange("(b j p) d -> p b j d", j=TJ, p=P)
    out_b = out.rearrange("(b j p) d -> p b j d", j=TJ, p=P)
    acc_b = [a[0:T, :].rearrange("(b j p) d -> p b j d", j=TJ, p=P) for a in accs]
    acc_r = [a[0:T, :].rearrange("(b r) d -> b r d", b=NB) for a in accs]
    x_r = x.rearrange("(b r) d -> b r d", b=NB)

    with ExitStack() as whole:
        sems = {}

        def sem(name):
            sems[name] = whole.enter_context(nc.semaphore(name))
            return sems[name]

        def psum(name, shape):
            return whole.enter_context(nc.psum_tensor(name, shape, F32))

        def sb(name, shape, dt=F32):
            return whole.enter_context(nc.sbuf_tensor(name, shape, dt))

        wff_at = -(-nc.sbuf_base // 32) * 32
        wff = sb("wff", [P, NE, 2, EW], F32R)
        cst = sb("cst", [P, C_END])
        base = sb("base", [P, NE])
        padtile = sb("padtile", [P, ROW])
        ident = cst[:, C_ID:C_ID + P]
        banks = [psum(f"bank{i}", [P, 512]) for i in range(8)]

        late = wff[:, NE - NLATE:NE, :, :].rearrange("p e h c -> p (e h c)")
        xs = late[:, 0:2 * 8 * S].rearrange("p (h k s) -> p h k s", h=2, k=8)

        g = Shared()
        g.x_b, g.x_r, g.out_b, g.out_flat, g.acc_b, g.acc_r = x_b, x_r, out_b, out, acc_b, acc_r
        g.accs, g.xlist, g.pw_ids, g.sel_ids, g.pw_tab, g.consts = accs, xlist, pw_ids, sel_ids, pw_tab, consts
        g.aw, g.int_w1, g.int_w2, g.int_b1, g.norm_bc, g.tabs = aw, int_w1, int_w2, int_b1, norm_bc, tabs
        g.tab_b, g.gate, g.mlp_in, g.mlp_w1, g.mlp_w2, g.mlp_b2 = tab_b, gate, mlp_in, mlp_w1, mlp_w2, mlp_b2
        g.mlp_cols, g.experts, g.wff, g.cst, g.base, g.padtile = mlp_cols, experts, wff, cst, base, padtile
        g.ident, g.banks, g.xs, g.wff_at = ident, banks, xs, wff_at
        tokens_block(nc, g, sem)
        experts_block(nc, g, sem)
        sum_block(nc, g, sem)


def tokens_block(nc, g, sem):
    wff, cst, base, padtile, ident, xs = g.wff, g.cst, g.base, g.padtile, g.ident, g.xs
    T0, T1, G0, G1, H0, H1, Y0, Y1 = g.banks
    tb, gb, hb, yb = [T0, T1], [G0, G1], [H0, H1], [Y0, Y1]

    with ExitStack() as ctx:
        def sb(name, shape, dt=F32):
            return ctx.enter_context(nc.sbuf_tensor(name, shape, dt))

        wsh = sb("wsh", [P, 2, EW], F32R)
        wint = sb("wint", [P, 2, 8, D], F32R)
        wout = sb("wout", [P, 2, KT, D], F32R)
        wgate = sb("wgate", [P, 2, KT, NE], F32R)
        tab = sb("tab", [SEL, 4, D], F32R)
        btab = sb("btab", [SEL, D], F32R)
        ones = sb("ones", [SEL, P], F32R)
        ones_bf = sb("ones_bf", [P, P], BF16)
        upper = sb("upper", [P, P], BF16)
        nbc = sb("nbc", [P, 2, D])
        vbias = sb("vbias", [P, KT, NB])
        neghalf = sb("neghalf", [P, 8])
        stage = sb("stage", [P, 2, EW])
        xt = sb("xt", [P, TJ, D])
        pid = sb("pid", [P, 2, TJ], I32)
        gt = sb("gt", [P, TJ, 2 * D])
        xh = sb("xh", [P, TJ, D])
        xhT = sb("xhT", [P, KT, S])
        hhT = sb("hhT", [P, KT, S])
        prod = sb("prod", [P, 3, S])
        oh = sb("oh", [SEL, S], F32R)
        ids = sb("ids", [SEL, S], I32)
        st1, st2, st3 = (sb(f"st{i}", [P, TJ, 6]) for i in (1, 2, 3))
        mv1, mv2, mv3 = (sb(f"mv{i}", [P, TJ, 2]) for i in (1, 2, 3))
        ve1, ve2, ve3 = (sb(f"ve{i}", [P, TJ]) for i in (1, 2, 3))
        rs1, rs2, rs3 = (sb(f"rs{i}", [P, TJ]) for i in (1, 2, 3))
        lg = sb("lg", [P, TJ, 24])
        top8 = sb("top8", [P, TJ, 8])
        rep8 = sb("rep8", [P, TJ, 8])
        repl = sb("repl", [P, TJ, 24])
        mask = sb("mask", [P, TJ, NE], BF16)
        ex = sb("ex", [P, TJ, NE])
        exs = sb("exs", [P, TJ])
        slot = sb("slot", [P, TJ, NE])
        slot8 = sb("slot8", [P, TJ, 8])
        idx = [sb(f"idx{i}", [P, TJ, TOPK], I32) for i in (0, 1)]
        arena_at = -(-nc.sbuf_base // 32) * 32
        sb("arena", [P, 5 * KT * S + 2 * TJ * ROW + TJ * D])
        at = [arena_at]

        def sb_at(name, shape, dt=F32):
            n = -(-int(np.prod(shape[1:])) * 4 // 32) * 32
            t = nc.alloc_sbuf_tensor_at(name, shape, dt, offset=at[0])
            at[0] += n
            return t

        sact = sb_at("sact", [P, KT, S])
        ssp = sb_at("ssp", [P, 2, KT, S], F32R)
        pay = [sb_at(f"pay{i}", [P, TJ, ROW]) for i in (0, 1)]
        csp = sb_at("csp", [P, 2, KT, S], F32R)
        ysh = sb_at("ysh", [P, TJ, D])
        at[0] = arena_at
        raw = sb_at("raw", [P, 6, KT, D])
        wm = sb_at("wm", [P, KT, D])
        rawtab = sb_at("rawtab", [SEL, 4, D])
        tabhi = sb_at("tabhi", [SEL, 4, D], F32R)
        m_b2 = sb_at("m_b2", [96, D])
        rawtb = sb_at("rawtb", [P, 3, KT, SEL])
        rawo = sb_at("rawo", [P, KT, D])
        at[0] = g.wff_at + 8 * 2 * EW * 4
        m_w1 = sb_at("m_w1", [P, 3, D])
        m_w2 = sb_at("m_w2", [P, 3, KT, D])
        rawg = sb_at("rawg", [P, KT, NE])
        small_at = sb_at("small_at", [P, 3 * 32 + 3 * 2 * 32 + 18 + 6 + 2 + 48 + 40])
        m_in = small_at[:, 0:96].rearrange("p (i c) -> p i c", i=3)
        m_h = small_at[:, 96:288].rearrange("p (i k c) -> p i k c", i=3, k=KT)
        m_cols = small_at[:, 288:306].rearrange("p (v k i) -> p v k i", v=3, k=KT)
        w6 = small_at[:, 306:312]
        b1 = small_at[:, 312:314]
        m_t = small_at[:, 314:362].rearrange("p (i k c) -> p i k c", i=3, k=KT)
        awt = small_at[:, 362:368]
        tmp = small_at[:, 368:402]

        s_x, s_ids, s_gt = sem("x_in"), sem("ids_in"), sem("gathered")
        s_pid = [sem("pid_in0"), sem("pid_in1")]
        s_c1, s_c2, s_c3, s_c4, s_c5 = (sem(f"setup_in{i}") for i in range(5))
        s_stage = [sem("stage_in0"), sem("stage_in1")]
        s_split_hi, s_split_lo = sem("expert_hi"), sem("expert_lo")
        s_bn1, s_mv1, s_ve1, s_rs1 = sem("bn1"), sem("mv1"), sem("ve1"), sem("rstd1")
        s_bn2, s_mv2, s_ve2, s_rs2 = sem("bn2"), sem("mv2"), sem("ve2"), sem("rstd2")
        s_bn3, s_mv3, s_ve3, s_rs3 = sem("bn3"), sem("mv3"), sem("ve3"), sem("rstd3")
        s_xh, s_u1, s_u2, s_hh = sem("xhat"), sem("gained"), sem("shifted"), sem("hhat")
        s_xT, s_xhT, s_hhT, s_g = sem("x_turned"), sem("xhat_turned"), sem("hhat_turned"), sem("gains")
        s_xhi, s_xlo, s_xhc, s_hhc = sem("x_hi"), sem("x_lo"), sem("xhat_copied"), sem("hhat_copied")
        s_oh, s_prod, s_phi, s_plo = sem("onehot"), sem("product"), sem("product_hi"), sem("product_lo")
        s_hid, s_silu, s_shi, s_slo = sem("hidden"), sem("hidden_silu"), sem("silu_hi"), sem("silu_lo")
        s_y2, s_c, s_cn, s_cT = sem("second"), sem("centred"), sem("c_rows"), sem("c_turned")
        s_chi, s_clo, s_gate = sem("c_hi"), sem("c_lo"), sem("logits")
        s_top, s_exp, s_rank, s_idx, s_pay = sem("top_step"), sem("exp_done"), sem("ranks"), sem("slots"), sem("row_ready")
        s_sc = [sem("rows_out0"), sem("rows_out1")]
        s_h, s_ss, s_sa, s_ahi, s_alo = sem("shared_h"), sem("shared_silu"), sem("shared_act"), sem("shared_hi"), sem("shared_lo")
        s_ys, s_ysh, s_acc, s_st = sem("shared_y"), sem("shared_out"), sem("sums_begun"), sem("shared_stored")
        s_k, s_pk, s_ak, s_ek = sem("dve_setup"), sem("pool_setup"), sem("act_setup"), sem("pe_setup")
        s_go = sem("wait_held")

        def held(eng):
            eng.sem_inc(s_go, 1)

        def held_wait(eng, sem, value):
            if not isinstance(value, int) or value > 0:
                eng.wait_ge(sem, value)
                held(eng)

        SETUP_EXPERTS = 3
        NCHUNK = NE + 1

        block = ctx.enter_context(nc.Block())

        @block.sync
        def _(sp):
            def load_front(n):
                held_wait(sp, s_xh, TJ * n)
                held_wait(sp, s_xT, KT * n)
                sp.dma_start(xt[:], g.x_b[:, bass.ds(n, 1), :, :].rearrange("p o j d -> p (o j) d")).then_inc(s_x, 16)
                held_wait(sp, s_oh, n)
                sp.dma_start(ids[:], g.sel_ids[:, bass.ds(n, 1), :].rearrange("p o s -> p (o s)")).then_inc(s_ids, 16)

            def load_pid(n, par):
                held_wait(sp, s_gt, 16 * TJ * (n - 1))
                sp.dma_start(pid[:, par, :], g.pw_ids[:, bass.ds(n, 1), :].rearrange("p o j -> p (o j)")).then_inc(s_pid[par], 16)

            def load_chunk(c, e, s):
                held_wait(sp, s_split_hi, c - 1)
                held_wait(sp, s_split_lo, c - 1)
                sp.dma_start(stage[:, s, :], g.experts[bass.ds(e, 1), :, :].rearrange("o p c -> p (o c)")).then_inc(s_stage[s], 16)

            def start_sums(n):
                sp.dma_start(g.acc_r[1][bass.ds(n, 1), :, :], g.x_r[bass.ds(n, 1), :, :]).then_inc(s_acc, 16)
                for a in range(2, NACC):
                    sp.dma_start(g.acc_b[a][:, bass.ds(n, 1), :, :].rearrange("p o j d -> p (o j) d"),
                                 zeros_src).then_inc(s_acc, 16)

            def store_shared(n):
                held_wait(sp, s_ysh, KT * (n + 1))
                sp.dma_start(g.acc_b[0][:, bass.ds(n, 1), :, :].rearrange("p o j d -> p (o j) d"), ysh[:]).then_inc(s_st, 16)

            zeros_src = padtile[:, 0:D].rearrange("p (o d) -> p o d", o=1).broadcast_to((P, TJ, D))
            load_front(0)
            load_pid(0, 0)
            load_pid(1, 1)
            sp.dma_start(cst[:], g.consts).then_inc(s_c1, 16)
            sp.dma_start(awt, g.aw).then_inc(s_c1, 16)
            sp.dma_start(rawtab[:], g.tabs).then_inc(s_c1, 16)
            sp.dma_start(raw[:], g.int_w1).then_inc(s_c2, 16)
            sp.dma_start(m_in, g.mlp_in).then_inc(s_c3, 16)
            sp.dma_start(m_cols, g.mlp_cols).then_inc(s_c3, 16)
            sp.dma_start(m_w1[:], g.mlp_w1).then_inc(s_c3, 16)
            sp.dma_start(m_w2[:], g.mlp_w2).then_inc(s_c3, 16)
            sp.dma_start(m_b2[:], g.mlp_b2).then_inc(s_c3, 16)
            sp.dma_start(rawtb[:], g.tab_b).then_inc(s_c4, 16)
            sp.dma_start(b1, g.int_b1).then_inc(s_c4, 16)
            sp.dma_start(nbc[:], g.norm_bc).then_inc(s_c5, 16)
            sp.dma_start(rawg[:], g.gate).then_inc(s_c5, 16)
            sp.dma_start(rawo[:], g.int_w2).then_inc(s_c5, 16)
            for c in (0, 1):
                load_chunk(c, (c - 1) % NCHUNK, c % 2)
            load_front(1)
            for c in range(2, SETUP_EXPERTS + 1):
                load_chunk(c, c - 1, c % 2)
            sp.wait_ge(s_k, 2)
            sp.dma_start(g.xlist[NE * CAP:NE * CAP + P, :], padtile[:]).then_inc(s_acc, 16)
            for a in range(NACC):
                sp.dma_start(g.accs[a][T:T + P, :], padtile[:, 0:D]).then_inc(s_acc, 16)

            def back(n, par):
                start_sums(n)
                c = n + SETUP_EXPERTS + 1
                load_chunk(c, c - 1, (par + SETUP_EXPERTS + 1) % 2)

            def step(n, par, front):
                back(n, par)
                if front:
                    load_front(n + 2)
                    load_pid(n + 2, par)
                store_shared(n)

            step(0, 0, True)
            with sp.Fori(0, NB // 2 - 2) as m:
                for q in (1, 2):
                    step(2 * m + q, q % 2, True)
            step(NB - 3, 1, True)
            step(NB - 2, 0, False)
            start_sums(NB - 1)
            for e in range(NE - NLATE, NE):
                load_chunk(e + 1, e, (e + 1) % 2)
            store_shared(NB - 1)
            sp.wait_ge(s_acc, 16 * (1 + NACC + NB * (NACC - 1)))
            sp.wait_ge(s_st, 16 * NB)

        @block.gpsimd
        def _(pool):
            pool.memset(neghalf[:], -0.5).then_inc(s_pk, 1)
            pool.memset(ones_bf[:], 1.0).then_inc(s_pk, 1)

            def rstd(rs, ve, s_ve, s_rs, n):
                pool.wait_ge(s_ve, n + 1)
                pool.tensor_tensor(rs[:], ve[:], neghalf[:, 0:TJ], ALU.pow).then_inc(s_rs, 1)

            def gathers(n, par):
                pool.wait_ge(s_pid[par], 8 * (n - par) + 16)
                wait_past(pool, s_hhT, KT * n)
                held(pool)
                for j in range(TJ):
                    pool.indirect_dma_start(gt[:, j, :], None, g.pw_tab,
                                            bass.IndirectOffsetOnAxis(ap=pid[:, par, j:j + 1], axis=0)).then_inc(s_gt, 16)

            def shift(n):
                pool.wait_ge(s_u1, n + 1)
                pool.tensor_tensor(gt[:, :, 0:D], gt[:, :, 0:D], gt[:, :, D:2 * D], ALU.add).then_inc(s_u2, 1)

            def scatter(n, par, first, last):
                if first == 0:
                    pool.wait_ge(s_pay, n + 1)
                    pool.wait_ge(s_idx, n + 1)
                    held(pool)
                for q in range(first, last):
                    j, k = q // TOPK, q % TOPK
                    pool.indirect_dma_start(g.xlist, bass.IndirectOffsetOnAxis(ap=idx[par][:, j, k:k + 1], axis=0),
                                            pay[par][:, j, :], None).then_inc(s_sc[par], 16)

            gathers(0, 0)
            pool.wait_ge(s_pk, 2)
            rstd(rs1, ve1, s_ve1, s_rs1, 0)
            shift(0)
            rstd(rs2, ve2, s_ve2, s_rs2, 0)
            pool.wait_ge(s_k, K_MVE)
            pool.tensor_tensor(tmp[0:96, 1:2], tmp[0:96, 0:1], neghalf[0:96, 0:1], ALU.pow).then_inc(s_pk, 1)
            gathers(1, 1)

            def step(n, par, front, prev):
                if front:
                    rstd(rs1, ve1, s_ve1, s_rs1, n + 1)
                if prev:
                    scatter(n - 1, 1 - par, 0, 6)
                if front:
                    shift(n + 1)
                    rstd(rs2, ve2, s_ve2, s_rs2, n + 1)
                if prev:
                    scatter(n - 1, 1 - par, 6, 11)
                rstd(rs3, ve3, s_ve3, s_rs3, n)
                if prev:
                    scatter(n - 1, 1 - par, 11, 16)

            step(0, 0, True, False)
            gathers(2, 0)
            with pool.Fori(0, NB // 2 - 2) as m:
                for q in (1, 2):
                    n = 2 * m + q
                    step(n, q % 2, True, True)
                    gathers(n + 2, q % 2)
            step(5, 1, True, True)
            gathers(7, 1)
            step(6, 0, True, True)
            step(7, 1, False, True)
            scatter(7, 1, 0, 16)
            for p in (0, 1):
                pool.wait_ge(s_sc[p], 16 * TOPK * TJ * (NB // 2))

        @block.scalar
        def _(act):
            def x_hi(n, h):
                if n is not None:
                    act.wait_ge(s_xT, KT * n + h + 1)
                    wait_past(act, s_hid, KT * n)
                    act.activation(xs[:, 0, h, :], tb[h][:], ACT.Copy).then_inc(s_xhi, 1)

            def xh_copy(n, h):
                act.wait_ge(s_xhT, KT * n + h + 1)
                wait_past(act, s_prod, 6 * n)
                act.activation(xhT[:, h, :], tb[h][:], ACT.Copy).then_inc(s_xhc, 1)

            def hh_copy(n, h):
                act.wait_ge(s_hhT, KT * n + h + 1)
                act.activation(hhT[:, h, :], tb[h][:], ACT.Copy).then_inc(s_hhc, 1)

            def p_hi(n, q):
                act.wait_ge(s_prod, 6 * n + q + 1)
                act.activation(xs[:, 0, kslot(q), :], prod[:, q % 3, :], ACT.Copy).then_inc(s_phi, 1)

            def silu(n, h):
                act.wait_ge(s_hid, KT * n + h + 1)
                wait_past(act, s_alo, n)
                wait_past(act, s_ys, KT * n)
                held(act)
                act.activation(sact[:, h, :], hb[h][:], ACT.Silu, bias=vbias[:, h, bass.ds(n, 1)]).then_inc(s_silu, 1)
                act.wait_ge(s_silu, KT * n + h + 1)
                act.activation(ssp[:, 0, h, :], sact[:, h, :], ACT.Copy).then_inc(s_shi, 1)

            def c_hi(n, h):
                act.wait_ge(s_cT, KT * n + h + 1)
                wait_past(act, s_h, 2 * n)
                act.activation(csp[:, 0, h, :], tb[h][:], ACT.Copy).then_inc(s_chi, 1)

            def exps(n):
                act.wait_ge(s_top, TOPS * n + 5)
                act.activation(ex[:], ex[:], ACT.Exp).then_inc(s_exp, 1)

            def shared_silu(n):
                act.wait_ge(s_h, 2 * n + 1)
                act.wait_ge(s_slo, KT * n + KT)
                act.activation(sact[:, 0, :], hb[0][:], ACT.Silu).then_inc(s_ss, 1)

            def shared_hi(n):
                act.wait_ge(s_sa, n + 1)
                act.wait_ge(s_y2, TJ * n + TJ)
                act.activation(ssp[:, 0, 0, :], sact[:, 1, :], ACT.Copy).then_inc(s_ahi, 1)

            def shared_out(n):
                for b in (0, 1):
                    act.wait_ge(s_ys, 2 * n + b + 1)
                    if b == 0:
                        wait_past(act, s_st, 16 * n)
                    act.activation(ysh[:, 2 * b:2 * b + 2, :].rearrange("p j d -> p (j d)"), yb[b][:], ACT.Copy).then_inc(s_ysh, 1)

            def split_hi(c, dst, s):
                act.wait_ge(s_stage[s], 16 * (c // 2 + 1))
                act.activation(dst, stage[:, s, :], ACT.Copy).then_inc(s_split_hi, 1)

            def split_hi_n(n, par):
                s = (par + SETUP_EXPERTS + 1) % 2
                act.wait_ge(s_stage[s], 8 * (n + SETUP_EXPERTS + 1 - s) + 16)
                held(act)
                act.activation(wff[:, bass.ds(n + SETUP_EXPERTS, 1), 0, :].rearrange("p o c -> p (o c)"),
                               stage[:, s, :], ACT.Copy).then_inc(s_split_hi, 1)

            act.wait_ge(s_k, K_AWD)
            act.activation(w6, w6, ACT.Exp).then_inc(s_ak, 1)
            act.wait_ge(s_ek, 1)
            act.wait_ge(s_c3, 80)
            for i in range(3):
                for h in range(KT):
                    ins = act.activation(m_h[:, i, h, :], H0[:, (i * KT + h) * 32:(i * KT + h) * 32 + 32], ACT.Silu,
                                         bias=m_cols[:, 0, h, i:i + 1])
            ins.then_inc(s_ak, 1)
            act.wait_ge(s_c1, 48)
            act.activation(tabhi[:], rawtab[:], ACT.Copy).then_inc(s_ak, 1)
            for h in (0, 1):
                x_hi(0, h)
            for h in (0, 1):
                xh_copy(0, h)
            act.wait_ge(s_k, K_WM)
            for k, src in enumerate((wm[:], raw[:, 0, :, :], raw[:, 1, :, :], raw[:, 5, :, :])):
                ins = act.activation(wint[:, 0, KT * k:KT * k + KT, :], src, ACT.Copy)
            ins.then_inc(s_ak, 1)
            for q in range(4):
                p_hi(0, q)
            for h in (0, 1):
                hh_copy(0, h)
            act.wait_ge(s_ek, 3)
            act.wait_ge(s_k, K_TAB)
            act.activation(tabhi[:, 0, :], Y0[0:SEL, 0:D], ACT.Copy).then_inc(s_ak, 1)
            act.wait_ge(s_c5, 48)
            act.activation(wgate[:, 0, :, :], rawg[:], ACT.Copy)
            act.activation(wout[:, 0, :, :], rawo[:], ACT.Copy).then_inc(s_ak, 1)
            for q in range(4, 6):
                p_hi(0, q)
            for c in range(SETUP_EXPERTS + 1):
                split_hi(c, wsh[:, 0, :] if c == 0 else wff[:, c - 1, 0, :], c % 2)

            def step(n, par, front):
                for h in (0, 1):
                    silu(n, h)
                if front:
                    for h in (0, 1):
                        x_hi(n + 1, h)
                    for h in (0, 1):
                        xh_copy(n + 1, h)
                    for q in (0, 1):
                        p_hi(n + 1, q)
                for h in (0, 1):
                    c_hi(n, h)
                if front:
                    for q in (2, 3):
                        p_hi(n + 1, q)
                exps(n)
                shared_silu(n)
                if front:
                    for h in (0, 1):
                        hh_copy(n + 1, h)
                    for q in (4, 5):
                        p_hi(n + 1, q)
                shared_hi(n)
                shared_out(n)

            step(0, 0, True)
            split_hi_n(0, 0)
            with act.Fori(0, NB // 2 - 1) as m:
                for q in (1, 2):
                    step(2 * m + q, q % 2, True)
                    split_hi_n(2 * m + q, q % 2)
            step(NB - 1, 1, False)
            for e in range(NE - NLATE, NE):
                split_hi(e + 1, wff[:, e, 0, :], (e + 1) % 2)

        @block.tensor
        def _(pe):
            def three(out, l, r, start=True, stop=True):
                pe.matmul(out, l(0), r(0), start=start, stop=False)
                pe.matmul(out, l(0), r(1), start=False, stop=False)
                return pe.matmul(out, l(1), r(0), start=False, stop=stop)

            def turn(h, src):
                for j in range(TJ):
                    mm = pe.transpose(tb[h][:, j * P:(j + 1) * P], src(j, h), ident)
                return mm

            def turn_x(n):
                pe.wait_ge(s_x, 16 * (n + 1))
                for h in (0, 1):
                    wait_past(pe, s_hhc, KT * (n - 1) + h + 1)
                    turn(h, lambda j, h: xt[:, j, h * P:(h + 1) * P]).then_inc(s_xT, 1)

            def turn_xh(n):
                pe.wait_ge(s_xh, TJ * (n + 1))
                for h in (0, 1):
                    pe.wait_ge(s_xhi, KT * n + h + 1)
                    pe.wait_ge(s_xlo, KT * n + h + 1)
                    turn(h, lambda j, h: xh[:, j, h * P:(h + 1) * P]).then_inc(s_xhT, 1)

            def turn_c(n, par, front):
                pe.wait_ge(s_cn, TJ * (n + 1))
                for h in (0, 1):
                    if front:
                        pe.wait_ge(s_xhc, KT * (n + 1) + h + 1)
                    else:
                        pe.wait_ge(s_hhc, KT * n + h + 1)
                    turn(h, lambda j, h: pay[par][:, j, h * P:(h + 1) * P]).then_inc(s_cT, 1)

            def turn_hh(n):
                pe.wait_ge(s_hh, TJ * (n + 1))
                for h in (0, 1):
                    pe.wait_ge(s_xhc, KT * n + h + 1)
                    wait_past(pe, s_chi, KT * (n - 1) + h + 1)
                    wait_past(pe, s_clo, KT * (n - 1) + h + 1)
                    turn(h, lambda j, h: gt[:, j, h * P:(h + 1) * P]).then_inc(s_hhT, 1)

            def gains(n, q):
                table, h = (1, 1, 2, 2, 0, 0)[q], q % 2
                pe.wait_ge(s_oh, n + 1)
                wait_past(pe, s_prod, 6 * n + q - 1)
                pe.matmul(gb[q % 2][:], tab[:, table, h * P:(h + 1) * P], oh[:], start=True, stop=True).then_inc(s_g, 1)

            def hidden(n):
                pe.wait_ge(s_phi, 6 * (n + 1))
                pe.wait_ge(s_plo, 6 * (n + 1))
                pe.wait_ge(s_xlo, KT * (n + 1))
                pe.wait_ge(s_xhi, KT * (n + 1))
                for h in (0, 1):
                    wait_past(pe, s_ss if h == 0 else s_sa, n)
                    for k in range(8):
                        three(hb[h][:], lambda w: wint[:, w, k, h * P:(h + 1) * P], lambda w: xs[:, w, k, :],
                              start=(k == 0), stop=False)
                    pe.matmul(hb[h][:], btab[:, h * P:(h + 1) * P], oh[:], start=False, stop=True).then_inc(s_hid, 1)

            def second(n):
                wait_past(pe, s_ysh, 2 * n)
                pe.wait_ge(s_shi, KT * (n + 1))
                pe.wait_ge(s_slo, KT * (n + 1))
                for j in range(TJ):
                    o = yb[j // 2][:, (j % 2) * D:(j % 2 + 1) * D]
                    for k in range(KT):
                        three(o, lambda w: ssp[:, w, k, j * P:(j + 1) * P], lambda w: wout[:, w, k, :],
                              start=(k == 0), stop=False)
                    pe.matmul(o, ones[:], tab[:, 3, :], start=False, stop=True).then_inc(s_y2, 1)

            def logits(n):
                pe.wait_ge(s_chi, KT * (n + 1))
                pe.wait_ge(s_clo, KT * (n + 1))
                for j in range(TJ):
                    for k in range(KT):
                        mm = three(Y0[:, j * NE:(j + 1) * NE], lambda w: csp[:, w, k, j * P:(j + 1) * P],
                                   lambda w: wgate[:, w, k, :], start=(k == 0), stop=(k == KT - 1))
                mm.then_inc(s_gate, 1)

            def shared_first(n):
                pe.wait_ge(s_silu, KT * (n + 1))
                for i in (0, 1):
                    for k in range(KT):
                        mm = three(hb[i][:], lambda w: wsh[:, w, k * 2 * HID + i * HID:k * 2 * HID + (i + 1) * HID],
                                   lambda w: csp[:, w, k, :], start=(k == 0), stop=(k == KT - 1))
                    mm.then_inc(s_h, 1)

            def ranks(n):
                pe.wait_ge(s_top, TOPS * n + 6)
                pe.matmul(Y1[:, 0:TJ * NE], upper[:], mask[:].rearrange("p j e -> p (j e)"), start=True, stop=False,
                          skip_group_check=True)
                for d in range(1, TJ):
                    pe.matmul(Y1[:, d * NE:TJ * NE], ones_bf[:], mask[:, 0:TJ - d, :].rearrange("p j e -> p (j e)"),
                              start=False, stop=(d == TJ - 1), skip_group_check=True)
                for j in range(TJ):
                    mm = pe.matmul(Y1[:, TJ * NE:(TJ + 1) * NE], ones_bf[:], mask[:, j, :], start=(j == 0),
                                   stop=(j == TJ - 1), skip_group_check=True)
                mm.then_inc(s_rank, 1)

            def shared_second(n):
                pe.wait_ge(s_ahi, n + 1)
                pe.wait_ge(s_alo, n + 1)
                pe.wait_ge(s_idx, n + 1)
                for b in (0, 1):
                    for j in (2 * b, 2 * b + 1):
                        mm = three(yb[b][:, (j % 2) * D:(j % 2 + 1) * D], lambda w: ssp[:, w, 0, j * P:(j + 1) * P],
                                   lambda w: wsh[:, w, KT * 2 * HID:EW])
                    mm.then_inc(s_ys, 1)

            pe.wait_ge(s_c3, 80)
            for i in range(3):
                for h in range(KT):
                    mm = pe.matmul(H0[:, (i * KT + h) * 32:(i * KT + h) * 32 + 32], m_w1[:, i, h * P:(h + 1) * P],
                                   m_in[:, i, :], start=True, stop=True)
            mm.then_inc(s_ek, 1)
            pe.wait_ge(s_ak, 2)
            for i in range(3):
                for k in range(KT):
                    mm = pe.matmul(H1[32 * i:32 * i + 32, 0:D], m_h[:, i, k, :], m_w2[:, i, k, :],
                                   start=(k == 0), stop=(k == KT - 1))
            mm.then_inc(s_ek, 1)
            pe.wait_ge(s_c1, 48)
            turn_x(0)
            turn_xh(0)
            pe.wait_ge(s_c4, 32)
            pe.wait_ge(s_k, K_WM)
            for q, (t, w) in enumerate(((0, 0), (1, 1), (2, 5))):
                for k in range(KT):
                    mm = pe.matmul(Y0[0:SEL, 0:D], rawtb[:, t, k, :], raw[:, w, k, :], start=(q + k == 0),
                                   stop=(q == 2 and k == KT - 1))
            mm.then_inc(s_ek, 1)
            pe.wait_ge(s_k, K_TAB)
            for q in range(4):
                gains(0, q)
            pe.wait_ge(s_k, K_MLN)
            for k in range(KT):
                mm = pe.transpose(Y1[:, k * 96:(k + 1) * 96], m_b2[0:96, k * P:(k + 1) * P], ident[0:96, 0:96])
            mm.then_inc(s_ek, 1)
            turn_hh(0)
            for q in range(4, 6):
                gains(0, q)
            pe.wait_ge(s_k, K_MT)
            for h in range(KT):
                for i in range(3):
                    for k in range(KT):
                        mm = pe.matmul(H0[:, h * NB:(h + 1) * NB], raw[:, 2 + i, k, h * P:(h + 1) * P], m_t[:, i, k, :],
                                       start=(i + k == 0), stop=(i == 2 and k == KT - 1))
            mm.then_inc(s_ek, 1)
            pe.wait_ge(s_k, K_END)
            pe.wait_ge(s_ak, 6)
            pe.wait_ge(s_split_hi, 1)
            pe.wait_ge(s_split_lo, 1)

            def step(n, par, front):
                hidden(n)
                if front:
                    turn_x(n + 1)
                    turn_xh(n + 1)
                    gains(n + 1, 0)
                    gains(n + 1, 1)
                second(n)
                if front:
                    gains(n + 1, 2)
                    gains(n + 1, 3)
                turn_c(n, par, front)
                logits(n)
                shared_first(n)
                if front:
                    turn_hh(n + 1)
                    gains(n + 1, 4)
                    gains(n + 1, 5)
                ranks(n)
                shared_second(n)

            step(0, 0, True)
            with pe.Fori(0, NB // 2 - 1) as m:
                for q in (1, 2):
                    step(2 * m + q, q % 2, True)
            step(NB - 1, 1, False)

        @block.vector
        def _(v):
            def stats(n, src, st, mv, ve, s_bn, s_mv, s_ve):
                for j in range(TJ):
                    v.bn_stats(st[:, j, :], src(j)).then_inc(s_bn, 1)
                for j in range(TJ):
                    if j == 0:
                        v.wait_ge(s_bn, TJ * (n + 1))
                        held(v)
                    v.bn_aggr(mv[:, j, :], st[:, j, :]).then_inc(s_mv, 1)
                v.wait_ge(s_mv, TJ * (n + 1))
                v.tensor_scalar(ve[:], mv[:, :, 1:2].rearrange("p j o -> p (j o)"), EPS, None, ALU.add).then_inc(s_ve, 1)

            def x_stats(n):
                v.wait_ge(s_x, 16 * (n + 1))
                stats(n, lambda j: xt[:, j, :], st1, mv1, ve1, s_bn1, s_mv1, s_ve1)

            def x_norm(n):
                v.wait_ge(s_rs1, n + 1)
                wait_past(v, s_xhT, KT * n)
                for j in range(TJ):
                    v.tensor_scalar(xh[:, j, :], xt[:, j, :], mv1[:, j, 0:1], rs1[:, j:j + 1], ALU.subtract,
                                    ALU.mult).then_inc(s_xh, 1)

            def gain(n):
                v.wait_ge(s_gt, 16 * TJ * (n + 1))
                v.wait_ge(s_xh, TJ * (n + 1))
                v.tensor_tensor(gt[:, :, 0:D], gt[:, :, 0:D], xh[:], ALU.mult).then_inc(s_u1, 1)

            def h_stats(n):
                v.wait_ge(s_u2, n + 1)
                stats(n, lambda j: gt[:, j, 0:D], st2, mv2, ve2, s_bn2, s_mv2, s_ve2)

            def h_norm(n):
                v.wait_ge(s_rs2, n + 1)
                for j in range(TJ):
                    v.tensor_scalar(gt[:, j, 0:D], gt[:, j, 0:D], mv2[:, j, 0:1], rs2[:, j:j + 1], ALU.subtract,
                                    ALU.mult).then_inc(s_hh, 1)

            def onehot(n):
                v.wait_ge(s_ids, 16 * (n + 1))
                wait_past(v, s_hid, KT * n)
                v.tensor_scalar(oh[:], ids[:], cst[0:SEL, C_SEL:C_SEL + 1], None, ALU.is_equal).then_inc(s_oh, 1)

            def x_lo(n, h):
                v.wait_ge(s_xhi, KT * n + h + 1)
                v.tensor_tensor(xs[:, 1, h, :], tb[h][:], xs[:, 0, h, :].bitcast(F32), ALU.subtract).then_inc(s_xlo, 1)

            def product(n, q):
                h = q % 2
                v.wait_ge(s_g, 6 * n + q + 1)
                v.wait_ge(s_xhc if q < 4 else s_hhc, KT * n + h + 1)
                wait_past(v, s_plo, 6 * n + q - 2)
                v.tensor_tensor(prod[:, q % 3, :], gb[q % 2][:], (xhT if q < 4 else hhT)[:, h, :], ALU.mult).then_inc(s_prod, 1)

            def p_lo(n, q):
                v.wait_ge(s_phi, 6 * n + q + 1)
                v.tensor_tensor(xs[:, 1, kslot(q), :], prod[:, q % 3, :], xs[:, 0, kslot(q), :].bitcast(F32),
                                ALU.subtract).then_inc(s_plo, 1)

            def silu_lo(n, h):
                v.wait_ge(s_shi, KT * n + h + 1)
                v.tensor_tensor(ssp[:, 1, h, :], sact[:, h, :], ssp[:, 0, h, :].bitcast(F32), ALU.subtract).then_inc(s_slo, 1)

            def c_stats(n):
                v.wait_ge(s_y2, TJ * (n + 1))
                stats(n, lambda j: yb[j // 2][:, (j % 2) * D:(j % 2 + 1) * D], st3, mv3, ve3, s_bn3, s_mv3, s_ve3)

            def c_rows(n, par):
                for j in range(TJ):
                    v.scalar_tensor_tensor(pay[par][:, j, 0:D], yb[j // 2][:, (j % 2) * D:(j % 2 + 1) * D],
                                           mv3[:, j, 0:1], nbc[:, 0, :], ALU.subtract, ALU.mult).then_inc(s_c, 1)
                v.wait_ge(s_rs3, n + 1)
                v.wait_ge(s_c, TJ * (n + 1))
                for j in range(TJ):
                    v.scalar_tensor_tensor(pay[par][:, j, 0:D], pay[par][:, j, 0:D], rs3[:, j:j + 1], nbc[:, 1, :],
                                           ALU.mult, ALU.add).then_inc(s_cn, 1)

            def c_lo(n, h):
                v.wait_ge(s_chi, KT * n + h + 1)
                v.tensor_tensor(csp[:, 1, h, :], tb[h][:], csp[:, 0, h, :].bitcast(F32), ALU.subtract).then_inc(s_clo, 1)

            def top_first(n):
                v.wait_ge(s_gate, n + 1)
                v.tensor_copy(lg[:, :, 0:NE], Y0[:, 0:TJ * NE].rearrange("p (j e) -> p j e", j=TJ)).then_inc(s_top, 1)
                v.wait_ge(s_top, TOPS * n + 1)
                held(v)
                for j in range(TJ):
                    ins = v.max(top8[:, j, :], lg[:, j, 0:NE])
                ins.then_inc(s_top, 1)
                v.wait_ge(s_top, TOPS * n + 2)
                v.tensor_copy(rep8[:, :, 0:TOPK], top8[:, :, 0:TOPK]).then_inc(s_top, 1)
                v.wait_ge(s_top, TOPS * n + 3)
                held(v)
                for j in range(TJ):
                    ins = v.match_replace(repl[:, j, :], rep8[:, j, :], lg[:, j, :], -BIG)
                ins.then_inc(s_top, 1)
                v.tensor_tensor(ex[:], lg[:, :, 0:NE], top8[:, :, 0:1].broadcast_to((P, TJ, NE)), ALU.subtract).then_inc(s_top, 1)
                v.wait_ge(s_top, TOPS * n + 4)
                v.tensor_scalar(mask[:], repl[:, :, 0:NE], -BIG, None, ALU.is_equal).then_inc(s_top, 1)

            def top_second(n, par):
                v.wait_ge(s_exp, n + 1)
                v.wait_ge(s_top, TOPS * n + 6)
                v.tensor_tensor(ex[:], ex[:], mask[:], ALU.mult).then_inc(s_top, 1)
                tok = pay[par][:, :, COL_TOK:COL_TOK + 1].bitcast(I32)
                v.tensor_scalar(tok, tok, float(2 * S), None, ALU.add).then_inc(s_top, 1)
                v.wait_ge(s_top, TOPS * n + 7)
                v.tensor_reduce(exs[:], ex[:], AX.X, ALU.add).then_inc(s_top, 1)
                v.wait_ge(s_rank, n + 1)
                v.tensor_tensor(slot[:], Y1[:, 0:TJ * NE].rearrange("p (j e) -> p j e", j=TJ),
                                base[:].rearrange("p (o e) -> p o e", o=1).broadcast_to((P, TJ, NE)), ALU.add).then_inc(s_top, 1)
                v.wait_ge(s_top, TOPS * n + 10)
                v.reciprocal(exs[:], exs[:]).then_inc(s_top, 1)
                v.tensor_tensor(slot[:], slot[:], mask[:], ALU.mult).then_inc(s_top, 1)
                v.wait_ge(s_top, TOPS * n + 12)
                held(v)
                v.tensor_tensor(pay[par][:, :, COL_W:COL_W + NE], ex[:],
                                exs[:].rearrange("p (j o) -> p j o", o=1).broadcast_to((P, TJ, NE)), ALU.mult).then_inc(s_pay, 1)
                for j in range(TJ):
                    ins = v.max(slot8[:, j, :], slot[:, j, :])
                ins.then_inc(s_top, 1)
                v.tensor_tensor(base[:], base[:], Y1[:, TJ * NE:(TJ + 1) * NE], ALU.add).then_inc(s_top, 1)
                v.wait_ge(s_top, TOPS * n + 14)
                v.tensor_scalar(idx[par][:], slot8[:, :, 0:TOPK], -1.0, None, ALU.add).then_inc(s_idx, 1)

            def shared_act(n):
                v.wait_ge(s_ss, n + 1)
                v.wait_ge(s_h, 2 * n + 2)
                v.tensor_tensor(sact[:, 1, :], sact[:, 0, :], hb[1][:], ALU.mult).then_inc(s_sa, 1)

            def shared_lo(n):
                v.wait_ge(s_ahi, n + 1)
                v.tensor_tensor(ssp[:, 1, 0, :], sact[:, 1, :], ssp[:, 0, 0, :].bitcast(F32), ALU.subtract).then_inc(s_alo, 1)

            def split_lo(c, w, e, s):
                v.wait_ge(s_split_hi, c + 1)
                v.tensor_tensor(w[:, e, 1, :] if e is not None else w[:, 1, :], stage[:, s, :],
                                (w[:, e, 0, :] if e is not None else w[:, 0, :]).bitcast(F32), ALU.subtract).then_inc(s_split_lo, 1)

            def split_lo_n(n, par):
                s = (par + SETUP_EXPERTS + 1) % 2
                e = bass.ds(n + SETUP_EXPERTS, 1)
                v.wait_ge(s_split_hi, n + SETUP_EXPERTS + 2)
                v.tensor_tensor(wff[:, e, 1, :].rearrange("p o c -> p (o c)"), stage[:, s, :],
                                wff[:, e, 0, :].rearrange("p o c -> p (o c)").bitcast(F32), ALU.subtract).then_inc(s_split_lo, 1)

            count = [0]

            def k(ins):
                count[0] += 1
                ins.then_inc(s_k, 1)

            def seen():
                v.wait_ge(s_k, count[0])

            k(v.memset(padtile[:], 0.0))
            v.memset(lg[:, :, NE:24], BIG)
            v.memset(rep8[:, :, TOPK:8], BIG)
            x_stats(0)
            v.wait_ge(s_c1, 48)
            seen()
            k(v.tensor_scalar(padtile[:, COL_TOK:COL_TOK + 1].bitcast(I32), cst[:, C_TOK:C_TOK + 1], float(T), None, ALU.add))
            k(v.tensor_reduce(tmp[:, 2:3], awt, AX.X, ALU.max))
            k(v.tensor_copy(base[:], cst[:, C_CAP:C_CAP + NE]))
            seen()
            k(v.tensor_scalar(w6, awt, tmp[:, 2:3], None, ALU.subtract))
            assert count[0] == K_AWD, count
            k(v.tensor_copy(upper[:], cst[:, C_UP:C_UP + P]))
            k(v.tensor_scalar(ones[:], cst[0:SEL, C_UP:C_UP + P], 0.0, 1.0, ALU.mult, ALU.add))
            v.wait_ge(s_ak, 1)
            k(v.tensor_reduce(tmp[:, 3:4], w6, AX.X, ALU.add))
            x_norm(0)
            gain(0)
            seen()
            k(v.reciprocal(tmp[:, 4:5], tmp[:, 3:4]))
            seen()
            k(v.tensor_scalar(w6, w6, tmp[:, 4:5], None, ALU.mult))
            seen()
            v.wait_ge(s_c2, 16)
            for i in range(6):
                ins = v.tensor_scalar(raw[:, i, :, :], raw[:, i, :, :], w6[:, i:i + 1], None, ALU.mult)
            k(ins)
            onehot(0)
            for h in (0, 1):
                x_lo(0, h)
            seen()
            k(v.tensor_tensor(wm[:], raw[:, 2, :, :], raw[:, 3, :, :], ALU.add))
            seen()
            k(v.tensor_tensor(wm[:], wm[:], raw[:, 4, :, :], ALU.add))
            assert count[0] == K_WM, count
            v.wait_ge(s_ak, 3)
            v.tensor_copy(tab[0:32, :, :], tabhi[0:32, :, :])
            k(v.tensor_tensor(tab[32:64, :, :], rawtab[32:64, :, :], tabhi[32:64, :, :].bitcast(F32), ALU.subtract))
            assert count[0] == K_TAB, count
            v.wait_ge(s_ek, 2)
            v.wait_ge(s_c3, 80)
            k(v.tensor_tensor(m_b2[:], H1[0:96, 0:D], m_b2[:], ALU.add))
            seen()
            k(v.bn_stats(tmp[0:96, 8:14], m_b2[:]))
            seen()
            k(v.bn_aggr(tmp[0:96, 14:16], tmp[0:96, 8:14]))
            seen()
            k(v.tensor_scalar(tmp[0:96, 0:1], tmp[0:96, 15:16], EPS, None, ALU.add))
            assert count[0] == K_MVE, count
            for q in range(2):
                product(0, q)
            for q in range(2):
                p_lo(0, q)
            h_stats(0)
            v.wait_ge(s_pk, 3)
            k(v.tensor_scalar(m_b2[:], m_b2[:], tmp[0:96, 14:15], tmp[0:96, 1:2], ALU.subtract, ALU.mult))
            assert count[0] == K_MLN, count
            for q in range(2, 4):
                product(0, q)
            for q in range(2, 4):
                p_lo(0, q)
            h_norm(0)
            v.wait_ge(s_ek, 4)
            for i in range(3):
                for kt in range(KT):
                    ins = v.tensor_scalar(m_t[:, i, kt, :], Y1[:, kt * 96 + 32 * i:kt * 96 + 32 * i + NB],
                                          m_cols[:, 1, kt, i:i + 1], m_cols[:, 2, kt, i:i + 1], ALU.mult, ALU.add)
            k(ins)
            assert count[0] == K_MT, count
            v.wait_ge(s_ak, 4)
            for q, src in enumerate((wm[:], raw[:, 0, :, :], raw[:, 1, :, :], raw[:, 5, :, :])):
                ins = v.tensor_tensor(wint[:, 1, KT * q:KT * q + KT, :], src, wint[:, 0, KT * q:KT * q + KT, :].bitcast(F32),
                                      ALU.subtract)
            k(ins)
            for q in range(4, 6):
                product(0, q)
            for q in range(4, 6):
                p_lo(0, q)
            v.wait_ge(s_ak, 5)
            v.tensor_copy(btab[0:32, :], tabhi[0:32, 0, :])
            k(v.tensor_tensor(btab[32:64, :], Y0[32:64, 0:D], tabhi[32:64, 0, :].bitcast(F32), ALU.subtract))
            v.wait_ge(s_ak, 6)
            v.tensor_tensor(wgate[:, 1, :, :], rawg[:], wgate[:, 0, :, :].bitcast(F32), ALU.subtract)
            k(v.tensor_tensor(wout[:, 1, :, :], rawo[:], wout[:, 0, :, :].bitcast(F32), ALU.subtract))
            v.wait_ge(s_ek, 5)
            v.wait_ge(s_c4, 32)
            for h in range(KT):
                ins = v.tensor_scalar(vbias[:, h, :], H0[:, h * NB:(h + 1) * NB], b1[:, h:h + 1], None, ALU.add)
            k(ins)
            seen()
            for p in (0, 1):
                v.memset(pay[p][:, :, D:ROW], 0.0).then_inc(s_k, 1)
            count[0] += 2
            seen()
            for p in (0, 1):
                ins = v.tensor_scalar(pay[p][:, :, COL_TOK:COL_TOK + 1].bitcast(I32),
                                      cst[:, C_TOK:C_TOK + TJ].rearrange("p (j o) -> p j o", o=1), float((p - 2) * S),
                                      None, ALU.add)
            k(ins)
            assert count[0] == K_END, count
            seen()
            for c in range(SETUP_EXPERTS + 1):
                split_lo(c, wsh if c == 0 else wff, None if c == 0 else c - 1, c % 2)

            def step(n, par, front):
                if front:
                    x_stats(n + 1)
                    x_norm(n + 1)
                    gain(n + 1)
                silu_lo(n, 0)
                if front:
                    onehot(n + 1)
                silu_lo(n, 1)
                if front:
                    for h in (0, 1):
                        x_lo(n + 1, h)
                    h_stats(n + 1)
                    for q in (0, 1):
                        product(n + 1, q)
                    h_norm(n + 1)
                c_stats(n)
                if front:
                    for q in (0, 1):
                        p_lo(n + 1, q)
                c_rows(n, par)
                if front:
                    for q in (2, 3):
                        product(n + 1, q)
                for h in (0, 1):
                    c_lo(n, h)
                if front:
                    for q in (2, 3):
                        p_lo(n + 1, q)
                top_first(n)
                if front:
                    for q in (4, 5):
                        product(n + 1, q)
                shared_act(n)
                if front:
                    for q in (4, 5):
                        p_lo(n + 1, q)
                shared_lo(n)
                top_second(n, par)
                if front and not (isinstance(n, int) and n == 0):
                    v.wait_ge(s_sc[1 - par], 8 * TOPK * TJ * (n - 1 - (1 - par)) + 16 * TOPK * TJ)

            step(0, 0, True)
            split_lo_n(0, 0)
            with v.Fori(0, NB // 2 - 1) as m:
                for q in (1, 2):
                    step(2 * m + q, q % 2, True)
                    split_lo_n(2 * m + q, q % 2)
            step(NB - 1, 1, False)
            for e in range(NE - NLATE, NE):
                split_lo(e + 1, wff, e, (e + 1) % 2)


K_AWD, K_WM, K_TAB, K_MVE, K_MLN, K_MT, K_END = 5, 13, 14, 18, 19, 20, 27
TOPS = 14


def kslot(q):
    return (4, 5, 6, 7, 2, 3)[q]

def experts_block(nc, g, sem):
    wff, cst, base, padtile, ident = g.wff, g.cst, g.base, g.padtile, g.ident
    X, H, A, Y = g.banks[0:2], g.banks[2:4], g.banks[4:6], g.banks[6:8]

    with ExitStack() as ctx:
        def sb(name, shape, dt=F32):
            return ctx.enter_context(nc.sbuf_tensor(name, shape, dt))

        cnt = sb("cnt", [P, NE])
        nblk = sb("nblk", [P, NE])
        cum = [sb(f"cum{i}", [P, 2 * NE]) for i in (0, 1)]
        done = sb("done", [P, 2, NE])
        dblk = sb("dblk", [P, 2, NE])
        route = sb("route", [P, 2, 2])
        start_blk = sb("start_blk", [P, 2])
        padrow = sb("padrow", [1, NE], I32)
        table = sb("table", [1, 4 * P], I32)
        rows = [sb(f"rows{i}", [P, ROW]) for i in range(RING)]
        xT = [sb(f"xT{i}", [P, 2, KT, P], F32R) for i in (0, 1)]
        sil = [sb(f"sil{i}", [P, HID]) for i in (0, 1)]
        act_t = [sb(f"act{i}", [P, HID]) for i in (0, 1)]
        aT = [sb(f"aT{i}", [P, 2, P], F32R) for i in (0, 1)]
        y = [sb(f"y{i}", [P, D]) for i in range(NACC)]

        s_route, s_cols, s_table = sem("route_step"), sem("route_cols"), sem("route_table")
        s_pads = sem("pads_out")
        s_in = [sem(f"rows_in{i}") for i in range(RING)]
        s_xT, s_xhi, s_xlo = sem("rows_turned"), sem("rows_hi"), sem("rows_lo")
        s_h, s_sil, s_act = sem("expert_h"), sem("expert_silu"), sem("expert_act")
        s_aT, s_ahi, s_alo = sem("act_turned"), sem("act_hi"), sem("act_lo")
        s_y, s_yout = sem("expert_y"), sem("expert_y_out")
        s_add = [sem(f"added{i}") for i in range(NACC)]
        s_go = sem("expert_wait_held")

        def held(eng):
            eng.sem_inc(s_go, 1)

        def schedule(eng, step):
            for s in range(RING):
                step(s, s, [i <= s for i in range(SKEW + 1)])
            with eng.Fori(0, NBLK // RING - 1) as m:
                for q in range(RING):
                    step(RING * m + (RING + q), q, [True] * (SKEW + 1))
            for s in range(NBLK, NBLK + SKEW):
                step(s, s % RING, [i > s - NBLK for i in range(SKEW + 1)])

        block = ctx.enter_context(nc.Block())

        @block.sync
        def _(sp):
            sp.wait_ge(s_route, R_PADROW)
            for e in range(NE):
                r = sp.value_load(padrow[0:1, e:e + 1], min_val=e * CAP, max_val=e * CAP + T)
                sp.dma_start(g.xlist[bass.ds(r, P), :], padtile[:]).then_inc(s_pads, 16)
            sp.wait_ge(s_table, 1)
            sp.wait_ge(s_pads, 16 * NE)

            def load(b, q):
                r = sp.value_load(table[0:1, bass.ds(b + 2 * P, 1)], min_val=0, max_val=NE * CAP)
                sp.dma_start(rows[q][:], g.xlist[bass.ds(r, P), :]).then_inc(s_in[q], 16)

            for b in range(RING):
                load(b, b)
            with sp.Fori(0, NBLK // RING - 1) as m:
                for q in range(RING):
                    sp.wait_ge(s_add[q % NACC], 16 * (RING // NACC) * m + 16 * (q // NACC + 1))
                    held(sp)
                    load(RING * m + (RING + q), q)

        @block.gpsimd
        def _(pool):
            def add(b, q, turn):
                pool.wait_ge(s_yout, b + 1)
                wait_past(pool, s_add[q % NACC], 16 * turn)
                held(pool)
                pool.indirect_dma_start(g.accs[q % NACC], bass.IndirectOffsetOnAxis(
                    ap=rows[q][:, COL_TOK:COL_TOK + 1].bitcast(I32), axis=0), y[q % NACC][:], None,
                    compute_op=ALU.add).then_inc(s_add[q % NACC], 16)

            for b in range(RING):
                add(b, b, b // NACC)
            with pool.Fori(0, NBLK // RING - 1) as m:
                for q in range(RING):
                    add(RING * m + (RING + q), q, (RING // NACC) * m + (RING + q) // NACC)
            for a in range(NACC):
                pool.wait_ge(s_add[a], 16 * NBLK // NACC)

        @block.scalar
        def _(act):
            def step(s, q, on):
                if on[4]:
                    b, i = s - SKEW, (q - SKEW) % RING
                    act.wait_ge(s_y, b + 1)
                    wait_past(act, s_add[i % NACC], (s - q) * (16 // NACC) + 16 * ((q - SKEW) // NACC))
                    held(act)
                    act.activation(y[i % NACC][:], Y[i % 2][:, 0:D], ACT.Copy).then_inc(s_yout, 1)
                if on[0]:
                    act.wait_ge(s_xT, s + 1)
                    act.activation(xT[q % 2][:, 0, :, :].rearrange("p k t -> p (k t)"), X[q % 2][:, 0:KT * P],
                                   ACT.Copy).then_inc(s_xhi, 1)
                if on[1]:
                    b = s - 1
                    act.wait_ge(s_h, b + 1)
                    act.activation(sil[(q - 1) % 2][:], H[(q - 1) % 2][:, 0:HID], ACT.Silu).then_inc(s_sil, 1)
                if on[2]:
                    b = s - 2
                    act.wait_ge(s_aT, b + 1)
                    act.activation(aT[q % 2][:, 0, :], A[q % 2][:, 0:P], ACT.Copy).then_inc(s_ahi, 1)

            schedule(act, step)

        @block.tensor
        def _(pe):
            pe.wait_ge(s_route, R_ROUTE)
            for q in range(4):
                mm = pe.matmul(A[0][0:1, q * P:(q + 1) * P], route[:, q // 2, q % 2:q % 2 + 1], ident, start=True, stop=True)
            mm.then_inc(s_cols, 1)
            pe.wait_ge(s_table, 1)

            def step(s, q, on):
                if on[0]:
                    pe.wait_ge(s_in[q], 16 * (s // RING) + 16 if isinstance(s, int) else 2 * (s - q) + 16)
                    wait_past(pe, s_xlo, s - 1)
                    for k in range(KT):
                        mm = pe.transpose(X[q % 2][:, k * P:(k + 1) * P], rows[q][:, k * P:(k + 1) * P], ident)
                    mm.then_inc(s_xT, 1)
                if on[1]:
                    b, i = s - 1, (q - 1) % 2
                    e = pe.value_load(table[0:1, bass.ds(b, 1)], min_val=0, max_val=NE - 1)
                    pe.wait_ge(s_xlo, b + 1)
                    wait_past(pe, s_act, b - 1)
                    for k in range(KT):
                        for t, w in ((0, 0), (0, 1), (1, 0)):
                            mm = pe.matmul(H[i][:, 0:2 * HID], xT[i][:, t, k, :],
                                           wff[:, bass.ds(e, 1), w, k * 2 * HID:(k + 1) * 2 * HID],
                                           start=(k == 0 and t + w == 0), stop=(k == KT - 1 and t == 1))
                    mm.then_inc(s_h, 1)
                if on[2]:
                    b, i = s - 2, q % 2
                    pe.wait_ge(s_act, b + 1)
                    wait_past(pe, s_alo, b - 1)
                    pe.transpose(A[i][:, 0:P], act_t[i][:], ident).then_inc(s_aT, 1)
                if on[3]:
                    b, i = s - 3, (q - 3) % 2
                    e = pe.value_load(table[0:1, bass.ds(b, 1)], min_val=0, max_val=NE - 1)
                    pe.wait_ge(s_alo, b + 1)
                    wait_past(pe, s_yout, b - 1)
                    for t, w in ((0, 0), (0, 1), (1, 0)):
                        mm = pe.matmul(Y[i][:, 0:D], aT[i][:, t, :], wff[:, bass.ds(e, 1), w, KT * 2 * HID:EW],
                                       start=(t + w == 0), stop=(t == 1))
                    mm.then_inc(s_y, 1)

            schedule(pe, step)

        @block.vector
        def _(v):
            count = [0]

            def k(ins):
                count[0] += 1
                ins.then_inc(s_route, 1)

            def seen():
                v.wait_ge(s_route, count[0])

            cap1 = cst[:, C_CAP:C_CAP + NE]
            blk = cst[:, C_BLK:C_BLK + 2]
            k(v.tensor_scalar(padrow[:], base[0:1, :], -1.0, None, ALU.add))
            assert count[0] == R_PADROW
            k(v.tensor_tensor(cnt[:], base[:], cap1, ALU.subtract))
            for c in cum:
                k(v.memset(c[:, 0:NE], 0.0))
            seen()
            k(v.tensor_scalar(nblk[:], cnt[:], 1.0 / P, (P / 2 - 0.5) / P, ALU.mult, ALU.add))
            seen()
            k(v.tensor_scalar(nblk[:], nblk[:], 2.0 ** 23, None, ALU.add))
            seen()
            k(v.tensor_scalar(nblk[:], nblk[:], 2.0 ** 23, None, ALU.subtract))
            seen()
            k(v.tensor_copy(cum[0][:, NE:], nblk[:]))
            src = 0
            for d in (1, 2, 4, 8):
                seen()
                k(v.tensor_tensor(cum[1 - src][:, NE:], cum[src][:, NE:], cum[src][:, NE - d:2 * NE - d], ALU.add))
                src = 1 - src
            seen()
            for h in (0, 1):
                k(v.tensor_scalar(done[:, h, :], cum[src][:, NE:], blk[:, h:h + 1], None, ALU.is_le))
            seen()
            k(v.tensor_tensor(dblk[:], done[:], nblk[:].rearrange("p (o e) -> p o e", o=1).broadcast_to((P, 2, NE)), ALU.mult))
            k(v.tensor_reduce(route[:, 0, :], done[:], AX.X, ALU.add))
            seen()
            k(v.tensor_reduce(start_blk[:], dblk[:], AX.X, ALU.add))
            seen()
            k(v.tensor_tensor(start_blk[:], blk, start_blk[:], ALU.subtract))
            k(v.tensor_scalar(route[:, 1, :], route[:, 0, :], float(CAP), None, ALU.mult))
            seen()
            k(v.scalar_tensor_tensor(route[:, 1, :], start_blk[:], float(P), route[:, 1, :], ALU.mult, ALU.add))
            k(v.tensor_scalar(route[:, 0, :], route[:, 0, :], float(NE - 1), None, ALU.min))
            seen()
            k(v.tensor_scalar(route[:, 1, :], route[:, 1, :], float(NE * CAP), None, ALU.min))
            assert count[0] == R_ROUTE, count
            v.wait_ge(s_cols, 1)
            v.tensor_copy(table[:], A[0][0:1, :]).then_inc(s_table, 1)
            v.wait_ge(s_table, 1)

            def step(s, q, on):
                if on[0]:
                    i = q % 2
                    v.wait_ge(s_xhi, s + 1)
                    v.tensor_tensor(xT[i][:, 1, :, :].rearrange("p k t -> p (k t)"), X[i][:, 0:KT * P],
                                    xT[i][:, 0, :, :].rearrange("p k t -> p (k t)").bitcast(F32), ALU.subtract).then_inc(s_xlo, 1)
                if on[1]:
                    b, i = s - 1, (q - 1) % 2
                    e = v.value_load(table[0:1, bass.ds(b, 1)], min_val=0, max_val=NE - 1)
                    v.wait_ge(s_sil, b + 1)
                    wait_past(v, s_aT, b - 1)
                    held(v)
                    v.scalar_tensor_tensor(act_t[i][:], sil[i][:], rows[(q - 1) % RING][:, bass.ds(e + COL_W, 1)],
                                           H[i][:, HID:2 * HID], ALU.mult, ALU.mult).then_inc(s_act, 1)
                if on[2]:
                    b, i = s - 2, q % 2
                    v.wait_ge(s_ahi, b + 1)
                    v.tensor_tensor(aT[i][:, 1, :], A[i][:, 0:P], aT[i][:, 0, :].bitcast(F32), ALU.subtract).then_inc(s_alo, 1)

            schedule(v, step)


RING = 8
SKEW = 4
R_PADROW, R_ROUTE = 1, 22
assert NBLK % RING == 0 and RING % NACC == 0 and RING > SKEW


def sum_block(nc, g, sem):
    with ExitStack() as ctx:
        parts = [[ctx.enter_context(nc.sbuf_tensor(f"part{i}_{a}", [P, TJ, D], F32)) for a in range(NACC)] for i in (0, 1)]
        s_part = [sem("parts_in0"), sem("parts_in1")]
        s_half, s_sum, s_out = sem("half_sums"), sem("sums"), [sem("out0"), sem("out1")]
        block = ctx.enter_context(nc.Block())

        @block.sync
        def _(sp):
            for n in range(NB):
                if n >= 2:
                    sp.wait_ge(s_out[n % 2], 16 * (n // 2))
                for a in range(NACC):
                    sp.dma_start(parts[n % 2][a][:], g.acc_b[a][:, n, :, :]).then_inc(s_part[n % 2], 16)
            for i in (0, 1):
                sp.wait_ge(s_out[i], 16 * (NB // 2))

        @block.scalar
        def _(act):
            for n in range(NB):
                act.wait_ge(s_sum, n + 1)
                act.dma_start(g.out_b[:, n, :, :], parts[n % 2][0][:]).then_inc(s_out[n % 2], 16)

        @block.vector
        def _(v):
            for n in range(NB):
                p = parts[n % 2]
                v.wait_ge(s_part[n % 2], 16 * NACC * (n // 2 + 1))
                v.tensor_tensor(p[0][:], p[0][:], p[1][:], ALU.add).then_inc(s_half, 1)
                v.tensor_tensor(p[2][:], p[2][:], p[3][:], ALU.add).then_inc(s_half, 1)
                v.wait_ge(s_half, 2 * n + 2)
                v.tensor_tensor(p[0][:], p[0][:], p[2][:], ALU.add).then_inc(s_sum, 1)


def kernel(**inputs):
    import numpy as _np
    import concourse.bacc as _bacc
    from concourse import mybir as _mybir
    from concourse.bass_utils import run_bass_kernel_spmd as _run

    a = {k: _np.asarray(v) for k, v in inputs.items()}
    f32 = _np.float32

    def cond(name):
        return a["L0_cond_" + name]

    def ktiles(w):
        return w.reshape(-1, P, w.shape[-1]).transpose(1, 0, 2)

    def columns(v):
        return v.reshape(KT, P).T

    c9, c4, mk = a["itok_BxS_0_999"], a["itok_BxS_0_4"], a["mask_BxS_ik0"]
    sel_ids = _np.zeros((SEL, NB, S), c4.dtype)
    tabs = _np.zeros((SEL, 4, D), f32)
    tab_b = _np.zeros((P, 3, KT, SEL), f32)
    consts = _np.zeros((P, C_END), f32)
    consts[:, C_SEL] = -1
    for r in (0, 32):
        sel_ids[r:r + NC] = c4
        sel_ids[r + NC:r + NC + NM] = mk
        consts[r:r + NC, C_SEL] = _np.arange(NC)
        consts[r + NC:r + NC + NM, C_SEL] = _np.arange(NM)
        tabs[r:r + NC, 0], tabs[r:r + NC, 1] = cond("cp_g"), cond("tm_g")
        tabs[r + NC:r + NC + NM, 2] = cond("ms_g")
        tabs[r, 3] = cond("int_b2")
        for t, name, at in ((0, "cp_b", r), (1, "tm_b", r), (2, "ms_b", r + NC)):
            b = cond(name)
            tab_b[:, t, :, at:at + len(b)] = b.reshape(len(b), KT, P).transpose(2, 1, 0)
    consts[:, C_ID:C_ID + P] = _np.eye(P)
    consts[:, C_UP:C_UP + P] = _np.triu(_np.ones((P, P)), 1)
    consts[:, C_CAP:C_CAP + NE] = _np.arange(NE) * CAP + 1
    consts[:, C_BLK], consts[:, C_BLK + 1] = _np.arange(P), _np.arange(P) + P
    consts[:, C_TOK:C_TOK + TJ] = _np.arange(P)[:, None] + P * _np.arange(TJ)

    mlp_in = _np.zeros((P, 3, 32), f32)
    mlp_w1 = _np.zeros((P, 3, D), f32)
    mlp_w2 = _np.zeros((P, 3, KT, D), f32)
    mlp_b2 = _np.zeros((96, D), f32)
    mlp_cols = _np.zeros((P, 3, KT, 3), f32)
    for i, (name, s) in enumerate((("mem", "cond_512"), ("noi", "cond_64"), ("res", "fside_Bx32_0"))):
        mlp_in[:a[s].shape[1], i, :NB] = a[s].T
        mlp_w1[:a[s].shape[1], i] = cond(name + "_W1")
        mlp_w2[:, i] = ktiles(cond(name + "_W2"))
        mlp_b2[32 * i:32 * i + 32] = cond(name + "_b2")
        for q, part in enumerate(("_b1", "_g", "_be")):
            mlp_cols[:, q, :, i] = columns(cond(name + part))

    w1 = _np.concatenate([a["L0_ffn_w1"], a["L0_ffn_sw1"][None]])
    w3 = _np.concatenate([a["L0_ffn_w3"], a["L0_ffn_sw3"][None]])
    w2 = _np.concatenate([a["L0_ffn_w2"], a["L0_ffn_sw2"][None]])
    first = _np.concatenate([w1, w3], 1).transpose(0, 2, 1).reshape(NE + 1, KT, P, 2 * HID).transpose(0, 2, 1, 3)
    experts = _np.concatenate([first.reshape(NE + 1, P, KT * 2 * HID), w2.transpose(0, 2, 1)], 2)

    arrays = {
        "x": a["x"].reshape(T, D),
        "pw_ids": c9.reshape(NB, TJ, P).transpose(2, 0, 1),
        "sel_ids": sel_ids,
        "pw_tab": _np.concatenate([cond("pw_g"), cond("pw_b")], 1),
        "consts": consts,
        "aw": _np.repeat(cond("aw")[None], P, 0),
        "int_w1": ktiles(cond("int_W1")).reshape(P, 6, KT, D),
        "int_w2": ktiles(cond("int_W2")),
        "int_b1": columns(cond("int_b1")),
        "norm_bc": _np.repeat(_np.stack([cond("int_g"), cond("int_be")])[None], P, 0),
        "tabs": tabs,
        "tab_b": tab_b,
        "gate": ktiles(a["L0_ffn_gate_w"].T),
        "mlp_in": mlp_in, "mlp_w1": mlp_w1, "mlp_w2": mlp_w2, "mlp_b2": mlp_b2, "mlp_cols": mlp_cols,
        "experts": experts,
    }
    arrays = {k: _np.ascontiguousarray(v) for k, v in arrays.items()}
    nc = _bacc.Bacc("TRN2", target_bir_lowering=False, num_devices=1)
    args = {k: nc.dram_tensor(k + "_in", v.shape, _mybir.dt.from_np(v.dtype), kind="ExternalInput").ap()
            for k, v in arrays.items()}
    out = nc.dram_tensor("out_dram", (T, D), _mybir.dt.float32, kind="ExternalOutput").ap()
    build(nc, out=out, **args)
    r = _run(nc, [{k + "_in": v for k, v in arrays.items()}], core_ids=[0])
    return r.results[0]["out_dram"].reshape(NB, S, D)
```

```python
from contextlib import ExitStack

import numpy as np

import concourse.bass as bass
from concourse import mybir

F32 = mybir.dt.float32
F32R = mybir.dt.float32r
BF16 = mybir.dt.bfloat16
I32 = mybir.dt.int32
ALU = mybir.AluOpType
ACT = mybir.ActivationFunctionType
AX = mybir.AxisListType

P = 128
NB, S, D = 8, 512, 256
T = NB * S
TJ = S // P
KT = D // P
NE, TOPK, HID = 16, 4, 128
EPS = 1e-5

BT = 2
BROWS = BT * P
CAP = T + BROWS
ROW = 280
COL_W, COL_TOK = D, D + NE
NACC = 2
NBLK = 80
assert P >= NBLK >= T * TOPK // BROWS + NE - 1 and NBLK % NACC == 0
BIG = 3.0e38

SEL = 64
NC, NM = 5, 3
EW = KT * 2 * HID + D
NLATE = 6

C_ID, C_UP, C_CAP, C_SEL, C_TOK, C_END = 0, 128, 256, 272, 273, 277


def wait_past(eng, sem, value):
    if not isinstance(value, int) or value > 0:
        eng.wait_ge(sem, value)


class Shared:
    pass


def build(nc, x, pw_ids, sel_ids, pw_tab, consts, aw, int_w1, int_w2, int_b1, norm_bc,
          tabs, tab_b, gate, mlp_in, mlp_w1, mlp_w2, mlp_b2, mlp_cols, experts, out):
    xlist = nc.dram_tensor("xlist", [NE * CAP + BROWS, ROW], F32, kind="Internal").ap()
    accs = [nc.dram_tensor(f"acc{a}", [T + BROWS, D], F32, kind="Internal").ap() for a in range(NACC)]

    x_b = x.rearrange("(b j p) d -> p b j d", j=TJ, p=P)
    out_b = out.rearrange("(b j p) d -> p b j d", j=TJ, p=P)
    acc_b = [a[0:T, :].rearrange("(b j p) d -> p b j d", j=TJ, p=P) for a in accs]
    acc_r = [a[0:T, :].rearrange("(b r) d -> b r d", b=NB) for a in accs]
    x_r = x.rearrange("(b r) d -> b r d", b=NB)

    with ExitStack() as whole:
        sems = {}

        def sem(name):
            sems[name] = whole.enter_context(nc.semaphore(name))
            return sems[name]

        def psum(name, shape):
            return whole.enter_context(nc.psum_tensor(name, shape, F32))

        def sb(name, shape, dt=F32):
            return whole.enter_context(nc.sbuf_tensor(name, shape, dt))

        wff_at = -(-nc.sbuf_base // 32) * 32
        wff = sb("wff", [P, NE, 2, EW], F32R)
        cst = sb("cst", [P, C_END])
        base = sb("base", [P, NE])
        ident = cst[:, C_ID:C_ID + P]
        banks = [psum(f"bank{i}", [P, 512]) for i in range(8)]

        late = wff[:, NE - NLATE:NE, :, :].rearrange("p e h c -> p (e h c)")
        xs = late[:, 0:2 * 8 * S].rearrange("p (h k s) -> p h k s", h=2, k=8)

        g = Shared()
        g.x_b, g.x_r, g.out_b, g.out_flat, g.acc_b, g.acc_r = x_b, x_r, out_b, out, acc_b, acc_r
        g.accs, g.xlist, g.pw_ids, g.sel_ids, g.pw_tab, g.consts = accs, xlist, pw_ids, sel_ids, pw_tab, consts
        g.aw, g.int_w1, g.int_w2, g.int_b1, g.norm_bc, g.tabs = aw, int_w1, int_w2, int_b1, norm_bc, tabs
        g.tab_b, g.gate, g.mlp_in, g.mlp_w1, g.mlp_w2, g.mlp_b2 = tab_b, gate, mlp_in, mlp_w1, mlp_w2, mlp_b2
        g.mlp_cols, g.experts, g.wff, g.cst, g.base = mlp_cols, experts, wff, cst, base
        g.ident, g.banks, g.xs, g.wff_at = ident, banks, xs, wff_at
        tokens_block(nc, g, sem)
        experts_block(nc, g, sem)
        sum_block(nc, g, sem)


def tokens_block(nc, g, sem):
    wff, cst, base, ident, xs = g.wff, g.cst, g.base, g.ident, g.xs
    T0, T1, G0, G1, H0, H1, Y0, Y1 = g.banks
    tb, gb, hb, yb = [T0, T1], [G0, G1], [H0, H1], [Y0, Y1]

    with ExitStack() as ctx:
        def sb(name, shape, dt=F32):
            return ctx.enter_context(nc.sbuf_tensor(name, shape, dt))

        wsh = sb("wsh", [P, 2, EW], F32R)
        wint = sb("wint", [P, 2, 8, D], F32R)
        wout = sb("wout", [P, 2, KT, D], F32R)
        wgate = sb("wgate", [P, 2, KT, NE], F32R)
        tab = sb("tab", [SEL, 4, D], F32R)
        btab = sb("btab", [SEL, D], F32R)
        ones = sb("ones", [SEL, P], F32R)
        ones_bf = sb("ones_bf", [P, P], BF16)
        upper = sb("upper", [P, P], BF16)
        nbc = sb("nbc", [P, 2, D])
        vbias = sb("vbias", [P, KT, NB])
        neghalf = sb("neghalf", [P, 8])
        zeros = sb("zeros", [P, D])
        stage = sb("stage", [P, 2, EW])
        xt = sb("xt", [P, TJ, D])
        pid = sb("pid", [P, 2, TJ], I32)
        gt = sb("gt", [P, TJ, 2 * D])
        xh = sb("xh", [P, TJ, D])
        xhT = sb("xhT", [P, KT, S])
        lgT = xhT[0:NE, 0, :]
        hhT = sb("hhT", [P, KT, S])
        prod = sb("prod", [P, 3, S])
        oh = sb("oh", [SEL, S], F32R)
        ids = sb("ids", [SEL, S], I32)
        st1, st2, st3 = (sb(f"st{i}", [P, TJ, 6]) for i in (1, 2, 3))
        mv1, mv2, mv3 = (sb(f"mv{i}", [P, TJ, 2]) for i in (1, 2, 3))
        ve1, ve2, ve3 = (sb(f"ve{i}", [P, TJ]) for i in (1, 2, 3))
        rs1, rs2, rs3 = (sb(f"rs{i}", [P, TJ]) for i in (1, 2, 3))
        nm1, nm2 = (sb(f"nm{i}", [P, TJ]) for i in (1, 2))
        lg = sb("lg", [P, TJ, 24])
        top8 = sb("top8", [P, TJ, 8])
        rep8 = sb("rep8", [P, TJ, 8])
        repl = sb("repl", [P, TJ, 24])
        mask = sb("mask", [P, TJ, NE], BF16)
        ex = sb("ex", [P, TJ, NE])
        exs = sb("exs", [P, TJ])
        slot = sb("slot", [P, TJ, NE])
        slot8 = sb("slot8", [P, TJ, 8])
        idx = [sb(f"idx{i}", [P, TJ, TOPK], I32) for i in (0, 1)]
        arena_at = -(-nc.sbuf_base // 32) * 32
        sb("arena", [P, 5 * KT * S + 2 * TJ * ROW + TJ * D])
        at = [arena_at]

        def sb_at(name, shape, dt=F32):
            n = -(-int(np.prod(shape[1:])) * 4 // 32) * 32
            t = nc.alloc_sbuf_tensor_at(name, shape, dt, offset=at[0])
            at[0] += n
            return t

        sact = sb_at("sact", [P, KT, S])
        ssp = sb_at("ssp", [P, 2, KT, S], F32R)
        pay = [sb_at(f"pay{i}", [P, TJ, ROW]) for i in (0, 1)]
        csp = sb_at("csp", [P, 2, KT, S], F32R)
        ysh = sb_at("ysh", [P, TJ, D])
        at[0] = arena_at
        raw = sb_at("raw", [P, 6, KT, D])
        wm = sb_at("wm", [P, KT, D])
        rawtab = sb_at("rawtab", [SEL, 4, D])
        tabhi = sb_at("tabhi", [SEL, 4, D], F32R)
        m_b2 = sb_at("m_b2", [96, D])
        rawtb = sb_at("rawtb", [P, 3, KT, SEL])
        rawo = sb_at("rawo", [P, KT, D])
        at[0] = g.wff_at + 8 * 2 * EW * 4
        m_w1 = sb_at("m_w1", [P, 3, D])
        m_w2 = sb_at("m_w2", [P, 3, KT, D])
        rawg = sb_at("rawg", [P, KT, NE])
        small_at = sb_at("small_at", [P, 3 * 32 + 3 * 2 * 32 + 18 + 6 + 2 + 48 + 40])
        m_in = small_at[:, 0:96].rearrange("p (i c) -> p i c", i=3)
        m_h = small_at[:, 96:288].rearrange("p (i k c) -> p i k c", i=3, k=KT)
        m_cols = small_at[:, 288:306].rearrange("p (v k i) -> p v k i", v=3, k=KT)
        w6 = small_at[:, 306:312]
        b1 = small_at[:, 312:314]
        m_t = small_at[:, 314:362].rearrange("p (i k c) -> p i k c", i=3, k=KT)
        awt = small_at[:, 362:368]
        tmp = small_at[:, 368:402]

        s_x, s_ids, s_gt = sem("x_in"), sem("ids_in"), sem("gathered")
        s_pid = [sem("pid_in0"), sem("pid_in1")]
        s_c1, s_c2, s_c3, s_c4, s_c5 = (sem(f"setup_in{i}") for i in range(5))
        s_stage = [sem("stage_in0"), sem("stage_in1")]
        s_split_hi, s_split_lo = sem("expert_hi"), sem("expert_lo")
        s_nm1, s_nm2 = sem("shift1"), sem("shift2")
        s_bn1, s_mv1, s_ve1, s_rs1 = sem("bn1"), sem("mv1"), sem("ve1"), sem("rstd1")
        s_bn2, s_mv2, s_ve2, s_rs2 = sem("bn2"), sem("mv2"), sem("ve2"), sem("rstd2")
        s_bn3, s_mv3, s_ve3, s_rs3 = sem("bn3"), sem("mv3"), sem("ve3"), sem("rstd3")
        s_xh, s_u1, s_u2, s_hh = sem("xhat"), sem("gained"), sem("shifted"), sem("hhat")
        s_xT, s_xhT, s_hhT, s_g = sem("x_turned"), sem("xhat_turned"), sem("hhat_turned"), sem("gains")
        s_xhi, s_xlo, s_xhc, s_hhc = sem("x_hi"), sem("x_lo"), sem("xhat_copied"), sem("hhat_copied")
        s_oh, s_prod, s_phi, s_plo = sem("onehot"), sem("product"), sem("product_hi"), sem("product_lo")
        s_hid, s_silu, s_shi, s_slo = sem("hidden"), sem("hidden_silu"), sem("silu_hi"), sem("silu_lo")
        s_y2, s_c, s_cn, s_cT = sem("second"), sem("centred"), sem("c_rows"), sem("c_turned")
        s_chi, s_clo, s_gate = sem("c_hi"), sem("c_lo"), sem("logits")
        s_lgT, s_lgc = sem("logits_in_rows"), sem("logits_copied")
        s_top, s_exp, s_rank, s_idx, s_pay = sem("top_step"), sem("exp_done"), sem("ranks"), sem("slots"), sem("row_ready")
        s_sc = [sem("rows_out0"), sem("rows_out1")]
        s_h, s_ss, s_sa, s_ahi, s_alo = sem("shared_h"), sem("shared_silu"), sem("shared_act"), sem("shared_hi"), sem("shared_lo")
        s_ys, s_ysh, s_acc, s_st = sem("shared_y"), sem("shared_out"), sem("sums_begun"), sem("shared_stored")
        s_k, s_pk, s_ak, s_ek = sem("dve_setup"), sem("pool_setup"), sem("act_setup"), sem("pe_setup")
        s_go = sem("wait_held")

        def held(eng):
            eng.sem_inc(s_go, 1)

        def held_wait(eng, sem, value):
            if not isinstance(value, int) or value > 0:
                eng.wait_ge(sem, value)
                held(eng)

        SETUP_EXPERTS = 3
        NCHUNK = NE + 1

        block = ctx.enter_context(nc.Block())

        @block.sync
        def _(sp):
            def load_front(n):
                held_wait(sp, s_xh, TJ * n)
                held_wait(sp, s_xT, KT * n)
                sp.dma_start(xt[:], g.x_b[:, bass.ds(n, 1), :, :].rearrange("p o j d -> p (o j) d")).then_inc(s_x, 16)
                held_wait(sp, s_oh, n)
                sp.dma_start(ids[:], g.sel_ids[:, bass.ds(n, 1), :].rearrange("p o s -> p (o s)")).then_inc(s_ids, 16)

            def load_pid(n, par):
                held_wait(sp, s_gt, 16 * TJ * (n - 1))
                sp.dma_start(pid[:, par, :], g.pw_ids[:, bass.ds(n, 1), :].rearrange("p o j -> p (o j)")).then_inc(s_pid[par], 16)

            def load_chunk(c, e, s):
                held_wait(sp, s_split_hi, c - 1)
                held_wait(sp, s_split_lo, c - 1)
                sp.dma_start(stage[:, s, :], g.experts[bass.ds(e, 1), :, :].rearrange("o p c -> p (o c)")).then_inc(s_stage[s], 16)

            def start_sums(n):
                sp.dma_start(g.acc_r[1][bass.ds(n, 1), :, :], g.x_r[bass.ds(n, 1), :, :]).then_inc(s_acc, 16)

            def store_shared(n):
                held_wait(sp, s_ysh, KT * (n + 1))
                sp.dma_start(g.acc_b[0][:, bass.ds(n, 1), :, :].rearrange("p o j d -> p (o j) d"), ysh[:]).then_inc(s_st, 16)

            load_front(0)
            load_pid(0, 0)
            load_pid(1, 1)
            sp.dma_start(cst[:], g.consts).then_inc(s_c1, 16)
            sp.dma_start(awt, g.aw).then_inc(s_c1, 16)
            sp.dma_start(rawtab[:], g.tabs).then_inc(s_c1, 16)
            sp.dma_start(raw[:], g.int_w1).then_inc(s_c2, 16)
            sp.dma_start(m_in, g.mlp_in).then_inc(s_c3, 16)
            sp.dma_start(m_cols, g.mlp_cols).then_inc(s_c3, 16)
            sp.dma_start(m_w1[:], g.mlp_w1).then_inc(s_c3, 16)
            sp.dma_start(m_w2[:], g.mlp_w2).then_inc(s_c3, 16)
            sp.dma_start(m_b2[:], g.mlp_b2).then_inc(s_c3, 16)
            sp.dma_start(rawtb[:], g.tab_b).then_inc(s_c4, 16)
            sp.dma_start(b1, g.int_b1).then_inc(s_c4, 16)
            sp.dma_start(nbc[:], g.norm_bc).then_inc(s_c5, 16)
            sp.dma_start(rawg[:], g.gate).then_inc(s_c5, 16)
            sp.dma_start(rawo[:], g.int_w2).then_inc(s_c5, 16)
            for c in (0, 1):
                load_chunk(c, (c - 1) % NCHUNK, c % 2)
            load_front(1)
            for c in range(2, SETUP_EXPERTS + 1):
                load_chunk(c, c - 1, c % 2)
            sp.wait_ge(s_k, 1)
            for a in range(NACC):
                for t in range(BT):
                    sp.dma_start(g.accs[a][T + t * P:T + (t + 1) * P, :], zeros[:]).then_inc(s_acc, 16)

            def back(n, par):
                start_sums(n)
                c = n + SETUP_EXPERTS + 1
                load_chunk(c, c - 1, (par + SETUP_EXPERTS + 1) % 2)

            def step(n, par, front, prev):
                back(n, par)
                if prev:
                    store_shared(n - 1)
                if front:
                    load_front(n + 2)
                    load_pid(n + 2, par)

            step(0, 0, True, False)
            with sp.Fori(0, NB // 2 - 2) as m:
                for q in (1, 2):
                    step(2 * m + q, q % 2, True, True)
            step(NB - 3, 1, True, True)
            step(NB - 2, 0, False, True)
            start_sums(NB - 1)
            store_shared(NB - 2)
            for e in range(NE - NLATE, NE):
                load_chunk(e + 1, e, (e + 1) % 2)
            store_shared(NB - 1)
            sp.wait_ge(s_acc, 16 * (NACC * BT + NB))
            sp.wait_ge(s_st, 16 * (NB + 1))

        @block.gpsimd
        def _(pool):
            pool.memset(neghalf[:], -0.5).then_inc(s_pk, 1)
            pool.memset(ones_bf[:], 1.0).then_inc(s_pk, 1)

            def rstd(rs, ve, s_ve, s_rs, n):
                pool.wait_ge(s_ve, n + 1)
                pool.tensor_tensor(rs[:], ve[:], neghalf[:, 0:TJ], ALU.pow).then_inc(s_rs, 1)

            def gathers(n, par):
                pool.wait_ge(s_pid[par], 8 * (n - par) + 16)
                wait_past(pool, s_hhT, KT * n)
                held(pool)
                for j in range(TJ):
                    pool.indirect_dma_start(gt[:, j, :], None, g.pw_tab,
                                            bass.IndirectOffsetOnAxis(ap=pid[:, par, j:j + 1], axis=0)).then_inc(s_gt, 16)

            def shift(n):
                pool.wait_ge(s_u1, n + 1)
                pool.tensor_tensor(gt[:, :, 0:D], gt[:, :, 0:D], gt[:, :, D:2 * D], ALU.add).then_inc(s_u2, 1)

            def scatter(n, par, first, last):
                if first == 0:
                    pool.wait_ge(s_pay, n + 1)
                    pool.wait_ge(s_idx, n + 1)
                    held(pool)
                for q in range(first, last):
                    j, k = q // TOPK, q % TOPK
                    pool.indirect_dma_start(g.xlist, bass.IndirectOffsetOnAxis(ap=idx[par][:, j, k:k + 1], axis=0),
                                            pay[par][:, j, :], None).then_inc(s_sc[par], 16)

            gathers(0, 0)
            pool.wait_ge(s_pk, 2)
            rstd(rs1, ve1, s_ve1, s_rs1, 0)
            shift(0)
            rstd(rs2, ve2, s_ve2, s_rs2, 0)
            pool.wait_ge(s_k, K_MVE)
            pool.tensor_tensor(tmp[0:96, 1:2], tmp[0:96, 0:1], neghalf[0:96, 0:1], ALU.pow).then_inc(s_pk, 1)
            gathers(1, 1)

            def step(n, par, front, prev, ahead):
                if front:
                    rstd(rs1, ve1, s_ve1, s_rs1, n + 1)
                    shift(n + 1)
                if prev:
                    scatter(n - 1, 1 - par, 0, 3)
                if front:
                    rstd(rs2, ve2, s_ve2, s_rs2, n + 1)
                if prev:
                    scatter(n - 1, 1 - par, 3, 12)
                rstd(rs3, ve3, s_ve3, s_rs3, n)
                if prev:
                    scatter(n - 1, 1 - par, 12, 16)
                if ahead:
                    gathers(n + 2, par)

            step(0, 0, True, False, True)
            with pool.Fori(0, NB // 2 - 2) as m:
                for q in (1, 2):
                    step(2 * m + q, q % 2, True, True, True)
            step(NB - 3, 1, True, True, True)
            step(NB - 2, 0, True, True, False)
            step(NB - 1, 1, False, True, False)
            scatter(NB - 1, 1, 0, 16)
            for p in (0, 1):
                pool.wait_ge(s_sc[p], 16 * TOPK * TJ * (NB // 2))

        @block.scalar
        def _(act):
            def x_hi(n, h):
                if n is not None:
                    act.wait_ge(s_xT, KT * n + h + 1)
                    wait_past(act, s_hid, KT * n)
                    act.activation(xs[:, 0, h, :], tb[h][:], ACT.Copy).then_inc(s_xhi, 1)

            def x_norm(n):
                act.wait_ge(s_nm1, n + 1)
                wait_past(act, s_xhT, KT * n)
                held(act)
                for j in range(TJ):
                    act.activation(xh[:, j, :], xt[:, j, :], ACT.Identity, bias=nm1[:, j:j + 1],
                                   scale=rs1[:, j:j + 1]).then_inc(s_xh, 1)

            def h_norm(n):
                act.wait_ge(s_nm2, n + 1)
                held(act)
                for j in range(TJ):
                    act.activation(gt[:, j, 0:D], gt[:, j, 0:D], ACT.Identity, bias=nm2[:, j:j + 1],
                                   scale=rs2[:, j:j + 1]).then_inc(s_hh, 1)

            def xh_copy(n, h):
                act.wait_ge(s_xhT, KT * n + h + 1)
                wait_past(act, s_prod, 6 * n)
                act.activation(xhT[:, h, :], tb[h][:], ACT.Copy).then_inc(s_xhc, 1)

            def hh_copy(n, h):
                act.wait_ge(s_hhT, KT * n + h + 1)
                act.activation(hhT[:, h, :], tb[h][:], ACT.Copy).then_inc(s_hhc, 1)

            def p_hi(n, q):
                act.wait_ge(s_prod, 6 * n + q + 1)
                act.activation(xs[:, 0, kslot(q), :], prod[:, q % 3, :], ACT.Copy).then_inc(s_phi, 1)

            def silu(n, h):
                act.wait_ge(s_hid, KT * n + h + 1)
                wait_past(act, s_alo, n)
                wait_past(act, s_ys, KT * n)
                held(act)
                act.activation(sact[:, h, :], hb[h][:], ACT.Silu, bias=vbias[:, h, bass.ds(n, 1)]).then_inc(s_silu, 1)
                act.wait_ge(s_silu, KT * n + h + 1)
                act.activation(ssp[:, 0, h, :], sact[:, h, :], ACT.Copy).then_inc(s_shi, 1)

            def c_hi(n, h):
                act.wait_ge(s_cT, KT * n + h + 1)
                wait_past(act, s_h, 2 * n)
                act.activation(csp[:, 0, h, :], tb[h][:], ACT.Copy).then_inc(s_chi, 1)

            def logits_copy(n):
                act.wait_ge(s_lgT, n + 1)
                act.activation(lgT, Y0[0:NE, :], ACT.Copy).then_inc(s_lgc, 1)

            def exps(n):
                act.wait_ge(s_top, TOPS * n + 5)
                act.activation(ex[:], ex[:], ACT.Exp).then_inc(s_exp, 1)

            def shared_silu(n):
                act.wait_ge(s_h, 2 * n + 1)
                act.wait_ge(s_slo, KT * n + KT)
                act.activation(sact[:, 0, :], gb[0][:], ACT.Silu).then_inc(s_ss, 1)

            def shared_hi(n):
                act.wait_ge(s_sa, n + 1)
                act.wait_ge(s_y2, TJ * n + TJ)
                act.activation(ssp[:, 0, 0, :], sact[:, 1, :], ACT.Copy).then_inc(s_ahi, 1)

            def shared_out(n):
                for b in (0, 1):
                    act.wait_ge(s_ys, 2 * n + b + 1)
                    if b == 0:
                        act.wait_ge(s_st, 16 * (n + 1))
                    act.activation(ysh[:, 2 * b:2 * b + 2, :].rearrange("p j d -> p (j d)"), gb[b][:], ACT.Copy).then_inc(s_ysh, 1)

            def split_hi(c, dst, s):
                act.wait_ge(s_stage[s], 16 * (c // 2 + 1))
                act.activation(dst, stage[:, s, :], ACT.Copy).then_inc(s_split_hi, 1)

            def split_hi_n(n, par):
                s = (par + SETUP_EXPERTS + 1) % 2
                act.wait_ge(s_stage[s], 8 * (n + SETUP_EXPERTS + 1 - s) + 16)
                held(act)
                act.activation(wff[:, bass.ds(n + SETUP_EXPERTS, 1), 0, :].rearrange("p o c -> p (o c)"),
                               stage[:, s, :], ACT.Copy).then_inc(s_split_hi, 1)

            act.wait_ge(s_k, K_AWD)
            act.activation(w6, w6, ACT.Exp).then_inc(s_ak, 1)
            x_norm(0)
            act.wait_ge(s_ek, 1)
            act.wait_ge(s_c3, 80)
            for i in range(3):
                for h in range(KT):
                    ins = act.activation(m_h[:, i, h, :], H0[:, (i * KT + h) * 32:(i * KT + h) * 32 + 32], ACT.Silu,
                                         bias=m_cols[:, 0, h, i:i + 1])
            ins.then_inc(s_ak, 1)
            act.wait_ge(s_c1, 48)
            act.activation(tabhi[:], rawtab[:], ACT.Copy).then_inc(s_ak, 1)
            act.sem_inc(s_st, 16)
            for h in (0, 1):
                xh_copy(0, h)
            for h in (0, 1):
                x_hi(0, h)
            act.wait_ge(s_k, K_WM)
            for k, src in enumerate((wm[:], raw[:, 0, :, :], raw[:, 1, :, :], raw[:, 5, :, :])):
                ins = act.activation(wint[:, 0, KT * k:KT * k + KT, :], src, ACT.Copy)
            ins.then_inc(s_ak, 1)
            for q in range(4):
                p_hi(0, q)
            h_norm(0)
            for h in (0, 1):
                hh_copy(0, h)
            act.wait_ge(s_ek, 3)
            act.wait_ge(s_k, K_TAB)
            act.activation(tabhi[:, 0, :], Y0[0:SEL, 0:D], ACT.Copy).then_inc(s_ak, 1)
            act.wait_ge(s_c5, 48)
            act.activation(wgate[:, 0, :, :], rawg[:], ACT.Copy)
            act.activation(wout[:, 0, :, :], rawo[:], ACT.Copy).then_inc(s_ak, 1)
            for q in range(4, 6):
                p_hi(0, q)
            for c in range(SETUP_EXPERTS + 1):
                split_hi(c, wsh[:, 0, :] if c == 0 else wff[:, c - 1, 0, :], c % 2)

            def step(n, front, prev):
                if prev:
                    logits_copy(n - 1)
                    shared_silu(n - 1)
                if front:
                    x_norm(n + 1)
                if prev:
                    shared_hi(n - 1)
                    exps(n - 1)
                if prev:
                    shared_out(n - 1)
                silu(n, 0)
                if front:
                    for h in (0, 1):
                        xh_copy(n + 1, h)
                    h_norm(n + 1)
                silu(n, 1)
                if front:
                    for h in (0, 1):
                        x_hi(n + 1, h)
                    for q in (0, 1, 2, 3):
                        p_hi(n + 1, q)
                    for h in (0, 1):
                        hh_copy(n + 1, h)
                    for q in (4, 5):
                        p_hi(n + 1, q)
                for h in (0, 1):
                    c_hi(n, h)

            step(0, True, False)
            split_hi_n(0, 0)
            with act.Fori(0, NB // 2 - 1) as m:
                for q in (1, 2):
                    step(2 * m + q, True, True)
                    split_hi_n(2 * m + q, q % 2)
            step(NB - 1, False, True)
            logits_copy(NB - 1)
            shared_silu(NB - 1)
            shared_hi(NB - 1)
            exps(NB - 1)
            shared_out(NB - 1)
            for e in range(NE - NLATE, NE):
                split_hi(e + 1, wff[:, e, 0, :], (e + 1) % 2)

        @block.tensor
        def _(pe):
            def three(out, l, r, start=True, stop=True):
                pe.matmul(out, l(0), r(0), start=start, stop=False)
                pe.matmul(out, l(0), r(1), start=False, stop=False)
                return pe.matmul(out, l(1), r(0), start=False, stop=stop)

            def turn(h, src):
                for j in range(TJ):
                    mm = pe.transpose(tb[h][:, j * P:(j + 1) * P], src(j, h), ident)
                return mm

            def turn_x(n):
                pe.wait_ge(s_x, 16 * (n + 1))
                for h in (0, 1):
                    pe.wait_ge(s_xhc, KT * n + h + 1)
                    turn(h, lambda j, h: xt[:, j, h * P:(h + 1) * P]).then_inc(s_xT, 1)

            def turn_xh(n):
                pe.wait_ge(s_xh, TJ * (n + 1))
                for h in (0, 1):
                    wait_past(pe, s_hhc, KT * (n - 1) + h + 1)
                    turn(h, lambda j, h: xh[:, j, h * P:(h + 1) * P]).then_inc(s_xhT, 1)

            def turn_c(n, par, front):
                pe.wait_ge(s_cn, TJ * (n + 1))
                for h in (0, 1):
                    pe.wait_ge(s_hhc, KT * (n + 1 if front else n) + h + 1)
                    turn(h, lambda j, h: pay[par][:, j, h * P:(h + 1) * P]).then_inc(s_cT, 1)

            def turn_hh(n):
                pe.wait_ge(s_hh, TJ * (n + 1))
                for h in (0, 1):
                    pe.wait_ge(s_xhi, KT * n + h + 1)
                    pe.wait_ge(s_xlo, KT * n + h + 1)
                    turn(h, lambda j, h: gt[:, j, h * P:(h + 1) * P]).then_inc(s_hhT, 1)

            def gains(n, q):
                table, h = (1, 1, 2, 2, 0, 0)[q], q % 2
                pe.wait_ge(s_oh, n + 1)
                if q < 2:
                    wait_past(pe, s_ysh, KT * (n - 1))
                else:
                    pe.wait_ge(s_prod, 6 * n + q - 1)
                pe.matmul(gb[q % 2][:], tab[:, table, h * P:(h + 1) * P], oh[:], start=True, stop=True).then_inc(s_g, 1)

            def hidden(n, h):
                pe.wait_ge(s_xlo, KT * (n + 1))
                pe.wait_ge(s_plo, 6 * n + 4)
                for k in (0, 1, 4, 5, 6, 7, 2, 3):
                    if h == 0 and k == 2:
                        pe.wait_ge(s_plo, 6 * (n + 1))
                    three(hb[h][:], lambda w: wint[:, w, k, h * P:(h + 1) * P], lambda w: xs[:, w, k, :],
                          start=(k == 0), stop=False)
                pe.matmul(hb[h][:], btab[:, h * P:(h + 1) * P], oh[:], start=False, stop=True).then_inc(s_hid, 1)

            def second(n):
                wait_past(pe, s_idx, n)
                pe.wait_ge(s_shi, KT * (n + 1))
                pe.wait_ge(s_slo, KT * (n + 1))
                for j in range(TJ):
                    o = yb[j // 2][:, (j % 2) * D:(j % 2 + 1) * D]
                    for k in range(KT):
                        three(o, lambda w: ssp[:, w, k, j * P:(j + 1) * P], lambda w: wout[:, w, k, :],
                              start=(k == 0), stop=False)
                    pe.matmul(o, ones[:], tab[:, 3, :], start=False, stop=True).then_inc(s_y2, 1)

            def logits(n):
                pe.wait_ge(s_chi, KT * (n + 1))
                pe.wait_ge(s_clo, KT * (n + 1))
                for k in range(KT):
                    mm = three(Y0[0:NE, :], lambda w: wgate[:, w, k, :], lambda w: csp[:, w, k, :],
                               start=(k == 0), stop=(k == KT - 1))
                mm.then_inc(s_lgT, 1)

            def turn_logits(n):
                pe.wait_ge(s_lgc, n + 1)
                held(pe)
                for j in range(TJ):
                    mm = pe.transpose(Y1[:, P + j * NE:P + (j + 1) * NE], lgT[:, j * P:(j + 1) * P], ident[0:NE, 0:NE])
                mm.then_inc(s_gate, 1)

            def shared_first(n, after):
                pe.wait_ge(s_prod, 6 * (after + 1))
                for i in (0, 1):
                    for k in range(KT):
                        mm = three(gb[i][:], lambda w: wsh[:, w, k * 2 * HID + i * HID:k * 2 * HID + (i + 1) * HID],
                                   lambda w: csp[:, w, k, :], start=(k == 0), stop=(k == KT - 1))
                    mm.then_inc(s_h, 1)

            def ranks(n):
                pe.wait_ge(s_top, TOPS * n + 6)
                pe.matmul(Y1[:, 0:TJ * NE], upper[:], mask[:].rearrange("p j e -> p (j e)"), start=True, stop=False,
                          skip_group_check=True)
                for d in range(1, TJ):
                    pe.matmul(Y1[:, d * NE:TJ * NE], ones_bf[:], mask[:, 0:TJ - d, :].rearrange("p j e -> p (j e)"),
                              start=False, stop=(d == TJ - 1), skip_group_check=True)
                for j in range(TJ):
                    mm = pe.matmul(Y1[:, TJ * NE:(TJ + 1) * NE], ones_bf[:], mask[:, j, :], start=(j == 0),
                                   stop=(j == TJ - 1), skip_group_check=True)
                mm.then_inc(s_rank, 1)

            def shared_second(n):
                pe.wait_ge(s_ahi, n + 1)
                pe.wait_ge(s_alo, n + 1)
                for b in (0, 1):
                    for j in (2 * b, 2 * b + 1):
                        mm = three(gb[b][:, (j % 2) * D:(j % 2 + 1) * D], lambda w: ssp[:, w, 0, j * P:(j + 1) * P],
                                   lambda w: wsh[:, w, KT * 2 * HID:EW])
                    mm.then_inc(s_ys, 1)

            pe.wait_ge(s_c3, 80)
            for i in range(3):
                for h in range(KT):
                    mm = pe.matmul(H0[:, (i * KT + h) * 32:(i * KT + h) * 32 + 32], m_w1[:, i, h * P:(h + 1) * P],
                                   m_in[:, i, :], start=True, stop=True)
            mm.then_inc(s_ek, 1)
            pe.wait_ge(s_ak, 2)
            for i in range(3):
                for k in range(KT):
                    mm = pe.matmul(H1[32 * i:32 * i + 32, 0:D], m_h[:, i, k, :], m_w2[:, i, k, :],
                                   start=(k == 0), stop=(k == KT - 1))
            mm.then_inc(s_ek, 1)
            pe.wait_ge(s_c1, 48)
            turn_xh(0)
            turn_x(0)
            pe.wait_ge(s_c4, 32)
            pe.wait_ge(s_k, K_WM)
            for q, (t, w) in enumerate(((0, 0), (1, 1), (2, 5))):
                for k in range(KT):
                    mm = pe.matmul(Y0[0:SEL, 0:D], rawtb[:, t, k, :], raw[:, w, k, :], start=(q + k == 0),
                                   stop=(q == 2 and k == KT - 1))
            mm.then_inc(s_ek, 1)
            pe.wait_ge(s_k, K_TAB)
            for q in range(4):
                gains(0, q)
            pe.wait_ge(s_k, K_MLN)
            for k in range(KT):
                mm = pe.transpose(Y1[:, k * 96:(k + 1) * 96], m_b2[0:96, k * P:(k + 1) * P], ident[0:96, 0:96])
            mm.then_inc(s_ek, 1)
            turn_hh(0)
            for q in range(4, 6):
                gains(0, q)
            pe.wait_ge(s_k, K_MT)
            for h in range(KT):
                for i in range(3):
                    for k in range(KT):
                        mm = pe.matmul(H0[:, h * NB:(h + 1) * NB], raw[:, 2 + i, k, h * P:(h + 1) * P], m_t[:, i, k, :],
                                       start=(i + k == 0), stop=(i == 2 and k == KT - 1))
            mm.then_inc(s_ek, 1)
            pe.wait_ge(s_k, K_END)
            pe.wait_ge(s_ak, 6)
            pe.wait_ge(s_split_hi, 1)
            pe.wait_ge(s_split_lo, 1)

            def step(n, par, front, prev):
                if prev:
                    logits(n - 1)
                    shared_first(n - 1, n)
                    turn_logits(n - 1)
                hidden(n, 0)
                if prev:
                    ranks(n - 1)
                    shared_second(n - 1)
                if front:
                    turn_xh(n + 1)
                hidden(n, 1)
                if front:
                    turn_x(n + 1)
                    for q in (0, 1):
                        gains(n + 1, q)
                second(n)
                if front:
                    for q in (2, 3):
                        gains(n + 1, q)
                    turn_hh(n + 1)
                    for q in (4, 5):
                        gains(n + 1, q)
                turn_c(n, par, front)

            step(0, 0, True, False)
            with pe.Fori(0, NB // 2 - 1) as m:
                for q in (1, 2):
                    step(2 * m + q, q % 2, True, True)
            step(NB - 1, 1, False, True)
            logits(NB - 1)
            shared_first(NB - 1, NB - 1)
            turn_logits(NB - 1)
            ranks(NB - 1)
            shared_second(NB - 1)

        @block.vector
        def _(v):
            def stats(n, src, st, mv, ve, s_bn, s_mv, s_ve):
                for j in range(TJ):
                    v.bn_stats(st[:, j, :], src(j)).then_inc(s_bn, 1)
                for j in range(TJ):
                    if j == 0:
                        v.wait_ge(s_bn, TJ * (n + 1))
                        held(v)
                    v.bn_aggr(mv[:, j, :], st[:, j, :]).then_inc(s_mv, 1)
                v.wait_ge(s_mv, TJ * (n + 1))
                v.tensor_scalar(ve[:], mv[:, :, 1:2].rearrange("p j o -> p (j o)"), EPS, None, ALU.add).then_inc(s_ve, 1)

            def x_stats(n):
                v.wait_ge(s_x, 16 * (n + 1))
                stats(n, lambda j: xt[:, j, :], st1, mv1, ve1, s_bn1, s_mv1, s_ve1)

            def x_shift(n):
                v.wait_ge(s_rs1, n + 1)
                v.scalar_tensor_tensor(nm1[:], mv1[:, :, 0:1].rearrange("p j o -> p (j o)"), -1.0, rs1[:], ALU.mult,
                                       ALU.mult).then_inc(s_nm1, 1)

            def gain(n):
                v.wait_ge(s_gt, 16 * TJ * (n + 1))
                v.wait_ge(s_xh, TJ * (n + 1))
                v.tensor_tensor(gt[:, :, 0:D], gt[:, :, 0:D], xh[:], ALU.mult).then_inc(s_u1, 1)

            def h_stats(n):
                v.wait_ge(s_u2, n + 1)
                stats(n, lambda j: gt[:, j, 0:D], st2, mv2, ve2, s_bn2, s_mv2, s_ve2)

            def h_shift(n):
                v.wait_ge(s_rs2, n + 1)
                v.scalar_tensor_tensor(nm2[:], mv2[:, :, 0:1].rearrange("p j o -> p (j o)"), -1.0, rs2[:], ALU.mult,
                                       ALU.mult).then_inc(s_nm2, 1)

            def onehot(n):
                v.wait_ge(s_ids, 16 * (n + 1))
                wait_past(v, s_hid, KT * n)
                v.tensor_scalar(oh[:], ids[:], cst[0:SEL, C_SEL:C_SEL + 1], None, ALU.is_equal).then_inc(s_oh, 1)

            def x_lo(n, h):
                v.wait_ge(s_xhi, KT * n + h + 1)
                v.tensor_tensor(xs[:, 1, h, :], tb[h][:], xs[:, 0, h, :].bitcast(F32), ALU.subtract).then_inc(s_xlo, 1)

            def product(n, q):
                h = q % 2
                v.wait_ge(s_g, 6 * n + q + 1)
                v.wait_ge(s_xhc if q < 4 else s_hhc, KT * n + h + 1)
                wait_past(v, s_plo, 6 * n + q - 2)
                v.tensor_tensor(prod[:, q % 3, :], gb[q % 2][:], (xhT if q < 4 else hhT)[:, h, :], ALU.mult).then_inc(s_prod, 1)

            def p_lo(n, q):
                v.wait_ge(s_phi, 6 * n + q + 1)
                v.tensor_tensor(xs[:, 1, kslot(q), :], prod[:, q % 3, :], xs[:, 0, kslot(q), :].bitcast(F32),
                                ALU.subtract).then_inc(s_plo, 1)

            def silu_lo(n, h):
                v.wait_ge(s_shi, KT * n + h + 1)
                v.tensor_tensor(ssp[:, 1, h, :], sact[:, h, :], ssp[:, 0, h, :].bitcast(F32), ALU.subtract).then_inc(s_slo, 1)

            def c_stats(n):
                v.wait_ge(s_y2, TJ * (n + 1))
                stats(n, lambda j: yb[j // 2][:, (j % 2) * D:(j % 2 + 1) * D], st3, mv3, ve3, s_bn3, s_mv3, s_ve3)

            def c_rows(n, par):
                for j in range(TJ):
                    v.scalar_tensor_tensor(pay[par][:, j, 0:D], yb[j // 2][:, (j % 2) * D:(j % 2 + 1) * D],
                                           mv3[:, j, 0:1], nbc[:, 0, :], ALU.subtract, ALU.mult).then_inc(s_c, 1)
                v.wait_ge(s_rs3, n + 1)
                v.wait_ge(s_c, TJ * (n + 1))
                for j in range(TJ):
                    v.scalar_tensor_tensor(pay[par][:, j, 0:D], pay[par][:, j, 0:D], rs3[:, j:j + 1], nbc[:, 1, :],
                                           ALU.mult, ALU.add).then_inc(s_cn, 1)

            def c_lo(n, h):
                v.wait_ge(s_chi, KT * n + h + 1)
                v.tensor_tensor(csp[:, 1, h, :], tb[h][:], csp[:, 0, h, :].bitcast(F32), ALU.subtract).then_inc(s_clo, 1)

            def top_first(n):
                v.wait_ge(s_gate, n + 1)
                v.tensor_copy(lg[:, :, 0:NE], Y1[:, P:P + TJ * NE].rearrange("p (j e) -> p j e", j=TJ)).then_inc(s_top, 1)
                v.wait_ge(s_top, TOPS * n + 1)
                held(v)
                for j in range(TJ):
                    ins = v.max(top8[:, j, :], lg[:, j, 0:NE])
                ins.then_inc(s_top, 1)
                v.wait_ge(s_top, TOPS * n + 2)
                v.tensor_copy(rep8[:, :, 0:TOPK], top8[:, :, 0:TOPK]).then_inc(s_top, 1)
                v.wait_ge(s_top, TOPS * n + 3)
                held(v)
                for j in range(TJ):
                    ins = v.match_replace(repl[:, j, :], rep8[:, j, :], lg[:, j, :], -BIG)
                ins.then_inc(s_top, 1)
                v.tensor_tensor(ex[:], lg[:, :, 0:NE], top8[:, :, 0:1].broadcast_to((P, TJ, NE)), ALU.subtract).then_inc(s_top, 1)
                v.wait_ge(s_top, TOPS * n + 4)
                v.tensor_scalar(mask[:], repl[:, :, 0:NE], -BIG, None, ALU.is_equal).then_inc(s_top, 1)

            def top_second(n, par):
                v.wait_ge(s_exp, n + 1)
                v.wait_ge(s_top, TOPS * n + 6)
                v.tensor_tensor(ex[:], ex[:], mask[:], ALU.mult).then_inc(s_top, 1)
                tok = pay[par][:, :, COL_TOK:COL_TOK + 1].bitcast(I32)
                v.tensor_scalar(tok, tok, float(2 * S), None, ALU.add).then_inc(s_top, 1)
                v.wait_ge(s_top, TOPS * n + 7)
                v.tensor_reduce(exs[:], ex[:], AX.X, ALU.add).then_inc(s_top, 1)
                v.wait_ge(s_rank, n + 1)
                v.tensor_tensor(slot[:], Y1[:, 0:TJ * NE].rearrange("p (j e) -> p j e", j=TJ),
                                base[:].rearrange("p (o e) -> p o e", o=1).broadcast_to((P, TJ, NE)), ALU.add).then_inc(s_top, 1)
                v.wait_ge(s_top, TOPS * n + 10)
                v.reciprocal(exs[:], exs[:]).then_inc(s_top, 1)
                v.tensor_tensor(slot[:], slot[:], mask[:], ALU.mult).then_inc(s_top, 1)
                v.wait_ge(s_top, TOPS * n + 12)
                held(v)
                v.tensor_tensor(pay[par][:, :, COL_W:COL_W + NE], ex[:],
                                exs[:].rearrange("p (j o) -> p j o", o=1).broadcast_to((P, TJ, NE)), ALU.mult).then_inc(s_pay, 1)
                for j in range(TJ):
                    ins = v.max(slot8[:, j, :], slot[:, j, :])
                ins.then_inc(s_top, 1)
                v.tensor_tensor(base[:], base[:], Y1[:, TJ * NE:(TJ + 1) * NE], ALU.add).then_inc(s_top, 1)
                v.wait_ge(s_top, TOPS * n + 14)
                v.tensor_scalar(idx[par][:], slot8[:, :, 0:TOPK], -1.0, None, ALU.add).then_inc(s_idx, 1)

            def shared_act(n):
                v.wait_ge(s_ss, n + 1)
                v.wait_ge(s_h, 2 * n + 2)
                v.tensor_tensor(sact[:, 1, :], sact[:, 0, :], gb[1][:], ALU.mult).then_inc(s_sa, 1)

            def shared_lo(n):
                v.wait_ge(s_ahi, n + 1)
                v.tensor_tensor(ssp[:, 1, 0, :], sact[:, 1, :], ssp[:, 0, 0, :].bitcast(F32), ALU.subtract).then_inc(s_alo, 1)

            def split_lo(c, w, e, s):
                v.wait_ge(s_split_hi, c + 1)
                v.tensor_tensor(w[:, e, 1, :] if e is not None else w[:, 1, :], stage[:, s, :],
                                (w[:, e, 0, :] if e is not None else w[:, 0, :]).bitcast(F32), ALU.subtract).then_inc(s_split_lo, 1)

            def split_lo_n(n, par):
                s = (par + SETUP_EXPERTS + 1) % 2
                e = bass.ds(n + SETUP_EXPERTS, 1)
                v.wait_ge(s_split_hi, n + SETUP_EXPERTS + 2)
                v.tensor_tensor(wff[:, e, 1, :].rearrange("p o c -> p (o c)"), stage[:, s, :],
                                wff[:, e, 0, :].rearrange("p o c -> p (o c)").bitcast(F32), ALU.subtract).then_inc(s_split_lo, 1)

            count = [0]

            def k(ins):
                count[0] += 1
                ins.then_inc(s_k, 1)

            def seen():
                v.wait_ge(s_k, count[0])

            k(v.memset(zeros[:], 0.0))
            v.memset(lg[:, :, NE:24], BIG)
            v.memset(rep8[:, :, TOPK:8], BIG)
            x_stats(0)
            v.wait_ge(s_c1, 48)
            seen()
            k(v.tensor_reduce(tmp[:, 2:3], awt, AX.X, ALU.max))
            k(v.tensor_copy(base[:], cst[:, C_CAP:C_CAP + NE]))
            seen()
            k(v.tensor_scalar(w6, awt, tmp[:, 2:3], None, ALU.subtract))
            assert count[0] == K_AWD, count
            k(v.tensor_copy(upper[:], cst[:, C_UP:C_UP + P]))
            k(v.tensor_scalar(ones[:], cst[0:SEL, C_UP:C_UP + P], 0.0, 1.0, ALU.mult, ALU.add))
            v.wait_ge(s_ak, 1)
            k(v.tensor_reduce(tmp[:, 3:4], w6, AX.X, ALU.add))
            x_shift(0)
            gain(0)
            seen()
            k(v.reciprocal(tmp[:, 4:5], tmp[:, 3:4]))
            seen()
            k(v.tensor_scalar(w6, w6, tmp[:, 4:5], None, ALU.mult))
            seen()
            v.wait_ge(s_c2, 16)
            for i in range(6):
                ins = v.tensor_scalar(raw[:, i, :, :], raw[:, i, :, :], w6[:, i:i + 1], None, ALU.mult)
            k(ins)
            onehot(0)
            for h in (0, 1):
                x_lo(0, h)
            seen()
            k(v.tensor_tensor(wm[:], raw[:, 2, :, :], raw[:, 3, :, :], ALU.add))
            seen()
            k(v.tensor_tensor(wm[:], wm[:], raw[:, 4, :, :], ALU.add))
            assert count[0] == K_WM, count
            v.wait_ge(s_ak, 3)
            v.tensor_copy(tab[0:32, :, :], tabhi[0:32, :, :])
            k(v.tensor_tensor(tab[32:64, :, :], rawtab[32:64, :, :], tabhi[32:64, :, :].bitcast(F32), ALU.subtract))
            assert count[0] == K_TAB, count
            v.wait_ge(s_ek, 2)
            v.wait_ge(s_c3, 80)
            k(v.tensor_tensor(m_b2[:], H1[0:96, 0:D], m_b2[:], ALU.add))
            seen()
            k(v.bn_stats(tmp[0:96, 8:14], m_b2[:]))
            seen()
            k(v.bn_aggr(tmp[0:96, 14:16], tmp[0:96, 8:14]))
            seen()
            k(v.tensor_scalar(tmp[0:96, 0:1], tmp[0:96, 15:16], EPS, None, ALU.add))
            assert count[0] == K_MVE, count
            for q in range(2):
                product(0, q)
            for q in range(2):
                p_lo(0, q)
            h_stats(0)
            v.wait_ge(s_pk, 3)
            k(v.tensor_scalar(m_b2[:], m_b2[:], tmp[0:96, 14:15], tmp[0:96, 1:2], ALU.subtract, ALU.mult))
            assert count[0] == K_MLN, count
            for q in range(2, 4):
                product(0, q)
            for q in range(2, 4):
                p_lo(0, q)
            h_shift(0)
            v.wait_ge(s_ek, 4)
            for i in range(3):
                for kt in range(KT):
                    ins = v.tensor_scalar(m_t[:, i, kt, :], Y1[:, kt * 96 + 32 * i:kt * 96 + 32 * i + NB],
                                          m_cols[:, 1, kt, i:i + 1], m_cols[:, 2, kt, i:i + 1], ALU.mult, ALU.add)
            k(ins)
            assert count[0] == K_MT, count
            v.wait_ge(s_ak, 4)
            for q, src in enumerate((wm[:], raw[:, 0, :, :], raw[:, 1, :, :], raw[:, 5, :, :])):
                ins = v.tensor_tensor(wint[:, 1, KT * q:KT * q + KT, :], src, wint[:, 0, KT * q:KT * q + KT, :].bitcast(F32),
                                      ALU.subtract)
            k(ins)
            for q in range(4, 6):
                product(0, q)
            for q in range(4, 6):
                p_lo(0, q)
            v.wait_ge(s_ak, 5)
            v.tensor_copy(btab[0:32, :], tabhi[0:32, 0, :])
            k(v.tensor_tensor(btab[32:64, :], Y0[32:64, 0:D], tabhi[32:64, 0, :].bitcast(F32), ALU.subtract))
            v.wait_ge(s_ak, 6)
            v.tensor_tensor(wgate[:, 1, :, :], rawg[:], wgate[:, 0, :, :].bitcast(F32), ALU.subtract)
            k(v.tensor_tensor(wout[:, 1, :, :], rawo[:], wout[:, 0, :, :].bitcast(F32), ALU.subtract))
            v.wait_ge(s_ek, 5)
            v.wait_ge(s_c4, 32)
            for h in range(KT):
                ins = v.tensor_scalar(vbias[:, h, :], H0[:, h * NB:(h + 1) * NB], b1[:, h:h + 1], None, ALU.add)
            k(ins)
            seen()
            for p in (0, 1):
                v.memset(pay[p][:, :, D:ROW], 0.0).then_inc(s_k, 1)
            count[0] += 2
            seen()
            for p in (0, 1):
                ins = v.tensor_scalar(pay[p][:, :, COL_TOK:COL_TOK + 1].bitcast(I32),
                                      cst[:, C_TOK:C_TOK + TJ].rearrange("p (j o) -> p j o", o=1), float((p - 2) * S),
                                      None, ALU.add)
            k(ins)
            assert count[0] == K_END, count
            seen()
            for c in range(SETUP_EXPERTS + 1):
                split_lo(c, wsh if c == 0 else wff, None if c == 0 else c - 1, c % 2)

            def step(n, par, front, prev):
                if front:
                    x_stats(n + 1)
                    x_shift(n + 1)
                if prev:
                    shared_act(n - 1)
                    top_first(n - 1)
                    shared_lo(n - 1)
                if front:
                    gain(n + 1)
                if prev:
                    top_second(n - 1, 1 - par)
                if front:
                    h_stats(n + 1)
                silu_lo(n, 0)
                if front:
                    h_shift(n + 1)
                    onehot(n + 1)
                silu_lo(n, 1)
                if front:
                    for h in (0, 1):
                        x_lo(n + 1, h)
                    for q in (0, 1):
                        product(n + 1, q)
                    for q in (0, 1):
                        p_lo(n + 1, q)
                c_stats(n)
                if front:
                    for q in (2, 3):
                        product(n + 1, q)
                c_rows(n, par)
                if front:
                    for q in (2, 3):
                        p_lo(n + 1, q)
                    for q in (4, 5):
                        product(n + 1, q)
                if front:
                    p_lo(n + 1, 4)
                for h in (0, 1):
                    c_lo(n, h)
                if front:
                    p_lo(n + 1, 5)
                if front and prev:
                    v.wait_ge(s_sc[1 - par], 8 * TOPK * TJ * (n - 1 - (1 - par)) + 16 * TOPK * TJ)

            step(0, 0, True, False)
            split_lo_n(0, 0)
            with v.Fori(0, NB // 2 - 1) as m:
                for q in (1, 2):
                    step(2 * m + q, q % 2, True, True)
                    split_lo_n(2 * m + q, q % 2)
            step(NB - 1, 1, False, True)
            shared_act(NB - 1)
            top_first(NB - 1)
            shared_lo(NB - 1)
            top_second(NB - 1, 1)
            for e in range(NE - NLATE, NE):
                split_lo(e + 1, wff, e, (e + 1) % 2)


K_AWD, K_WM, K_TAB, K_MVE, K_MLN, K_MT, K_END = 4, 12, 13, 17, 18, 19, 26
TOPS = 14


def kslot(q):
    return (4, 5, 6, 7, 2, 3)[q]

RING = 4
SKEW = 4
R_PAD, R_PADROW, R_ROUTE = 3, 4, 24
assert NBLK % RING == 0 and RING % NACC == 0 and SKEW == RING


def experts_block(nc, g, sem):
    wff, cst, base, ident = g.wff, g.cst, g.base, g.ident
    X, H, A, Y = g.banks[0:2], g.banks[2:4], g.banks[4:6], g.banks[6:8]

    with ExitStack() as ctx:
        def sb(name, shape, dt=F32):
            return ctx.enter_context(nc.sbuf_tensor(name, shape, dt))

        cnt = sb("cnt", [P, NE])
        nblk = sb("nblk", [P, NE])
        cum = [sb(f"cum{i}", [P, 2 * NE]) for i in (0, 1)]
        done = sb("done", [P, NE])
        dblk = sb("dblk", [P, NE])
        route = sb("route", [P, 2])
        start_blk = sb("start_blk", [P, 1])
        padrow = sb("padrow", [1, NE], I32)
        table = sb("table", [1, 2 * P], I32)
        padtile = sb("padtile", [P, BT, ROW])
        rows = [sb(f"rows{i}", [P, BT, ROW]) for i in range(2 * RING)]
        xT = [sb(f"xT{i}", [P, 2, KT * BROWS], F32R) for i in (0, 1)]
        sil = [sb(f"sil{i}", [P, BT, HID]) for i in (0, 1)]
        act_t = [sb(f"act{i}", [P, BT, HID]) for i in (0, 1)]
        aT = [sb(f"aT{i}", [P, 2, BROWS], F32R) for i in (0, 1)]
        y = [sb(f"y{i}", [P, BT, D]) for i in range(RING)]

        s_route, s_cols, s_table = sem("route_step"), sem("route_cols"), sem("route_table")
        s_pads = sem("pads_out")
        s_in = [sem(f"rows_in{i}") for i in range(2 * RING)]
        s_xT, s_xhi, s_xlo = sem("rows_turned"), sem("rows_hi"), sem("rows_lo")
        s_h, s_sil, s_act = sem("expert_h"), sem("expert_silu"), sem("expert_act")
        s_aT, s_ahi, s_alo = sem("act_turned"), sem("act_hi"), sem("act_lo")
        s_y, s_yout = sem("expert_y"), sem("expert_y_out")
        s_add = [sem(f"added{i}") for i in range(NACC)]
        s_go = sem("expert_wait_held")
        ADDED = 16 * BT

        def held(eng):
            eng.sem_inc(s_go, 1)

        def schedule(eng, step):
            for s in range(2 * RING):
                step(s, s, [i <= s for i in range(SKEW + 1)])
            with eng.Fori(0, NBLK // (2 * RING) - 1) as m:
                for q in range(2 * RING):
                    step(2 * RING * m + (2 * RING + q), q, [True] * (SKEW + 1))
            for s in range(NBLK, NBLK + SKEW):
                step(s, s % (2 * RING), [i > s - NBLK for i in range(SKEW + 1)])

        block = ctx.enter_context(nc.Block())

        @block.sync
        def _(sp):
            sp.wait_ge(s_route, R_PAD)
            sp.dma_start(g.xlist[NE * CAP:NE * CAP + BROWS, :].rearrange("(p t) c -> p t c", t=BT), padtile[:]).then_inc(s_pads, 16)
            sp.wait_ge(s_route, R_PADROW)
            for e in range(NE):
                r = sp.value_load(padrow[0:1, e:e + 1], min_val=e * CAP, max_val=e * CAP + T)
                sp.dma_start(g.xlist[bass.ds(r, BROWS), :].rearrange("(p t) c -> p t c", t=BT), padtile[:]).then_inc(s_pads, 16)
            sp.wait_ge(s_table, 1)
            sp.wait_ge(s_pads, 16 * (NE + 1))

            def load(b, q):
                r = sp.value_load(table[0:1, bass.ds(b + P, 1)], min_val=0, max_val=NE * CAP)
                sp.dma_start(rows[q][:], g.xlist[bass.ds(r, BROWS), :].rearrange("(p t) c -> p t c", t=BT)).then_inc(s_in[q], 16)

            for b in range(2 * RING):
                load(b, b)
            with sp.Fori(0, NBLK // (2 * RING) - 1) as m:
                for q in range(2 * RING):
                    sp.wait_ge(s_add[q % NACC], ADDED * (2 * RING // NACC) * m + ADDED * (q // NACC + 1))
                    held(sp)
                    load(2 * RING * m + (2 * RING + q), q)

        @block.gpsimd
        def _(pool):
            def add(b, q, turn):
                pool.wait_ge(s_yout, b + 1)
                wait_past(pool, s_add[q % NACC], ADDED * turn)
                held(pool)
                for t in range(BT):
                    pool.indirect_dma_start(g.accs[q % NACC], bass.IndirectOffsetOnAxis(
                        ap=rows[q][:, t, COL_TOK:COL_TOK + 1].bitcast(I32), axis=0), y[q % RING][:, t, :], None,
                        compute_op=ALU.add).then_inc(s_add[q % NACC], 16)

            for b in range(2 * RING):
                add(b, b, b // NACC)
            with pool.Fori(0, NBLK // (2 * RING) - 1) as m:
                for q in range(2 * RING):
                    add(2 * RING * m + (2 * RING + q), q, (2 * RING // NACC) * m + (2 * RING + q) // NACC)
            for a in range(NACC):
                pool.wait_ge(s_add[a], ADDED * (NBLK // NACC))

        @block.scalar
        def _(act):
            def step(s, q, on):
                if on[4]:
                    b, i = s - SKEW, (q - SKEW) % RING
                    act.wait_ge(s_y, b + 1)
                    wait_past(act, s_add[i % NACC], (s - q) * (ADDED // NACC) + ADDED * ((q - SKEW - RING) // NACC + 1))
                    held(act)
                    act.activation(y[i][:].rearrange("p t d -> p (t d)"), Y[i % 2][:], ACT.Copy).then_inc(s_yout, 1)
                if on[0]:
                    act.wait_ge(s_xT, s + 1)
                    act.activation(xT[q % 2][:, 0, :], X[q % 2][:], ACT.Copy).then_inc(s_xhi, 1)
                if on[1]:
                    b, i = s - 1, (q - 1) % 2
                    act.wait_ge(s_h, b + 1)
                    act.activation(sil[i][:], H[i][:].rearrange("p (t c) -> p t c", t=BT)[:, :, 0:HID], ACT.Silu).then_inc(s_sil, 1)
                if on[2]:
                    b, i = s - 2, q % 2
                    act.wait_ge(s_aT, b + 1)
                    act.activation(aT[i][:, 0, :], A[i][:, 0:BROWS], ACT.Copy).then_inc(s_ahi, 1)

            schedule(act, step)

        @block.tensor
        def _(pe):
            pe.wait_ge(s_route, R_ROUTE)
            for q in range(2):
                mm = pe.matmul(A[0][0:1, q * P:(q + 1) * P], route[:, q:q + 1], ident, start=True, stop=True)
            mm.then_inc(s_cols, 1)
            pe.wait_ge(s_table, 1)

            def step(s, q, on):
                if on[0]:
                    n = 2 * RING
                    pe.wait_ge(s_in[q], 16 * (s // n) + 16 if isinstance(s, int) else (16 // n) * (s - q) + 16)
                    for k in range(KT):
                        for t in range(BT):
                            mm = pe.transpose(X[q % 2][:, (k * BT + t) * P:(k * BT + t + 1) * P],
                                              rows[q][:, t, k * P:(k + 1) * P], ident)
                    mm.then_inc(s_xT, 1)
                if on[1]:
                    b, i = s - 1, (q - 1) % 2
                    e = pe.value_load(table[0:1, bass.ds(b, 1)], min_val=0, max_val=NE - 1)
                    pe.wait_ge(s_xlo, b + 1)
                    for t in range(BT):
                        for k in range(KT):
                            at = (k * BT + t) * P
                            for x, w in ((0, 0), (0, 1), (1, 0)):
                                mm = pe.matmul(H[i][:, t * 2 * HID:(t + 1) * 2 * HID], xT[i][:, x, at:at + P],
                                               wff[:, bass.ds(e, 1), w, k * 2 * HID:(k + 1) * 2 * HID],
                                               start=(k == 0 and x + w == 0), stop=(k == KT - 1 and x == 1))
                    mm.then_inc(s_h, 1)
                if on[2]:
                    b, i = s - 2, q % 2
                    pe.wait_ge(s_act, b + 1)
                    for t in range(BT):
                        mm = pe.transpose(A[i][:, t * P:(t + 1) * P], act_t[i][:, t, :], ident)
                    mm.then_inc(s_aT, 1)
                if on[3]:
                    b, i = s - 3, (q - 3) % 2
                    e = pe.value_load(table[0:1, bass.ds(b, 1)], min_val=0, max_val=NE - 1)
                    pe.wait_ge(s_alo, b + 1)
                    for t in range(BT):
                        for x, w in ((0, 0), (0, 1), (1, 0)):
                            mm = pe.matmul(Y[i][:, t * D:(t + 1) * D], aT[i][:, x, t * P:(t + 1) * P],
                                           wff[:, bass.ds(e, 1), w, KT * 2 * HID:EW], start=(x + w == 0), stop=(x == 1))
                    mm.then_inc(s_y, 1)

            schedule(pe, step)

        @block.vector
        def _(v):
            count = [0]

            def k(ins):
                count[0] += 1
                ins.then_inc(s_route, 1)

            def seen():
                v.wait_ge(s_route, count[0])

            cap1 = cst[:, C_CAP:C_CAP + NE]
            blk = cst[:, C_TOK:C_TOK + 1]
            k(v.memset(padtile[:], 0.0))
            seen()
            for t in range(BT):
                k(v.tensor_scalar(padtile[:, t, COL_TOK:COL_TOK + 1].bitcast(I32), cst[:, C_TOK:C_TOK + 1], float(BT),
                                  float(T + t), ALU.mult, ALU.add))
            assert count[0] == R_PAD, count
            k(v.tensor_scalar(padrow[:], base[0:1, :], -1.0, None, ALU.add))
            assert count[0] == R_PADROW, count
            k(v.tensor_tensor(cnt[:], base[:], cap1, ALU.subtract))
            for c in cum:
                k(v.memset(c[:, 0:NE], 0.0))
            seen()
            k(v.tensor_scalar(nblk[:], cnt[:], 1.0 / BROWS, (BROWS / 2 - 0.5) / BROWS, ALU.mult, ALU.add))
            seen()
            k(v.tensor_scalar(nblk[:], nblk[:], 2.0 ** 23, None, ALU.add))
            seen()
            k(v.tensor_scalar(nblk[:], nblk[:], 2.0 ** 23, None, ALU.subtract))
            seen()
            k(v.tensor_copy(cum[0][:, NE:], nblk[:]))
            src = 0
            for d in (1, 2, 4, 8):
                seen()
                k(v.tensor_tensor(cum[1 - src][:, NE:], cum[src][:, NE:], cum[src][:, NE - d:2 * NE - d], ALU.add))
                src = 1 - src
            seen()
            k(v.tensor_scalar(done[:], cum[src][:, NE:], blk, None, ALU.is_le))
            seen()
            k(v.tensor_tensor(dblk[:], done[:], nblk[:], ALU.mult))
            k(v.tensor_reduce(route[:, 0:1], done[:], AX.X, ALU.add))
            seen()
            k(v.tensor_reduce(start_blk[:], dblk[:], AX.X, ALU.add))
            seen()
            k(v.tensor_tensor(start_blk[:], blk, start_blk[:], ALU.subtract))
            k(v.tensor_scalar(route[:, 1:2], route[:, 0:1], float(CAP), None, ALU.mult))
            seen()
            k(v.scalar_tensor_tensor(route[:, 1:2], start_blk[:], float(BROWS), route[:, 1:2], ALU.mult, ALU.add))
            k(v.tensor_scalar(route[:, 0:1], route[:, 0:1], float(NE - 1), None, ALU.min))
            seen()
            k(v.tensor_scalar(route[:, 1:2], route[:, 1:2], float(NE * CAP), None, ALU.min))
            assert count[0] == R_ROUTE, count
            v.wait_ge(s_cols, 1)
            v.tensor_copy(table[:], A[0][0:1, 0:2 * P]).then_inc(s_table, 1)
            v.wait_ge(s_table, 1)

            def step(s, q, on):
                if on[0]:
                    i = q % 2
                    v.wait_ge(s_xhi, s + 1)
                    v.tensor_tensor(xT[i][:, 1, :], X[i][:], xT[i][:, 0, :].bitcast(F32), ALU.subtract).then_inc(s_xlo, 1)
                if on[1]:
                    b, i = s - 1, (q - 1) % 2
                    e = v.value_load(table[0:1, bass.ds(b, 1)], min_val=0, max_val=NE - 1)
                    v.wait_ge(s_sil, b + 1)
                    held(v)
                    for t in range(BT):
                        ins = v.scalar_tensor_tensor(
                            act_t[i][:, t, :], sil[i][:, t, :], rows[(q - 1) % (2 * RING)][:, t, bass.ds(e + COL_W, 1)],
                            H[i][:, t * 2 * HID + HID:(t + 1) * 2 * HID], ALU.mult, ALU.mult)
                    ins.then_inc(s_act, 1)
                if on[2]:
                    b, i = s - 2, q % 2
                    v.wait_ge(s_ahi, b + 1)
                    v.tensor_tensor(aT[i][:, 1, :], A[i][:, 0:BROWS], aT[i][:, 0, :].bitcast(F32), ALU.subtract).then_inc(s_alo, 1)

            schedule(v, step)


def sum_block(nc, g, sem):
    with ExitStack() as ctx:
        parts = [[ctx.enter_context(nc.sbuf_tensor(f"part{i}_{a}", [P, TJ, D], F32)) for a in range(NACC)] for i in (0, 1)]
        s_part = [sem("parts_in0"), sem("parts_in1")]
        s_sum, s_out = sem("sums"), [sem("out0"), sem("out1")]
        block = ctx.enter_context(nc.Block())

        @block.sync
        def _(sp):
            for n in range(NB):
                if n >= 2:
                    sp.wait_ge(s_out[n % 2], 16 * (n // 2))
                for a in range(NACC):
                    sp.dma_start(parts[n % 2][a][:], g.acc_b[a][:, n, :, :]).then_inc(s_part[n % 2], 16)
            for i in (0, 1):
                sp.wait_ge(s_out[i], 16 * (NB // 2))

        @block.scalar
        def _(act):
            for n in range(NB):
                act.wait_ge(s_sum, n + 1)
                act.dma_start(g.out_b[:, n, :, :], parts[n % 2][0][:]).then_inc(s_out[n % 2], 16)

        @block.vector
        def _(v):
            for n in range(NB):
                p = parts[n % 2]
                v.wait_ge(s_part[n % 2], 16 * NACC * (n // 2 + 1))
                v.tensor_tensor(p[0][:], p[0][:], p[1][:], ALU.add).then_inc(s_sum, 1)


def kernel(**inputs):
    import numpy as _np
    import concourse.bacc as _bacc
    from concourse import mybir as _mybir
    from concourse.bass_utils import run_bass_kernel_spmd as _run

    a = {k: _np.asarray(v) for k, v in inputs.items()}
    f32 = _np.float32

    def cond(name):
        return a["L0_cond_" + name]

    def ktiles(w):
        return w.reshape(-1, P, w.shape[-1]).transpose(1, 0, 2)

    def columns(v):
        return v.reshape(KT, P).T

    c9, c4, mk = a["itok_BxS_0_999"], a["itok_BxS_0_4"], a["mask_BxS_ik0"]
    sel_ids = _np.zeros((SEL, NB, S), c4.dtype)
    tabs = _np.zeros((SEL, 4, D), f32)
    tab_b = _np.zeros((P, 3, KT, SEL), f32)
    consts = _np.zeros((P, C_END), f32)
    consts[:, C_SEL] = -1
    for r in (0, 32):
        sel_ids[r:r + NC] = c4
        sel_ids[r + NC:r + NC + NM] = mk
        consts[r:r + NC, C_SEL] = _np.arange(NC)
        consts[r + NC:r + NC + NM, C_SEL] = _np.arange(NM)
        tabs[r:r + NC, 0], tabs[r:r + NC, 1] = cond("cp_g"), cond("tm_g")
        tabs[r + NC:r + NC + NM, 2] = cond("ms_g")
        tabs[r, 3] = cond("int_b2")
        for t, name, at in ((0, "cp_b", r), (1, "tm_b", r), (2, "ms_b", r + NC)):
            b = cond(name)
            tab_b[:, t, :, at:at + len(b)] = b.reshape(len(b), KT, P).transpose(2, 1, 0)
    consts[:, C_ID:C_ID + P] = _np.eye(P)
    consts[:, C_UP:C_UP + P] = _np.triu(_np.ones((P, P)), 1)
    consts[:, C_CAP:C_CAP + NE] = _np.arange(NE) * CAP + 1
    consts[:, C_TOK:C_TOK + TJ] = _np.arange(P)[:, None] + P * _np.arange(TJ)

    mlp_in = _np.zeros((P, 3, 32), f32)
    mlp_w1 = _np.zeros((P, 3, D), f32)
    mlp_w2 = _np.zeros((P, 3, KT, D), f32)
    mlp_b2 = _np.zeros((96, D), f32)
    mlp_cols = _np.zeros((P, 3, KT, 3), f32)
    for i, (name, s) in enumerate((("mem", "cond_512"), ("noi", "cond_64"), ("res", "fside_Bx32_0"))):
        mlp_in[:a[s].shape[1], i, :NB] = a[s].T
        mlp_w1[:a[s].shape[1], i] = cond(name + "_W1")
        mlp_w2[:, i] = ktiles(cond(name + "_W2"))
        mlp_b2[32 * i:32 * i + 32] = cond(name + "_b2")
        for q, part in enumerate(("_b1", "_g", "_be")):
            mlp_cols[:, q, :, i] = columns(cond(name + part))

    w1 = _np.concatenate([a["L0_ffn_w1"], a["L0_ffn_sw1"][None]])
    w3 = _np.concatenate([a["L0_ffn_w3"], a["L0_ffn_sw3"][None]])
    w2 = _np.concatenate([a["L0_ffn_w2"], a["L0_ffn_sw2"][None]])
    first = _np.concatenate([w1, w3], 1).transpose(0, 2, 1).reshape(NE + 1, KT, P, 2 * HID).transpose(0, 2, 1, 3)
    experts = _np.concatenate([first.reshape(NE + 1, P, KT * 2 * HID), w2.transpose(0, 2, 1)], 2)

    arrays = {
        "x": a["x"].reshape(T, D),
        "pw_ids": c9.reshape(NB, TJ, P).transpose(2, 0, 1),
        "sel_ids": sel_ids,
        "pw_tab": _np.concatenate([cond("pw_g"), cond("pw_b")], 1),
        "consts": consts,
        "aw": _np.repeat(cond("aw")[None], P, 0),
        "int_w1": ktiles(cond("int_W1")).reshape(P, 6, KT, D),
        "int_w2": ktiles(cond("int_W2")),
        "int_b1": columns(cond("int_b1")),
        "norm_bc": _np.repeat(_np.stack([cond("int_g"), cond("int_be")])[None], P, 0),
        "tabs": tabs,
        "tab_b": tab_b,
        "gate": ktiles(a["L0_ffn_gate_w"].T),
        "mlp_in": mlp_in, "mlp_w1": mlp_w1, "mlp_w2": mlp_w2, "mlp_b2": mlp_b2, "mlp_cols": mlp_cols,
        "experts": experts,
    }
    arrays = {k: _np.ascontiguousarray(v) for k, v in arrays.items()}
    nc = _bacc.Bacc("TRN2", target_bir_lowering=False, num_devices=1)
    args = {k: nc.dram_tensor(k + "_in", v.shape, _mybir.dt.from_np(v.dtype), kind="ExternalInput").ap()
            for k, v in arrays.items()}
    out = nc.dram_tensor("out_dram", (T, D), _mybir.dt.float32, kind="ExternalOutput").ap()
    build(nc, out=out, **args)
    r = _run(nc, [{k + "_in": v for k, v in arrays.items()}], core_ids=[0])
    return r.results[0]["out_dram"].reshape(NB, S, D)
```

```python
from contextlib import ExitStack

import numpy as np

import concourse.bass as bass
from concourse import mybir

F32 = mybir.dt.float32
F32R = mybir.dt.float32r
BF16 = mybir.dt.bfloat16
I32 = mybir.dt.int32
ALU = mybir.AluOpType
ACT = mybir.ActivationFunctionType
AX = mybir.AxisListType

P = 128
NB, S, D = 8, 512, 256
T = NB * S
TJ = S // P
KT = D // P
NE, TOPK, HID = 16, 4, 128
EPS = 1e-5

BT = 2
BROWS = BT * P
CAP = T + BROWS
ROW = 280
COL_W, COL_TOK = D, D + NE
NACC = 2
NBLK = 80
assert P >= NBLK >= T * TOPK // BROWS + NE - 1 and NBLK % NACC == 0
BIG = 3.0e38

SEL = 64
NC, NM = 5, 3
EW = KT * 2 * HID + D
NLATE = 6

C_ID, C_UP, C_CAP, C_SEL, C_TOK, C_END = 0, 128, 256, 272, 273, 277


def wait_past(eng, sem, value):
    if not isinstance(value, int) or value > 0:
        eng.wait_ge(sem, value)


class Shared:
    pass


def build(nc, x, pw_ids, sel_ids, pw_tab, consts, aw, int_w1, int_w2, int_b1, norm_bc,
          tabs, tab_b, gate, mlp_in, mlp_w1, mlp_w2, mlp_b2, mlp_cols, experts, out):
    xlist = nc.dram_tensor("xlist", [NE * CAP + BROWS, ROW], F32, kind="Internal").ap()
    accs = [out] + [nc.dram_tensor(f"acc{a}", [T, D], F32, kind="Internal").ap() for a in range(1, NACC)]

    x_b = x.rearrange("(b j p) d -> p b j d", j=TJ, p=P)
    out_b = out.rearrange("(b j p) d -> p b j d", j=TJ, p=P)
    acc_b = [a.rearrange("(b j p) d -> p b j d", j=TJ, p=P) for a in accs]
    acc_r = [a.rearrange("(b r) d -> b r d", b=NB) for a in accs]
    x_r = x.rearrange("(b r) d -> b r d", b=NB)

    with ExitStack() as whole:
        sems = {}

        def sem(name):
            sems[name] = whole.enter_context(nc.semaphore(name))
            return sems[name]

        def psum(name, shape):
            return whole.enter_context(nc.psum_tensor(name, shape, F32))

        def sb(name, shape, dt=F32):
            return whole.enter_context(nc.sbuf_tensor(name, shape, dt))

        wff_at = -(-nc.sbuf_base // 32) * 32
        wff = sb("wff", [P, NE, 2, EW], F32R)
        cst = sb("cst", [P, C_END])
        base = sb("base", [P, NE])
        table = sb("table", [1, 2 * NBLK], I32)
        ident = cst[:, C_ID:C_ID + P]
        banks = [psum(f"bank{i}", [P, 512]) for i in range(8)]

        late = wff[:, NE - NLATE:NE, :, :].rearrange("p e h c -> p (e h c)")
        xs = late[:, 0:2 * 8 * S].rearrange("p (h k s) -> p h k s", h=2, k=8)

        g = Shared()
        g.x_b, g.x_r, g.out_b, g.acc_b, g.acc_r = x_b, x_r, out_b, acc_b, acc_r
        g.accs, g.xlist, g.pw_ids, g.sel_ids, g.pw_tab, g.consts = accs, xlist, pw_ids, sel_ids, pw_tab, consts
        g.aw, g.int_w1, g.int_w2, g.int_b1, g.norm_bc, g.tabs = aw, int_w1, int_w2, int_b1, norm_bc, tabs
        g.tab_b, g.gate, g.mlp_in, g.mlp_w1, g.mlp_w2, g.mlp_b2 = tab_b, gate, mlp_in, mlp_w1, mlp_w2, mlp_b2
        g.mlp_cols, g.experts, g.wff, g.cst, g.base = mlp_cols, experts, wff, cst, base
        g.ident, g.banks, g.xs, g.wff_at, g.table = ident, banks, xs, wff_at, table
        tokens_block(nc, g, sem)
        experts_block(nc, g, sem)
        sum_block(nc, g, sem)


def tokens_block(nc, g, sem):
    wff, cst, base, ident, xs = g.wff, g.cst, g.base, g.ident, g.xs
    T0, T1, G0, G1, H0, H1, Y0, Y1 = g.banks
    tb, gb, hb, yb = [T0, T1], [G0, G1], [H0, H1], [Y0, Y1]

    with ExitStack() as ctx:
        def sb(name, shape, dt=F32):
            return ctx.enter_context(nc.sbuf_tensor(name, shape, dt))

        wsh = sb("wsh", [P, 2, EW], F32R)
        wint = sb("wint", [P, 2, 8, D], F32R)
        wout = sb("wout", [P, 2, KT, D], F32R)
        wgate = sb("wgate", [P, 2, KT, NE], F32R)
        tab = sb("tab", [SEL, 4, D], F32R)
        btab = sb("btab", [SEL, D], F32R)
        ones = sb("ones", [SEL, P], F32R)
        ones_bf = sb("ones_bf", [P, P], BF16)
        upper = sb("upper", [P, P], BF16)
        nbc = sb("nbc", [P, 2, D])
        vbias = sb("vbias", [P, KT, NB])
        neghalf = sb("neghalf", [P, 8])
        stage = sb("stage", [P, 2, EW])
        xt = sb("xt", [P, TJ, D])
        pid = sb("pid", [P, 2, TJ], I32)
        gt = sb("gt", [P, TJ, 2 * D])
        xh = sb("xh", [P, TJ, D])
        xhT = sb("xhT", [P, KT, S])
        lgT = xhT[0:NE, 0, :]
        hhT = sb("hhT", [P, KT, S])
        prod = sb("prod", [P, 2, S])
        pbuf = [prod[:, 0, :], prod[:, 1, :], xhT[:, 0, :], xhT[:, 1, :], hhT[:, 0, :], hhT[:, 1, :]]
        oh = sb("oh", [SEL, S], F32R)
        ids = sb("ids", [SEL, S], I32)
        st1, st2, st3 = (sb(f"st{i}", [P, TJ, 6]) for i in (1, 2, 3))
        mv1, mv2, mv3 = (sb(f"mv{i}", [P, TJ, 2]) for i in (1, 2, 3))
        ve1, ve2, ve3 = (sb(f"ve{i}", [P, TJ]) for i in (1, 2, 3))
        rs1, rs2, rs3 = (sb(f"rs{i}", [P, TJ]) for i in (1, 2, 3))
        nm1, nm2 = (sb(f"nm{i}", [P, TJ]) for i in (1, 2))
        lg = sb("lg", [P, TJ, 24])
        top8 = sb("top8", [P, TJ, 8])
        rep8 = sb("rep8", [P, TJ, 8])
        repl = sb("repl", [P, TJ, 24])
        mask = sb("mask", [P, TJ, NE], BF16)
        ex = sb("ex", [P, TJ, NE])
        exs = sb("exs", [P, TJ])
        slot = sb("slot", [P, TJ, NE])
        slot8 = sb("slot8", [P, TJ, 8])
        idx = [sb(f"idx{i}", [P, TJ, TOPK], I32) for i in (0, 1)]
        arena_at = -(-nc.sbuf_base // 32) * 32
        sb("arena", [P, 5 * KT * S + 2 * TJ * ROW + TJ * D])
        at = [arena_at]

        def sb_at(name, shape, dt=F32):
            n = -(-int(np.prod(shape[1:])) * 4 // 32) * 32
            t = nc.alloc_sbuf_tensor_at(name, shape, dt, offset=at[0])
            at[0] += n
            return t

        sact = sb_at("sact", [P, KT, S])
        ssp = sb_at("ssp", [P, 2, KT, S], F32R)
        pay = [sb_at(f"pay{i}", [P, TJ, ROW]) for i in (0, 1)]
        csp = sb_at("csp", [P, 2, KT, S], F32R)
        ysh = sb_at("ysh", [P, TJ, D])
        at[0] = arena_at
        raw = sb_at("raw", [P, 6, KT, D])
        wm = sb_at("wm", [P, KT, D])
        rawtab = sb_at("rawtab", [SEL, 4, D])
        tabhi = sb_at("tabhi", [SEL, 4, D], F32R)
        m_b2 = sb_at("m_b2", [96, D])
        rawtb = sb_at("rawtb", [P, 3, KT, SEL])
        rawo = sb_at("rawo", [P, KT, D])
        at[0] = g.wff_at + 8 * 2 * EW * 4
        m_w1 = sb_at("m_w1", [P, 3, D])
        m_w2 = sb_at("m_w2", [P, 3, KT, D])
        rawg = sb_at("rawg", [P, KT, NE])
        small_at = sb_at("small_at", [P, 3 * 32 + 3 * 2 * 32 + 18 + 6 + 2 + 48 + 40])
        m_in = small_at[:, 0:96].rearrange("p (i c) -> p i c", i=3)
        m_h = small_at[:, 96:288].rearrange("p (i k c) -> p i k c", i=3, k=KT)
        m_cols = small_at[:, 288:306].rearrange("p (v k i) -> p v k i", v=3, k=KT)
        w6 = small_at[:, 306:312]
        b1 = small_at[:, 312:314]
        m_t = small_at[:, 314:362].rearrange("p (i k c) -> p i k c", i=3, k=KT)
        awt = small_at[:, 362:368]
        tmp = small_at[:, 368:402]

        padtile = xh[:].rearrange("p j d -> p (j d)")[:, 0:BT * ROW].rearrange("p (t c) -> p t c", t=BT)
        flat = xt[:].rearrange("p j d -> p (j d)")
        cnt, nblk = flat[:, 0:NE], flat[:, NE:2 * NE]
        cum = [flat[:, 2 * NE:4 * NE], flat[:, 4 * NE:6 * NE]]
        done, dblk = flat[:, 6 * NE:7 * NE], flat[:, 7 * NE:8 * NE]
        route = flat[:, 8 * NE:8 * NE + 2]
        start_blk = flat[:, 9 * NE:9 * NE + 1]
        padrow = flat[0:1, 10 * NE:11 * NE].bitcast(I32)
        table = g.table

        s_x, s_ids, s_gt = sem("x_in"), sem("ids_in"), sem("gathered")
        s_pid = [sem("pid_in0"), sem("pid_in1")]
        s_c1, s_c2, s_c3, s_c4, s_c5 = (sem(f"setup_in{i}") for i in range(5))
        s_stage = [sem("stage_in0"), sem("stage_in1")]
        s_split_hi, s_split_lo = sem("expert_hi"), sem("expert_lo")
        s_nm1, s_nm2 = sem("shift1"), sem("shift2")
        s_bn1, s_mv1, s_ve1, s_rs1 = sem("bn1"), sem("mv1"), sem("ve1"), sem("rstd1")
        s_bn2, s_mv2, s_ve2, s_rs2 = sem("bn2"), sem("mv2"), sem("ve2"), sem("rstd2")
        s_bn3, s_mv3, s_ve3, s_rs3 = sem("bn3"), sem("mv3"), sem("ve3"), sem("rstd3")
        s_xh, s_u1, s_u2, s_hh = sem("xhat"), sem("gained"), sem("shifted"), sem("hhat")
        s_xT, s_xhT, s_hhT, s_g = sem("x_turned"), sem("xhat_turned"), sem("hhat_turned"), sem("gains")
        s_xhi, s_xlo, s_xhc, s_hhc = sem("x_hi"), sem("x_lo"), sem("xhat_copied"), sem("hhat_copied")
        s_oh, s_prod, s_phi, s_plo = sem("onehot"), sem("product"), sem("product_hi"), sem("product_lo")
        s_hid, s_silu, s_shi, s_slo = sem("hidden"), sem("hidden_silu"), sem("silu_hi"), sem("silu_lo")
        s_y2, s_c, s_cn, s_cT = sem("second"), sem("centred"), sem("c_rows"), sem("c_turned")
        s_chi, s_clo, s_gate = sem("c_hi"), sem("c_lo"), sem("logits")
        s_lgT, s_lgc = sem("logits_in_rows"), sem("logits_copied")
        s_top, s_exp, s_rank, s_idx, s_pay = sem("top_step"), sem("exp_done"), sem("ranks"), sem("slots"), sem("row_ready")
        s_sc = [sem("rows_out0"), sem("rows_out1")]
        s_ohu = sem("onehot_used")
        s_h, s_ss, s_sa, s_ahi, s_alo = sem("shared_h"), sem("shared_silu"), sem("shared_act"), sem("shared_hi"), sem("shared_lo")
        s_ys, s_ysh, s_acc, s_st = sem("shared_y"), sem("shared_out"), sem("sums_begun"), sem("shared_stored")
        s_k, s_pk, s_ak, s_ek = sem("dve_setup"), sem("pool_setup"), sem("act_setup"), sem("pe_setup")
        s_go = sem("wait_held")
        s_route, s_cols, s_table, s_pads = sem("route_step"), sem("route_cols"), sem("route_table"), sem("pads_out")
        s_late = sem("late_in")

        def held(eng):
            eng.sem_inc(s_go, 1)

        def held_wait(eng, sem, value):
            if not isinstance(value, int) or value > 0:
                eng.wait_ge(sem, value)
                held(eng)

        LATE = NE - NLATE
        front_mem = [gt[:].rearrange("p j c -> p (j c)"), hhT[:].rearrange("p k s -> p (k s)"),
                     prod[:].rearrange("p q s -> p (q s)")]
        late_stage = [front_mem[0][:, 0:EW], front_mem[0][:, EW:2 * EW], front_mem[1][:, 0:EW], front_mem[2][:, 0:EW]]
        assert len(late_stage) == NLATE - 2
        SETUP_EXPERTS = 1

        def pads(eng, of):
            eng.wait_ge(s_route, R_PADROW)
            for e in of:
                r = eng.value_load(padrow[0:1, e:e + 1], min_val=e * CAP, max_val=e * CAP + T)
                eng.dma_start(g.xlist[bass.ds(r, BROWS), :].rearrange("(p t) c -> p t c", t=BT), padtile).then_inc(s_pads, 16)

        def batches(eng, step):
            for n in (0, 1):
                step(n, n, n > 0, True, True)
            with eng.Fori(0, NB // 2 - 2) as m:
                for q in (2, 3):
                    step(2 * m + q, q % 2, True, True, True)
            for n in (NB - 2, NB - 1):
                step(n, n % 2, True, n < NB - 1, False)

        block = ctx.enter_context(nc.Block())

        @block.sync
        def _(sp):
            def load_front(n):
                held_wait(sp, s_xh, TJ * n)
                held_wait(sp, s_xT, KT * n)
                sp.dma_start(xt[:], g.x_b[:, bass.ds(n, 1), :, :].rearrange("p o j d -> p (o j) d")).then_inc(s_x, 16)
                held_wait(sp, s_oh, n)
                sp.dma_start(ids[:], g.sel_ids[:, bass.ds(n, 1), :].rearrange("p o s -> p (o s)")).then_inc(s_ids, 16)

            def load_pid(n, par):
                held_wait(sp, s_gt, 16 * TJ * (n - 1))
                sp.dma_start(pid[:, par, :], g.pw_ids[:, bass.ds(n, 1), :].rearrange("p o j -> p (o j)")).then_inc(s_pid[par], 16)

            def load_chunk(c, e, s):
                held_wait(sp, s_split_hi, c - 1)
                held_wait(sp, s_split_lo, c - 1)
                sp.dma_start(stage[:, s, :], g.experts[bass.ds(e, 1), :, :].rearrange("o p c -> p (o c)")).then_inc(s_stage[s], 16)

            def start_sums(n):
                sp.dma_start(g.acc_r[1][bass.ds(n, 1), :, :], g.x_r[bass.ds(n, 1), :, :]).then_inc(s_acc, 16)

            def store_shared(n):
                held_wait(sp, s_ysh, KT * (n + 1))
                sp.dma_start(g.acc_b[0][:, bass.ds(n, 1), :, :].rearrange("p o j d -> p (o j) d"), ysh[:]).then_inc(s_st, 16)

            load_pid(0, 0)
            load_front(0)
            sp.dma_start(cst[:], g.consts).then_inc(s_c1, 16)
            sp.dma_start(awt, g.aw).then_inc(s_c1, 16)
            sp.dma_start(rawtab[:], g.tabs).then_inc(s_c1, 16)
            sp.dma_start(m_in, g.mlp_in).then_inc(s_c3, 16)
            sp.dma_start(m_cols, g.mlp_cols).then_inc(s_c3, 16)
            sp.dma_start(m_w1[:], g.mlp_w1).then_inc(s_c3, 16)
            sp.dma_start(m_w2[:], g.mlp_w2).then_inc(s_c3, 16)
            sp.dma_start(m_b2[:], g.mlp_b2).then_inc(s_c3, 16)
            sp.dma_start(raw[:], g.int_w1).then_inc(s_c2, 16)
            sp.dma_start(rawtb[:], g.tab_b).then_inc(s_c4, 16)
            sp.dma_start(b1, g.int_b1).then_inc(s_c4, 16)
            sp.dma_start(nbc[:], g.norm_bc).then_inc(s_c5, 16)
            sp.dma_start(rawg[:], g.gate).then_inc(s_c5, 16)
            sp.dma_start(rawo[:], g.int_w2).then_inc(s_c5, 16)
            load_pid(1, 1)
            load_front(1)
            for c in range(SETUP_EXPERTS + 1):
                load_chunk(c, c - 1 if c else NE, c % 2)

            def step(n, par, prev, front, ahead):
                start_sums(n)
                c = n + SETUP_EXPERTS + 1
                if front:
                    load_chunk(c, c - 1, (par + SETUP_EXPERTS + 1) % 2)
                if ahead:
                    load_front(n + 2)
                    load_pid(n + 2, par)
                if prev:
                    store_shared(n - 1)

            batches(sp, step)
            for e in range(SETUP_EXPERTS + NB - 1, LATE):
                load_chunk(e + 1, e, (e + 1) % 2)
            sp.wait_ge(s_hhT, KT * NB)
            sp.wait_ge(s_plo, 6 * NB)
            for e, dst in enumerate(late_stage, LATE + 2):
                sp.dma_start(dst, g.experts[e, :, :]).then_inc(s_late, 16)
            for e in (LATE, LATE + 1):
                load_chunk(e + 1, e, (e + 1) % 2)
            pads(sp, range(0, NE // 2))
            sp.wait_ge(s_route, R_PAD)
            sp.dma_start(g.xlist[NE * CAP:NE * CAP + BROWS, :].rearrange("(p t) c -> p t c", t=BT), padtile).then_inc(s_pads, 16)
            store_shared(NB - 1)
            sp.wait_ge(s_acc, 16 * NB)
            sp.wait_ge(s_st, 16 * (NB + 1))
            sp.wait_ge(s_pads, 16 * (NE + 1))

        @block.gpsimd
        def _(pool):
            pool.memset(neghalf[:], -0.5).then_inc(s_pk, 1)
            pool.memset(ones_bf[:], 1.0).then_inc(s_pk, 1)

            def rstd(rs, ve, s_ve, s_rs, n):
                pool.wait_ge(s_ve, n + 1)
                pool.tensor_tensor(rs[:], ve[:], neghalf[:, 0:TJ], ALU.pow).then_inc(s_rs, 1)

            def gathers(n, par):
                pool.wait_ge(s_pid[par], 8 * (n - par) + 16)
                wait_past(pool, s_hhT, KT * n)
                held(pool)
                for j in range(TJ):
                    pool.indirect_dma_start(gt[:, j, :], None, g.pw_tab,
                                            bass.IndirectOffsetOnAxis(ap=pid[:, par, j:j + 1], axis=0)).then_inc(s_gt, 16)

            def shift(n):
                pool.wait_ge(s_u1, n + 1)
                pool.tensor_tensor(gt[:, :, 0:D], gt[:, :, 0:D], gt[:, :, D:2 * D], ALU.add).then_inc(s_u2, 1)

            def scatter(n, par, first, last):
                if first == 0:
                    pool.wait_ge(s_pay, n + 1)
                    pool.wait_ge(s_idx, n + 1)
                    held(pool)
                for q in range(first, last):
                    j, k = q // TOPK, q % TOPK
                    pool.indirect_dma_start(g.xlist, bass.IndirectOffsetOnAxis(ap=idx[par][:, j, k:k + 1], axis=0),
                                            pay[par][:, j, :], None).then_inc(s_sc[par], 16)

            gathers(0, 0)
            pool.wait_ge(s_pk, 2)
            rstd(rs1, ve1, s_ve1, s_rs1, 0)
            shift(0)
            rstd(rs2, ve2, s_ve2, s_rs2, 0)
            pool.wait_ge(s_k, K_MVE)
            pool.tensor_tensor(tmp[0:96, 1:2], tmp[0:96, 0:1], neghalf[0:96, 0:1], ALU.pow).then_inc(s_pk, 1)
            rstd(rs1, ve1, s_ve1, s_rs1, 1)
            gathers(1, 1)

            def step(n, par, prev, front, ahead):
                if front:
                    shift(n + 1)
                    rstd(rs2, ve2, s_ve2, s_rs2, n + 1)
                if prev:
                    scatter(n - 1, 1 - par, 0, 5)
                if ahead:
                    rstd(rs1, ve1, s_ve1, s_rs1, n + 2)
                if prev:
                    scatter(n - 1, 1 - par, 5, 11)
                rstd(rs3, ve3, s_ve3, s_rs3, n)
                if ahead:
                    gathers(n + 2, par)
                if prev:
                    scatter(n - 1, 1 - par, 11, 16)

            batches(pool, step)
            scatter(NB - 1, 1, 0, 16)
            for p in (0, 1):
                pool.wait_ge(s_sc[p], 16 * TOPK * TJ * (NB // 2))

        @block.scalar
        def _(act):
            def x_hi(n, h):
                act.wait_ge(s_xT, KT * n + h + 1)
                wait_past(act, s_hid, KT * n)
                act.activation(xs[:, 0, h, :], tb[h][:], ACT.Copy).then_inc(s_xhi, 1)

            def x_norm(n):
                act.wait_ge(s_nm1, n + 1)
                wait_past(act, s_xhT, KT * n)
                held(act)
                for j in range(TJ):
                    act.activation(xh[:, j, :], xt[:, j, :], ACT.Identity, bias=nm1[:, j:j + 1],
                                   scale=rs1[:, j:j + 1]).then_inc(s_xh, 1)

            def h_norm(n):
                act.wait_ge(s_nm2, n + 1)
                held(act)
                for j in range(TJ):
                    act.activation(gt[:, j, 0:D], gt[:, j, 0:D], ACT.Identity, bias=nm2[:, j:j + 1],
                                   scale=rs2[:, j:j + 1]).then_inc(s_hh, 1)

            def xh_copy(n, h):
                act.wait_ge(s_xhT, KT * n + h + 1)
                wait_past(act, s_plo, 6 * n)
                wait_past(act, s_gate, n - 1)
                act.activation(xhT[:, h, :], tb[h][:], ACT.Copy).then_inc(s_xhc, 1)

            def hh_copy(n, h):
                act.wait_ge(s_hhT, KT * n + h + 1)
                act.activation(hhT[:, h, :], tb[h][:], ACT.Copy).then_inc(s_hhc, 1)

            def p_hi(n, q):
                act.wait_ge(s_prod, 6 * n + q + 1)
                act.activation(xs[:, 0, kslot(q), :], pbuf[q], ACT.Copy).then_inc(s_phi, 1)

            def silu(n, h):
                act.wait_ge(s_hid, KT * n + h + 1)
                held(act)
                act.activation(sact[:, h, :], hb[h][:], ACT.Silu, bias=vbias[:, h, bass.ds(n, 1)]).then_inc(s_silu, 1)
                act.wait_ge(s_silu, KT * n + h + 1)
                act.activation(ssp[:, 0, h, :], sact[:, h, :], ACT.Copy).then_inc(s_shi, 1)

            def c_hi(n, h):
                act.wait_ge(s_cT, KT * n + h + 1)
                wait_past(act, s_h, 2 * n)
                act.activation(csp[:, 0, h, :], tb[h][:], ACT.Copy).then_inc(s_chi, 1)

            def logits_copy(n):
                act.wait_ge(s_lgT, n + 1)
                act.activation(lgT, Y0[0:NE, :], ACT.Copy).then_inc(s_lgc, 1)

            def exps(n):
                act.wait_ge(s_top, TOPS * n + 5)
                act.activation(ex[:], ex[:], ACT.Exp).then_inc(s_exp, 1)

            def shared_silu(n, after):
                act.wait_ge(s_h, 2 * n + 1)
                act.wait_ge(s_slo, KT * after + KT)
                act.activation(sact[:, 0, :], hb[0][:], ACT.Silu).then_inc(s_ss, 1)

            def shared_hi(n, after):
                act.wait_ge(s_sa, n + 1)
                act.wait_ge(s_y2, TJ * after + TJ)
                act.activation(ssp[:, 0, 0, :], sact[:, 1, :], ACT.Copy).then_inc(s_ahi, 1)

            def shared_out(n):
                for b in (0, 1):
                    act.wait_ge(s_ys, 2 * n + b + 1)
                    if b == 0:
                        act.wait_ge(s_st, 16 * (n + 1))
                    act.activation(ysh[:, 2 * b:2 * b + 2, :].rearrange("p j d -> p (j d)"), hb[b][:], ACT.Copy).then_inc(s_ysh, 1)

            def split_hi(c, dst, s):
                act.wait_ge(s_stage[s], 16 * (c // 2 + 1))
                act.activation(dst, stage[:, s, :], ACT.Copy).then_inc(s_split_hi, 1)

            def split_hi_n(n, par):
                s = (par + SETUP_EXPERTS + 1) % 2
                act.wait_ge(s_stage[s], 8 * (n + SETUP_EXPERTS + 1 - s) + 16)
                held(act)
                act.activation(wff[:, bass.ds(n + SETUP_EXPERTS, 1), 0, :].rearrange("p o c -> p (o c)"),
                               stage[:, s, :], ACT.Copy).then_inc(s_split_hi, 1)

            act.wait_ge(s_k, K_AWD)
            act.activation(w6, w6, ACT.Exp).then_inc(s_ak, 1)
            act.wait_ge(s_c1, 48)
            act.activation(tabhi[:], rawtab[:], ACT.Copy).then_inc(s_ak, 1)
            x_norm(0)
            for h in (0, 1):
                xh_copy(0, h)
            for h in (0, 1):
                x_hi(0, h)
            for q in range(2):
                p_hi(0, q)
            act.wait_ge(s_ek, 1)
            act.wait_ge(s_c3, 80)
            for i in range(3):
                for h in range(KT):
                    ins = act.activation(m_h[:, i, h, :], H0[:, (i * KT + h) * 32:(i * KT + h) * 32 + 32], ACT.Silu,
                                         bias=m_cols[:, 0, h, i:i + 1])
            ins.then_inc(s_ak, 1)
            act.sem_inc(s_st, 16)
            act.wait_ge(s_k, K_WM)
            for k, src in enumerate((wm[:], raw[:, 0, :, :], raw[:, 1, :, :], raw[:, 5, :, :])):
                ins = act.activation(wint[:, 0, KT * k:KT * k + KT, :], src, ACT.Copy)
            ins.then_inc(s_ak, 1)
            h_norm(0)
            for q in range(2, 4):
                p_hi(0, q)
            for h in (0, 1):
                hh_copy(0, h)
            x_norm(1)
            act.wait_ge(s_ek, 3)
            act.wait_ge(s_k, K_TAB)
            act.activation(tabhi[:, 0, :], Y0[0:SEL, 0:D], ACT.Copy).then_inc(s_ak, 1)
            for q in range(4, 6):
                p_hi(0, q)
            act.wait_ge(s_c5, 48)
            act.activation(wgate[:, 0, :, :], rawg[:], ACT.Copy)
            act.activation(wout[:, 0, :, :], rawo[:], ACT.Copy).then_inc(s_ak, 1)
            for c in range(SETUP_EXPERTS + 1):
                split_hi(c, wsh[:, 0, :] if c == 0 else wff[:, c - 1, 0, :], c % 2)
            act.wait_ge(s_k, K_END)

            def step(n, par, prev, front, ahead):
                if prev:
                    logits_copy(n - 1)
                if front:
                    for h in (0, 1):
                        xh_copy(n + 1, h)
                if prev:
                    exps(n - 1)
                silu(n, 0)
                if front:
                    h_norm(n + 1)
                silu(n, 1)
                if front:
                    for h in (0, 1):
                        x_hi(n + 1, h)
                    for q in (0, 1):
                        p_hi(n + 1, q)
                    split_hi_n(n, par)
                    for q in (2, 3):
                        p_hi(n + 1, q)
                    for h in (0, 1):
                        hh_copy(n + 1, h)
                if prev:
                    shared_silu(n - 1, n)
                for h in (0, 1):
                    c_hi(n, h)
                if prev:
                    shared_hi(n - 1, n)
                if front:
                    for q in (4, 5):
                        p_hi(n + 1, q)
                if ahead:
                    x_norm(n + 2)
                if prev:
                    shared_out(n - 1)

            batches(act, step)
            logits_copy(NB - 1)
            exps(NB - 1)
            for e in range(SETUP_EXPERTS + NB - 1, LATE):
                split_hi(e + 1, wff[:, e, 0, :], (e + 1) % 2)
            shared_silu(NB - 1, NB - 1)
            shared_hi(NB - 1, NB - 1)
            shared_out(NB - 1)
            for e in (LATE, LATE + 1):
                split_hi(e + 1, wff[:, e, 0, :], (e + 1) % 2)
            act.wait_ge(s_late, 16 * len(late_stage))
            for e, src in enumerate(late_stage, LATE + 2):
                act.activation(wff[:, e, 0, :], src, ACT.Copy).then_inc(s_split_hi, 1)
            pads(act, range(NE // 2, NE))

        @block.tensor
        def _(pe):
            def three(out, l, r, start=True, stop=True):
                pe.matmul(out, l(0), r(0), start=start, stop=False)
                pe.matmul(out, l(0), r(1), start=False, stop=False)
                return pe.matmul(out, l(1), r(0), start=False, stop=stop)

            def turn(h, src):
                for j in range(TJ):
                    mm = pe.transpose(tb[h][:, j * P:(j + 1) * P], src(j, h), ident)
                return mm

            def turn_x(n):
                pe.wait_ge(s_x, 16 * (n + 1))
                for h in (0, 1):
                    pe.wait_ge(s_xhc, KT * n + h + 1)
                    turn(h, lambda j, h: xt[:, j, h * P:(h + 1) * P]).then_inc(s_xT, 1)

            def turn_xh(n):
                pe.wait_ge(s_xh, TJ * (n + 1))
                for h in (0, 1):
                    wait_past(pe, s_hhc, KT * (n - 1) + h + 1)
                    turn(h, lambda j, h: xh[:, j, h * P:(h + 1) * P]).then_inc(s_xhT, 1)

            def turn_c(n, par, front):
                for h in (0, 1):
                    pe.wait_ge(s_hhc, KT * (n + 1 if front else n) + h + 1)
                    for j in range(TJ):
                        if h == 0:
                            pe.wait_ge(s_cn, TJ * n + j + 1)
                        mm = pe.transpose(tb[h][:, j * P:(j + 1) * P], pay[par][:, j, h * P:(h + 1) * P], ident)
                    mm.then_inc(s_cT, 1)

            def turn_hh(n):
                pe.wait_ge(s_hh, TJ * (n + 1))
                for h in (0, 1):
                    pe.wait_ge(s_xhi, KT * n + h + 1)
                    pe.wait_ge(s_xlo, KT * n + h + 1)
                    turn(h, lambda j, h: gt[:, j, h * P:(h + 1) * P]).then_inc(s_hhT, 1)

            def gains(n, q):
                table, h = (1, 1, 2, 2, 0, 0)[q], q % 2
                pe.wait_ge(s_oh, n + 1)
                wait_past(pe, s_prod, 6 * n + q - 1)
                pe.matmul(gb[q % 2][:], tab[:, table, h * P:(h + 1) * P], oh[:], start=True, stop=True).then_inc(s_g, 1)

            def hidden(n, h, ks=(0, 1, 4, 5, 6, 7, 2, 3)):
                pe.wait_ge(s_xlo, KT * (n + 1))
                pe.wait_ge(s_plo, 6 * n + 4)
                if h == 0 and ks[0] == 0:
                    wait_past(pe, s_ysh, 2 * (n - 1))
                    for i in (0, 1):
                        mm = pe.matmul(hb[i][:], btab[:, i * P:(i + 1) * P], oh[:], start=True, stop=False)
                    mm.then_inc(s_ohu, 1)
                for k in ks:
                    if h == 0 and k == 2:
                        pe.wait_ge(s_plo, 6 * (n + 1))
                    mm = three(hb[h][:], lambda w: wint[:, w, k, h * P:(h + 1) * P], lambda w: xs[:, w, k, :],
                               start=False, stop=(k == 3))
                if ks[-1] == 3:
                    mm.then_inc(s_hid, 1)

            def second(n):
                wait_past(pe, s_idx, n)
                pe.wait_ge(s_shi, KT * (n + 1))
                pe.wait_ge(s_slo, KT * (n + 1))
                for j in range(TJ):
                    o = yb[j // 2][:, (j % 2) * D:(j % 2 + 1) * D]
                    for k in range(KT):
                        three(o, lambda w: ssp[:, w, k, j * P:(j + 1) * P], lambda w: wout[:, w, k, :],
                              start=(k == 0), stop=False)
                    pe.matmul(o, ones[:], tab[:, 3, :], start=False, stop=True).then_inc(s_y2, 1)

            def logits(n):
                pe.wait_ge(s_chi, KT * (n + 1))
                pe.wait_ge(s_clo, KT * (n + 1))
                for k in range(KT):
                    mm = three(Y0[0:NE, :], lambda w: wgate[:, w, k, :], lambda w: csp[:, w, k, :],
                               start=(k == 0), stop=(k == KT - 1))
                mm.then_inc(s_lgT, 1)

            def turn_logits(n):
                pe.wait_ge(s_lgc, n + 1)
                held(pe)
                for j in range(TJ):
                    mm = pe.transpose(Y1[:, P + j * NE:P + (j + 1) * NE], lgT[:, j * P:(j + 1) * P], ident[0:NE, 0:NE])
                mm.then_inc(s_gate, 1)

            def shared_first(n, after):
                pe.wait_ge(s_silu, KT * (after + 1))
                for i in (0, 1):
                    for k in range(KT):
                        mm = three(hb[i][:], lambda w: wsh[:, w, k * 2 * HID + i * HID:k * 2 * HID + (i + 1) * HID],
                                   lambda w: csp[:, w, k, :], start=(k == 0), stop=(k == KT - 1))
                    mm.then_inc(s_h, 1)

            def ranks(n):
                pe.wait_ge(s_top, TOPS * n + 6)
                pe.matmul(Y1[:, 0:TJ * NE], upper[:], mask[:].rearrange("p j e -> p (j e)"), start=True, stop=False,
                          skip_group_check=True)
                for d in range(1, TJ):
                    pe.matmul(Y1[:, d * NE:TJ * NE], ones_bf[:], mask[:, 0:TJ - d, :].rearrange("p j e -> p (j e)"),
                              start=False, stop=(d == TJ - 1), skip_group_check=True)
                for j in range(TJ):
                    mm = pe.matmul(Y1[:, TJ * NE:(TJ + 1) * NE], ones_bf[:], mask[:, j, :], start=(j == 0),
                                   stop=(j == TJ - 1), skip_group_check=True)
                mm.then_inc(s_rank, 1)

            def shared_second(n):
                pe.wait_ge(s_ahi, n + 1)
                pe.wait_ge(s_alo, n + 1)
                for b in (0, 1):
                    for j in (2 * b, 2 * b + 1):
                        mm = three(hb[b][:, (j % 2) * D:(j % 2 + 1) * D], lambda w: ssp[:, w, 0, j * P:(j + 1) * P],
                                   lambda w: wsh[:, w, KT * 2 * HID:EW])
                    mm.then_inc(s_ys, 1)

            pe.wait_ge(s_c1, 48)
            turn_xh(0)
            turn_x(0)
            pe.wait_ge(s_k, K_TAB)
            for q in range(2):
                gains(0, q)
            pe.wait_ge(s_c3, 80)
            for i in range(3):
                for h in range(KT):
                    mm = pe.matmul(H0[:, (i * KT + h) * 32:(i * KT + h) * 32 + 32], m_w1[:, i, h * P:(h + 1) * P],
                                   m_in[:, i, :], start=True, stop=True)
            mm.then_inc(s_ek, 1)
            pe.wait_ge(s_ak, 3)
            for i in range(3):
                for k in range(KT):
                    mm = pe.matmul(H1[32 * i:32 * i + 32, 0:D], m_h[:, i, k, :], m_w2[:, i, k, :],
                                   start=(k == 0), stop=(k == KT - 1))
            mm.then_inc(s_ek, 1)
            pe.wait_ge(s_c4, 32)
            pe.wait_ge(s_k, K_WM)
            for q, (t, w) in enumerate(((0, 0), (1, 1), (2, 5))):
                for k in range(KT):
                    mm = pe.matmul(Y0[0:SEL, 0:D], rawtb[:, t, k, :], raw[:, w, k, :], start=(q + k == 0),
                                   stop=(q == 2 and k == KT - 1))
            mm.then_inc(s_ek, 1)
            for q in range(2, 4):
                gains(0, q)
            pe.wait_ge(s_k, K_MLN)
            for k in range(KT):
                mm = pe.transpose(Y1[:, k * 96:(k + 1) * 96], m_b2[0:96, k * P:(k + 1) * P], ident[0:96, 0:96])
            mm.then_inc(s_ek, 1)
            turn_hh(0)
            for q in range(4, 6):
                gains(0, q)
            pe.wait_ge(s_k, K_MT)
            for h in range(KT):
                for i in range(3):
                    for k in range(KT):
                        mm = pe.matmul(H0[:, h * NB:(h + 1) * NB], raw[:, 2 + i, k, h * P:(h + 1) * P], m_t[:, i, k, :],
                                       start=(i + k == 0), stop=(i == 2 and k == KT - 1))
            mm.then_inc(s_ek, 1)
            pe.wait_ge(s_k, K_VB)

            def step(n, par, prev, front, ahead):
                if prev:
                    logits(n - 1)
                if front:
                    turn_xh(n + 1)
                if prev:
                    turn_logits(n - 1)
                hidden(n, 0)
                if prev:
                    ranks(n - 1)
                if front:
                    turn_x(n + 1)
                    for q in (0, 1):
                        gains(n + 1, q)
                hidden(n, 1, (0, 1, 4, 5))
                if front:
                    for q in (2, 3):
                        gains(n + 1, q)
                hidden(n, 1, (6, 7, 2, 3))
                if not prev:
                    pe.wait_ge(s_k, K_END)
                    pe.wait_ge(s_ak, 6)
                    pe.wait_ge(s_split_hi, 1)
                    pe.wait_ge(s_split_lo, 1)
                second(n)
                if front:
                    turn_hh(n + 1)
                if prev:
                    shared_first(n - 1, n)
                if front:
                    for q in (4, 5):
                        gains(n + 1, q)
                turn_c(n, par, front)
                if prev:
                    shared_second(n - 1)

            batches(pe, step)
            logits(NB - 1)
            turn_logits(NB - 1)
            shared_first(NB - 1, NB - 1)
            ranks(NB - 1)
            shared_second(NB - 1)
            pe.wait_ge(s_route, R_ROUTE)
            for q in range(2):
                mm = pe.matmul(T0[0:1, q * P:(q + 1) * P], route[:, q:q + 1], ident, start=True, stop=True)
            mm.then_inc(s_cols, 1)

        @block.vector
        def _(v):
            def stats(n, src, st, mv, ve, s_bn, s_mv, s_ve, s_src=None):
                for j in range(TJ):
                    if s_src is not None and j % 2 == 0:
                        v.wait_ge(s_src, TJ * n + j + 2)
                    v.bn_stats(st[:, j, :], src(j)).then_inc(s_bn, 1)
                for j in range(TJ):
                    if j == 0:
                        v.wait_ge(s_bn, TJ * (n + 1))
                        held(v)
                    v.bn_aggr(mv[:, j, :], st[:, j, :]).then_inc(s_mv, 1)
                v.wait_ge(s_mv, TJ * (n + 1))
                v.tensor_scalar(ve[:], mv[:, :, 1:2].rearrange("p j o -> p (j o)"), EPS, None, ALU.add).then_inc(s_ve, 1)

            def x_stats(n):
                v.wait_ge(s_x, 16 * (n + 1))
                stats(n, lambda j: xt[:, j, :], st1, mv1, ve1, s_bn1, s_mv1, s_ve1)

            def x_shift(n):
                v.wait_ge(s_rs1, n + 1)
                v.scalar_tensor_tensor(nm1[:], mv1[:, :, 0:1].rearrange("p j o -> p (j o)"), -1.0, rs1[:], ALU.mult,
                                       ALU.mult).then_inc(s_nm1, 1)

            def gain(n):
                v.wait_ge(s_gt, 16 * TJ * (n + 1))
                v.wait_ge(s_xh, TJ * (n + 1))
                v.tensor_tensor(gt[:, :, 0:D], gt[:, :, 0:D], xh[:], ALU.mult).then_inc(s_u1, 1)

            def h_stats(n):
                v.wait_ge(s_u2, n + 1)
                stats(n, lambda j: gt[:, j, 0:D], st2, mv2, ve2, s_bn2, s_mv2, s_ve2)

            def h_shift(n):
                v.wait_ge(s_rs2, n + 1)
                v.scalar_tensor_tensor(nm2[:], mv2[:, :, 0:1].rearrange("p j o -> p (j o)"), -1.0, rs2[:], ALU.mult,
                                       ALU.mult).then_inc(s_nm2, 1)

            def onehot(n):
                v.wait_ge(s_ids, 16 * (n + 1))
                wait_past(v, s_ohu, n)
                v.tensor_scalar(oh[:], ids[:], cst[0:SEL, C_SEL:C_SEL + 1], None, ALU.is_equal).then_inc(s_oh, 1)

            def x_lo(n, h):
                v.wait_ge(s_xhi, KT * n + h + 1)
                v.tensor_tensor(xs[:, 1, h, :], tb[h][:], xs[:, 0, h, :].bitcast(F32), ALU.subtract).then_inc(s_xlo, 1)

            def product(n, q):
                h = q % 2
                v.wait_ge(s_g, 6 * n + q + 1)
                v.wait_ge(s_xhc if q < 4 else s_hhc, KT * n + h + 1)
                wait_past(v, s_plo, 6 * (n - 1) + q + 1)
                v.tensor_tensor(pbuf[q], gb[q % 2][:], (xhT if q < 4 else hhT)[:, h, :], ALU.mult).then_inc(s_prod, 1)

            def p_lo(n, q):
                v.wait_ge(s_phi, 6 * n + q + 1)
                v.tensor_tensor(xs[:, 1, kslot(q), :], pbuf[q], xs[:, 0, kslot(q), :].bitcast(F32),
                                ALU.subtract).then_inc(s_plo, 1)

            def silu_lo(n, h):
                v.wait_ge(s_shi, KT * n + h + 1)
                v.tensor_tensor(ssp[:, 1, h, :], sact[:, h, :], ssp[:, 0, h, :].bitcast(F32), ALU.subtract).then_inc(s_slo, 1)

            def c_stats(n):
                stats(n, lambda j: yb[j // 2][:, (j % 2) * D:(j % 2 + 1) * D], st3, mv3, ve3, s_bn3, s_mv3, s_ve3, s_y2)

            def c_rows(n, par):
                for j in range(TJ):
                    v.scalar_tensor_tensor(pay[par][:, j, 0:D], yb[j // 2][:, (j % 2) * D:(j % 2 + 1) * D],
                                           mv3[:, j, 0:1], nbc[:, 0, :], ALU.subtract, ALU.mult).then_inc(s_c, 1)
                v.wait_ge(s_rs3, n + 1)
                v.wait_ge(s_c, TJ * (n + 1))
                for j in range(TJ):
                    v.scalar_tensor_tensor(pay[par][:, j, 0:D], pay[par][:, j, 0:D], rs3[:, j:j + 1], nbc[:, 1, :],
                                           ALU.mult, ALU.add).then_inc(s_cn, 1)

            def c_lo(n, h):
                v.wait_ge(s_chi, KT * n + h + 1)
                v.tensor_tensor(csp[:, 1, h, :], tb[h][:], csp[:, 0, h, :].bitcast(F32), ALU.subtract).then_inc(s_clo, 1)

            def top_first(n):
                v.wait_ge(s_gate, n + 1)
                v.tensor_copy(lg[:, :, 0:NE], Y1[:, P:P + TJ * NE].rearrange("p (j e) -> p j e", j=TJ)).then_inc(s_top, 1)
                v.wait_ge(s_top, TOPS * n + 1)
                held(v)
                for j in range(TJ):
                    ins = v.max(top8[:, j, :], lg[:, j, 0:NE])
                ins.then_inc(s_top, 1)
                v.wait_ge(s_top, TOPS * n + 2)
                v.tensor_copy(rep8[:, :, 0:TOPK], top8[:, :, 0:TOPK]).then_inc(s_top, 1)
                v.wait_ge(s_top, TOPS * n + 3)
                held(v)
                for j in range(TJ):
                    ins = v.match_replace(repl[:, j, :], rep8[:, j, :], lg[:, j, :], -BIG)
                ins.then_inc(s_top, 1)
                v.tensor_tensor(ex[:], lg[:, :, 0:NE], top8[:, :, 0:1].broadcast_to((P, TJ, NE)), ALU.subtract).then_inc(s_top, 1)
                v.wait_ge(s_top, TOPS * n + 4)
                v.tensor_scalar(mask[:], repl[:, :, 0:NE], -BIG, None, ALU.is_equal).then_inc(s_top, 1)

            def top_second(n, par):
                v.wait_ge(s_exp, n + 1)
                v.wait_ge(s_top, TOPS * n + 6)
                v.tensor_tensor(ex[:], ex[:], mask[:], ALU.mult).then_inc(s_top, 1)
                tok = pay[par][:, :, COL_TOK:COL_TOK + 1].bitcast(I32)
                v.tensor_scalar(tok, tok, float(2 * S), None, ALU.add).then_inc(s_top, 1)
                v.wait_ge(s_top, TOPS * n + 7)
                v.tensor_reduce(exs[:], ex[:], AX.X, ALU.add).then_inc(s_top, 1)
                v.wait_ge(s_rank, n + 1)
                v.tensor_tensor(slot[:], Y1[:, 0:TJ * NE].rearrange("p (j e) -> p j e", j=TJ),
                                base[:].rearrange("p (o e) -> p o e", o=1).broadcast_to((P, TJ, NE)), ALU.add).then_inc(s_top, 1)
                v.wait_ge(s_top, TOPS * n + 10)
                v.reciprocal(exs[:], exs[:]).then_inc(s_top, 1)
                v.tensor_tensor(slot[:], slot[:], mask[:], ALU.mult).then_inc(s_top, 1)
                v.wait_ge(s_top, TOPS * n + 12)
                held(v)
                v.tensor_tensor(pay[par][:, :, COL_W:COL_W + NE], ex[:],
                                exs[:].rearrange("p (j o) -> p j o", o=1).broadcast_to((P, TJ, NE)), ALU.mult).then_inc(s_pay, 1)
                for j in range(TJ):
                    ins = v.max(slot8[:, j, :], slot[:, j, :])
                ins.then_inc(s_top, 1)
                v.tensor_tensor(base[:], base[:], Y1[:, TJ * NE:(TJ + 1) * NE], ALU.add).then_inc(s_top, 1)
                v.wait_ge(s_top, TOPS * n + 14)
                v.tensor_scalar(idx[par][:], slot8[:, :, 0:TOPK], -1.0, None, ALU.add).then_inc(s_idx, 1)

            def shared_act(n):
                v.wait_ge(s_ss, n + 1)
                v.wait_ge(s_h, 2 * n + 2)
                v.tensor_tensor(sact[:, 1, :], sact[:, 0, :], hb[1][:], ALU.mult).then_inc(s_sa, 1)

            def shared_lo(n):
                v.wait_ge(s_ahi, n + 1)
                v.tensor_tensor(ssp[:, 1, 0, :], sact[:, 1, :], ssp[:, 0, 0, :].bitcast(F32), ALU.subtract).then_inc(s_alo, 1)

            def split_lo(c, w, e, s):
                v.wait_ge(s_split_hi, c + 1)
                v.tensor_tensor(w[:, e, 1, :] if e is not None else w[:, 1, :], stage[:, s, :],
                                (w[:, e, 0, :] if e is not None else w[:, 0, :]).bitcast(F32), ALU.subtract).then_inc(s_split_lo, 1)

            def split_lo_n(n, par):
                s = (par + SETUP_EXPERTS + 1) % 2
                e = bass.ds(n + SETUP_EXPERTS, 1)
                v.wait_ge(s_split_hi, n + SETUP_EXPERTS + 2)
                v.tensor_tensor(wff[:, e, 1, :].rearrange("p o c -> p (o c)"), stage[:, s, :],
                                wff[:, e, 0, :].rearrange("p o c -> p (o c)").bitcast(F32), ALU.subtract).then_inc(s_split_lo, 1)

            count = [0]

            def r(ins):
                count[0] += 1
                ins.then_inc(s_route, 1)

            def known():
                v.wait_ge(s_route, count[0])

            def k(ins):
                count[0] += 1
                ins.then_inc(s_k, 1)

            def seen():
                v.wait_ge(s_k, count[0])

            v.memset(lg[:, :, NE:24], BIG)
            v.memset(rep8[:, :, TOPK:8], BIG)
            x_stats(0)
            v.wait_ge(s_c1, 48)
            seen()
            k(v.tensor_reduce(tmp[:, 2:3], awt, AX.X, ALU.max))
            k(v.tensor_copy(base[:], cst[:, C_CAP:C_CAP + NE]))
            seen()
            k(v.tensor_scalar(w6, awt, tmp[:, 2:3], None, ALU.subtract))
            assert count[0] == K_AWD, count
            k(v.tensor_copy(upper[:], cst[:, C_UP:C_UP + P]))
            k(v.tensor_scalar(ones[:], cst[0:SEL, C_UP:C_UP + P], 0.0, 1.0, ALU.mult, ALU.add))
            x_shift(0)
            v.wait_ge(s_ak, 1)
            k(v.tensor_reduce(tmp[:, 3:4], w6, AX.X, ALU.add))
            seen()
            k(v.reciprocal(tmp[:, 4:5], tmp[:, 3:4]))
            seen()
            k(v.tensor_scalar(w6, w6, tmp[:, 4:5], None, ALU.mult))
            onehot(0)
            v.wait_ge(s_ak, 2)
            v.tensor_copy(tab[0:32, :, :], tabhi[0:32, :, :])
            k(v.tensor_tensor(tab[32:64, :, :], rawtab[32:64, :, :], tabhi[32:64, :, :].bitcast(F32), ALU.subtract))
            assert count[0] == K_TAB, count
            for h in (0, 1):
                x_lo(0, h)
            for q in range(2):
                product(0, q)
            for q in range(2):
                p_lo(0, q)
            gain(0)
            seen()
            v.wait_ge(s_c2, 16)
            for i in range(6):
                ins = v.tensor_scalar(raw[:, i, :, :], raw[:, i, :, :], w6[:, i:i + 1], None, ALU.mult)
            k(ins)
            h_stats(0)
            seen()
            k(v.tensor_tensor(wm[:], raw[:, 2, :, :], raw[:, 3, :, :], ALU.add))
            seen()
            k(v.tensor_tensor(wm[:], wm[:], raw[:, 4, :, :], ALU.add))
            assert count[0] == K_WM, count
            h_shift(0)
            v.wait_ge(s_ek, 2)
            v.wait_ge(s_c3, 80)
            k(v.tensor_tensor(m_b2[:], H1[0:96, 0:D], m_b2[:], ALU.add))
            seen()
            k(v.bn_stats(tmp[0:96, 8:14], m_b2[:]))
            seen()
            k(v.bn_aggr(tmp[0:96, 14:16], tmp[0:96, 8:14]))
            seen()
            k(v.tensor_scalar(tmp[0:96, 0:1], tmp[0:96, 15:16], EPS, None, ALU.add))
            assert count[0] == K_MVE, count
            v.wait_ge(s_pk, 3)
            k(v.tensor_scalar(m_b2[:], m_b2[:], tmp[0:96, 14:15], tmp[0:96, 1:2], ALU.subtract, ALU.mult))
            assert count[0] == K_MLN, count
            x_stats(1)
            for q in range(2, 4):
                product(0, q)
            v.wait_ge(s_ak, 4)
            for q, src in enumerate((wm[:], raw[:, 0, :, :], raw[:, 1, :, :], raw[:, 5, :, :])):
                ins = v.tensor_tensor(wint[:, 1, KT * q:KT * q + KT, :], src, wint[:, 0, KT * q:KT * q + KT, :].bitcast(F32),
                                      ALU.subtract)
            k(ins)
            v.wait_ge(s_ek, 4)
            for i in range(3):
                for kt in range(KT):
                    ins = v.tensor_scalar(m_t[:, i, kt, :], Y1[:, kt * 96 + 32 * i:kt * 96 + 32 * i + NB],
                                          m_cols[:, 1, kt, i:i + 1], m_cols[:, 2, kt, i:i + 1], ALU.mult, ALU.add)
            k(ins)
            assert count[0] == K_MT, count
            x_shift(1)
            for q in range(2, 4):
                p_lo(0, q)
            for q in range(4, 6):
                product(0, q)
            v.wait_ge(s_ak, 5)
            v.tensor_copy(btab[0:32, :], tabhi[0:32, 0, :])
            k(v.tensor_tensor(btab[32:64, :], Y0[32:64, 0:D], tabhi[32:64, 0, :].bitcast(F32), ALU.subtract))
            for q in range(4, 6):
                p_lo(0, q)
            v.wait_ge(s_ek, 5)
            v.wait_ge(s_c4, 32)
            for h in range(KT):
                ins = v.tensor_scalar(vbias[:, h, :], H0[:, h * NB:(h + 1) * NB], b1[:, h:h + 1], None, ALU.add)
            k(ins)
            assert count[0] == K_VB, count
            v.wait_ge(s_ak, 6)
            v.tensor_tensor(wgate[:, 1, :, :], rawg[:], wgate[:, 0, :, :].bitcast(F32), ALU.subtract)
            k(v.tensor_tensor(wout[:, 1, :, :], rawo[:], wout[:, 0, :, :].bitcast(F32), ALU.subtract))
            seen()
            for p in (0, 1):
                v.memset(pay[p][:, :, D:ROW], 0.0).then_inc(s_k, 1)
            count[0] += 2
            seen()
            for p in (0, 1):
                ins = v.tensor_scalar(pay[p][:, :, COL_TOK:COL_TOK + 1].bitcast(I32),
                                      cst[:, C_TOK:C_TOK + TJ].rearrange("p (j o) -> p j o", o=1), float((p - 2) * S),
                                      None, ALU.add)
            k(ins)
            assert count[0] == K_END, count
            seen()
            for c in range(SETUP_EXPERTS + 1):
                split_lo(c, wsh if c == 0 else wff, None if c == 0 else c - 1, c % 2)

            def step(n, par, prev, front, ahead):
                if front:
                    gain(n + 1)
                if prev:
                    split_lo_n(n - 1, 1 - par)
                    top_first(n - 1)
                if front:
                    h_stats(n + 1)
                    onehot(n + 1)
                if prev:
                    top_second(n - 1, 1 - par)
                silu_lo(n, 0)
                if front:
                    h_shift(n + 1)
                    for q in (0, 1):
                        product(n + 1, q)
                if ahead:
                    x_stats(n + 2)
                if front:
                    for q in (2, 3):
                        product(n + 1, q)
                silu_lo(n, 1)
                if front:
                    for h in (0, 1):
                        x_lo(n + 1, h)
                if ahead:
                    x_shift(n + 2)
                if front:
                    for q in (0, 1):
                        p_lo(n + 1, q)
                c_stats(n)
                if prev and (not isinstance(n, int) or n >= 2):
                    v.wait_ge(s_sc[par], 8 * TOPK * TJ * (n - par))
                if front:
                    p_lo(n + 1, 2)
                c_rows(n, par)
                if front:
                    p_lo(n + 1, 3)
                if prev:
                    shared_act(n - 1)
                if front:
                    for q in (4, 5):
                        product(n + 1, q)
                if prev:
                    shared_lo(n - 1)
                for h in (0, 1):
                    c_lo(n, h)
                if front:
                    for q in (4, 5):
                        p_lo(n + 1, q)

            batches(v, step)
            top_first(NB - 1)
            top_second(NB - 1, 1)
            count[0] = 0
            r(v.memset(padtile, 0.0))
            known()
            for t in range(BT):
                r(v.tensor_scalar(padtile[:, t, COL_TOK:COL_TOK + 1].bitcast(I32), cst[:, C_TOK:C_TOK + 1], float(BT),
                                  float(T + t), ALU.mult, ALU.add))
            assert count[0] == R_PAD, count
            r(v.tensor_scalar(padrow, base[0:1, :], -1.0, None, ALU.add))
            assert count[0] == R_PADROW, count
            shared_act(NB - 1)
            shared_lo(NB - 1)
            for e in range(SETUP_EXPERTS + NB - 1, LATE):
                split_lo(e + 1, wff, e, (e + 1) % 2)
            cap1 = cst[:, C_CAP:C_CAP + NE]
            blk = cst[:, C_TOK:C_TOK + 1]
            r(v.tensor_tensor(cnt, base[:], cap1, ALU.subtract))
            for c in cum:
                r(v.memset(c[:, 0:NE], 0.0))
            known()
            r(v.tensor_scalar(nblk, cnt, 1.0 / BROWS, (BROWS / 2 - 0.5) / BROWS, ALU.mult, ALU.add))
            known()
            r(v.tensor_scalar(nblk, nblk, 2.0 ** 23, None, ALU.add))
            known()
            r(v.tensor_scalar(nblk, nblk, 2.0 ** 23, None, ALU.subtract))
            known()
            r(v.tensor_copy(cum[0][:, NE:], nblk))
            src = 0
            for d in (1, 2, 4, 8):
                known()
                r(v.tensor_tensor(cum[1 - src][:, NE:], cum[src][:, NE:], cum[src][:, NE - d:2 * NE - d], ALU.add))
                src = 1 - src
            known()
            r(v.tensor_scalar(done, cum[src][:, NE:], blk, None, ALU.is_le))
            known()
            r(v.tensor_tensor(dblk, done, nblk, ALU.mult))
            r(v.tensor_reduce(route[:, 0:1], done, AX.X, ALU.add))
            known()
            r(v.tensor_reduce(start_blk, dblk, AX.X, ALU.add))
            known()
            r(v.tensor_tensor(start_blk, blk, start_blk, ALU.subtract))
            r(v.tensor_scalar(route[:, 1:2], route[:, 0:1], float(CAP), None, ALU.mult))
            known()
            r(v.scalar_tensor_tensor(route[:, 1:2], start_blk, float(BROWS), route[:, 1:2], ALU.mult, ALU.add))
            r(v.tensor_scalar(route[:, 0:1], route[:, 0:1], float(NE - 1), None, ALU.min))
            known()
            r(v.tensor_scalar(route[:, 1:2], route[:, 1:2], float(NE * CAP), None, ALU.min))
            assert count[0] == R_ROUTE, count
            v.wait_ge(s_cols, 1)
            v.tensor_copy(table[:].rearrange("p (q b) -> p q b", q=2),
                          T0[0:1, 0:2 * P].rearrange("p (q b) -> p q b", q=2)[:, :, 0:NBLK]).then_inc(s_table, 1)
            v.wait_ge(s_table, 1)
            for e in (LATE, LATE + 1):
                split_lo(e + 1, wff, e, (e + 1) % 2)
            for e, src in enumerate(late_stage, LATE + 2):
                v.wait_ge(s_split_hi, e + 2)
                v.tensor_tensor(wff[:, e, 1, :], src, wff[:, e, 0, :].bitcast(F32), ALU.subtract).then_inc(s_split_lo, 1)


K_AWD, K_TAB, K_WM, K_MVE, K_MLN, K_MT, K_VB, K_END = 3, 9, 12, 16, 17, 19, 21, 25
TOPS = 14


def kslot(q):
    return (4, 5, 6, 7, 2, 3)[q]


RING = 4
SKEW = 4
R_PAD, R_PADROW, R_ROUTE = 3, 4, 24
assert NBLK % RING == 0 and NACC == 2 and RING % NACC == 0 and SKEW == RING


def experts_block(nc, g, sem):
    wff, ident, table = g.wff, g.ident, g.table
    X, H, A, Y = g.banks[0:2], g.banks[2:4], g.banks[4:6], g.banks[6:8]

    with ExitStack() as ctx:
        def sb(name, shape, dt=F32):
            return ctx.enter_context(nc.sbuf_tensor(name, shape, dt))

        rows = [sb(f"rows{i}", [P, BT, ROW]) for i in range(2 * RING)]
        xT = [sb(f"xT{i}", [P, 2, KT * BROWS], F32R) for i in (0, 1)]
        sil = [sb(f"sil{i}", [P, BT, HID]) for i in (0, 1)]
        act_t = [sb(f"act{i}", [P, BT, HID]) for i in (0, 1)]
        aT = [sb(f"aT{i}", [P, 2, BROWS], F32R) for i in (0, 1)]
        y = [sb(f"y{i}", [P, BT, D]) for i in range(RING)]

        s_in = [sem(f"rows_in{i}") for i in range(2 * RING)]
        s_xT, s_xhi, s_xlo = sem("rows_turned"), sem("rows_hi"), sem("rows_lo")
        s_h, s_sil, s_act = sem("expert_h"), sem("expert_silu"), sem("expert_act")
        s_aT, s_ahi, s_alo = sem("act_turned"), sem("act_hi"), sem("act_lo")
        s_y, s_yout = sem("expert_y"), sem("expert_y_out")
        s_add = [sem(f"added{i}") for i in range(NACC)]
        s_go = sem("expert_wait_held")
        ADDED = 16 * BT

        def held(eng):
            eng.sem_inc(s_go, 1)

        def schedule(eng, step):
            for s in range(2 * RING):
                step(s, s, [i <= s for i in range(SKEW + 1)])
            with eng.Fori(0, NBLK // (2 * RING) - 1) as m:
                for q in range(2 * RING):
                    step(2 * RING * m + (2 * RING + q), q, [True] * (SKEW + 1))
            for s in range(NBLK, NBLK + SKEW):
                step(s, s % (2 * RING), [i > s - NBLK for i in range(SKEW + 1)])

        block = ctx.enter_context(nc.Block())

        @block.sync
        def _(sp):
            def load(b, q):
                r = sp.value_load(table[0:1, bass.ds(b + NBLK, 1)], min_val=0, max_val=NE * CAP)
                sp.dma_start(rows[q][:], g.xlist[bass.ds(r, BROWS), :].rearrange("(p t) c -> p t c", t=BT)).then_inc(s_in[q], 16)

            for b in range(2 * RING):
                load(b, b)
            with sp.Fori(0, NBLK // (2 * RING) - 1) as m:
                for q in range(2 * RING):
                    sp.wait_ge(s_add[q % NACC], ADDED * (2 * RING // NACC) * m + ADDED * (q // NACC + 1))
                    held(sp)
                    load(2 * RING * m + (2 * RING + q), q)

        @block.gpsimd
        def _(pool):
            def add(b, q, turn):
                pool.wait_ge(s_yout, b + 1)
                wait_past(pool, s_add[q % NACC], ADDED * turn)
                held(pool)
                for t in range(BT):
                    pool.indirect_dma_start(g.accs[q % NACC], bass.IndirectOffsetOnAxis(
                        ap=rows[q][:, t, COL_TOK:COL_TOK + 1].bitcast(I32), axis=0), y[q % RING][:, t, :], None,
                        bounds_check=T - 1, oob_is_err=False, compute_op=ALU.add).then_inc(s_add[q % NACC], 16)

            for b in range(2 * RING):
                add(b, b, b // NACC)
            with pool.Fori(0, NBLK // (2 * RING) - 1) as m:
                for q in range(2 * RING):
                    add(2 * RING * m + (2 * RING + q), q, (2 * RING // NACC) * m + (2 * RING + q) // NACC)
            for a in range(NACC):
                pool.wait_ge(s_add[a], ADDED * (NBLK // NACC))

        @block.scalar
        def _(act):
            def step(s, q, on):
                if on[4]:
                    b, i = s - SKEW, (q - SKEW) % RING
                    act.wait_ge(s_y, b + 1)
                    wait_past(act, s_add[i % NACC], (s - q) * (ADDED // NACC) + ADDED * ((q - SKEW - RING) // NACC + 1))
                    held(act)
                    act.activation(y[i][:].rearrange("p t d -> p (t d)"), Y[i % 2][:], ACT.Copy).then_inc(s_yout, 1)
                if on[0]:
                    act.wait_ge(s_xT, s + 1)
                    act.activation(xT[q % 2][:, 0, :], X[q % 2][:], ACT.Copy).then_inc(s_xhi, 1)
                if on[1]:
                    b, i = s - 1, (q - 1) % 2
                    act.wait_ge(s_h, b + 1)
                    act.activation(sil[i][:], H[i][:].rearrange("p (t c) -> p t c", t=BT)[:, :, 0:HID], ACT.Silu).then_inc(s_sil, 1)
                if on[2]:
                    b, i = s - 2, q % 2
                    act.wait_ge(s_aT, b + 1)
                    act.activation(aT[i][:, 0, :], A[i][:, 0:BROWS], ACT.Copy).then_inc(s_ahi, 1)

            schedule(act, step)

        @block.tensor
        def _(pe):
            def step(s, q, on):
                if on[0]:
                    n = 2 * RING
                    pe.wait_ge(s_in[q], 16 * (s // n) + 16 if isinstance(s, int) else (16 // n) * (s - q) + 16)
                    for k in range(KT):
                        for t in range(BT):
                            mm = pe.transpose(X[q % 2][:, (k * BT + t) * P:(k * BT + t + 1) * P],
                                              rows[q][:, t, k * P:(k + 1) * P], ident)
                    mm.then_inc(s_xT, 1)
                if on[1]:
                    b, i = s - 1, (q - 1) % 2
                    e = pe.value_load(table[0:1, bass.ds(b, 1)], min_val=0, max_val=NE - 1)
                    pe.wait_ge(s_xlo, b + 1)
                    for t in range(BT):
                        for k in range(KT):
                            at = (k * BT + t) * P
                            for x, w in ((0, 0), (0, 1), (1, 0)):
                                mm = pe.matmul(H[i][:, t * 2 * HID:(t + 1) * 2 * HID], xT[i][:, x, at:at + P],
                                               wff[:, bass.ds(e, 1), w, k * 2 * HID:(k + 1) * 2 * HID],
                                               start=(k == 0 and x + w == 0), stop=(k == KT - 1 and x == 1))
                    mm.then_inc(s_h, 1)
                if on[2]:
                    b, i = s - 2, q % 2
                    pe.wait_ge(s_act, b + 1)
                    for t in range(BT):
                        mm = pe.transpose(A[i][:, t * P:(t + 1) * P], act_t[i][:, t, :], ident)
                    mm.then_inc(s_aT, 1)
                if on[3]:
                    b, i = s - 3, (q - 3) % 2
                    e = pe.value_load(table[0:1, bass.ds(b, 1)], min_val=0, max_val=NE - 1)
                    pe.wait_ge(s_alo, b + 1)
                    for t in range(BT):
                        for x, w in ((0, 0), (0, 1), (1, 0)):
                            mm = pe.matmul(Y[i][:, t * D:(t + 1) * D], aT[i][:, x, t * P:(t + 1) * P],
                                           wff[:, bass.ds(e, 1), w, KT * 2 * HID:EW], start=(x + w == 0), stop=(x == 1))
                    mm.then_inc(s_y, 1)

            schedule(pe, step)

        @block.vector
        def _(v):
            def step(s, q, on):
                if on[0]:
                    i = q % 2
                    v.wait_ge(s_xhi, s + 1)
                    v.tensor_tensor(xT[i][:, 1, :], X[i][:], xT[i][:, 0, :].bitcast(F32), ALU.subtract).then_inc(s_xlo, 1)
                if on[1]:
                    b, i = s - 1, (q - 1) % 2
                    e = v.value_load(table[0:1, bass.ds(b, 1)], min_val=0, max_val=NE - 1)
                    v.wait_ge(s_sil, b + 1)
                    held(v)
                    for t in range(BT):
                        ins = v.scalar_tensor_tensor(
                            act_t[i][:, t, :], sil[i][:, t, :], rows[(q - 1) % (2 * RING)][:, t, bass.ds(e + COL_W, 1)],
                            H[i][:, t * 2 * HID + HID:(t + 1) * 2 * HID], ALU.mult, ALU.mult)
                    ins.then_inc(s_act, 1)
                if on[2]:
                    b, i = s - 2, q % 2
                    v.wait_ge(s_ahi, b + 1)
                    v.tensor_tensor(aT[i][:, 1, :], A[i][:, 0:BROWS], aT[i][:, 0, :].bitcast(F32), ALU.subtract).then_inc(s_alo, 1)

            schedule(v, step)


def sum_block(nc, g, sem):
    with ExitStack() as ctx:
        part = [ctx.enter_context(nc.sbuf_tensor(f"part{n}", [P, TJ, D], F32)) for n in range(NB)]
        s_part = [sem(f"part_in{n}") for n in range(NB)]
        s_out = sem("out")
        block = ctx.enter_context(nc.Block())

        @block.sync
        def _(sp):
            for n in range(NB):
                sp.dma_start(part[n][:], g.acc_b[1][:, n, :, :]).then_inc(s_part[n], 16)

        @block.gpsimd
        def _(pool):
            for n in range(NB):
                pool.wait_ge(s_part[n], 16)
                pool.dma_start(g.out_b[:, n, :, :], part[n][:], accum_op=ALU.add).then_inc(s_out, 16)
            pool.wait_ge(s_out, 16 * NB)


def kernel(**inputs):
    import numpy as _np
    import concourse.bacc as _bacc
    from concourse import mybir as _mybir
    from concourse.bass_utils import run_bass_kernel_spmd as _run

    a = {k: _np.asarray(v) for k, v in inputs.items()}
    f32 = _np.float32

    def cond(name):
        return a["L0_cond_" + name]

    def ktiles(w):
        return w.reshape(-1, P, w.shape[-1]).transpose(1, 0, 2)

    def columns(v):
        return v.reshape(KT, P).T

    c9, c4, mk = a["itok_BxS_0_999"], a["itok_BxS_0_4"], a["mask_BxS_ik0"]
    sel_ids = _np.zeros((SEL, NB, S), c4.dtype)
    tabs = _np.zeros((SEL, 4, D), f32)
    tab_b = _np.zeros((P, 3, KT, SEL), f32)
    consts = _np.zeros((P, C_END), f32)
    consts[:, C_SEL] = -1
    for r in (0, 32):
        sel_ids[r:r + NC] = c4
        sel_ids[r + NC:r + NC + NM] = mk
        consts[r:r + NC, C_SEL] = _np.arange(NC)
        consts[r + NC:r + NC + NM, C_SEL] = _np.arange(NM)
        tabs[r:r + NC, 0], tabs[r:r + NC, 1] = cond("cp_g"), cond("tm_g")
        tabs[r + NC:r + NC + NM, 2] = cond("ms_g")
        tabs[r, 3] = cond("int_b2")
        for t, name, at in ((0, "cp_b", r), (1, "tm_b", r), (2, "ms_b", r + NC)):
            b = cond(name)
            tab_b[:, t, :, at:at + len(b)] = b.reshape(len(b), KT, P).transpose(2, 1, 0)
    consts[:, C_ID:C_ID + P] = _np.eye(P)
    consts[:, C_UP:C_UP + P] = _np.triu(_np.ones((P, P)), 1)
    consts[:, C_CAP:C_CAP + NE] = _np.arange(NE) * CAP + 1
    consts[:, C_TOK:C_TOK + TJ] = _np.arange(P)[:, None] + P * _np.arange(TJ)

    mlp_in = _np.zeros((P, 3, 32), f32)
    mlp_w1 = _np.zeros((P, 3, D), f32)
    mlp_w2 = _np.zeros((P, 3, KT, D), f32)
    mlp_b2 = _np.zeros((96, D), f32)
    mlp_cols = _np.zeros((P, 3, KT, 3), f32)
    for i, (name, s) in enumerate((("mem", "cond_512"), ("noi", "cond_64"), ("res", "fside_Bx32_0"))):
        mlp_in[:a[s].shape[1], i, :NB] = a[s].T
        mlp_w1[:a[s].shape[1], i] = cond(name + "_W1")
        mlp_w2[:, i] = ktiles(cond(name + "_W2"))
        mlp_b2[32 * i:32 * i + 32] = cond(name + "_b2")
        for q, part in enumerate(("_b1", "_g", "_be")):
            mlp_cols[:, q, :, i] = columns(cond(name + part))

    w1 = _np.concatenate([a["L0_ffn_w1"], a["L0_ffn_sw1"][None]])
    w3 = _np.concatenate([a["L0_ffn_w3"], a["L0_ffn_sw3"][None]])
    w2 = _np.concatenate([a["L0_ffn_w2"], a["L0_ffn_sw2"][None]])
    first = _np.concatenate([w1, w3], 1).transpose(0, 2, 1).reshape(NE + 1, KT, P, 2 * HID).transpose(0, 2, 1, 3)
    experts = _np.concatenate([first.reshape(NE + 1, P, KT * 2 * HID), w2.transpose(0, 2, 1)], 2)

    arrays = {
        "x": a["x"].reshape(T, D),
        "pw_ids": c9.reshape(NB, TJ, P).transpose(2, 0, 1),
        "sel_ids": sel_ids,
        "pw_tab": _np.concatenate([cond("pw_g"), cond("pw_b")], 1),
        "consts": consts,
        "aw": _np.repeat(cond("aw")[None], P, 0),
        "int_w1": ktiles(cond("int_W1")).reshape(P, 6, KT, D),
        "int_w2": ktiles(cond("int_W2")),
        "int_b1": columns(cond("int_b1")),
        "norm_bc": _np.repeat(_np.stack([cond("int_g"), cond("int_be")])[None], P, 0),
        "tabs": tabs,
        "tab_b": tab_b,
        "gate": ktiles(a["L0_ffn_gate_w"].T),
        "mlp_in": mlp_in, "mlp_w1": mlp_w1, "mlp_w2": mlp_w2, "mlp_b2": mlp_b2, "mlp_cols": mlp_cols,
        "experts": experts,
    }
    arrays = {k: _np.ascontiguousarray(v) for k, v in arrays.items()}
    nc = _bacc.Bacc("TRN2", target_bir_lowering=False, num_devices=1)
    args = {k: nc.dram_tensor(k + "_in", v.shape, _mybir.dt.from_np(v.dtype), kind="ExternalInput").ap()
            for k, v in arrays.items()}
    out = nc.dram_tensor("out_dram", (T, D), _mybir.dt.float32, kind="ExternalOutput").ap()
    build(nc, out=out, **args)
    r = _run(nc, [{k + "_in": v for k, v in arrays.items()}], core_ids=[0])
    return r.results[0]["out_dram"].reshape(NB, S, D)
```
